# Optimizing a Trainium2 kernel written in Bass

```python
import numpy as np
import jax
import jax.numpy as jnp

def _softmax(x, axis=-1):
    return jax.nn.softmax(x, axis=axis)

def _gelu(x):
    return jax.nn.gelu(x, approximate=True)

def _silu(x):
    return jax.nn.silu(x)

def _sigmoid(x):
    return jax.nn.sigmoid(x)

def _layernorm(x, axis=-1, eps=1e-05):
    m = jnp.mean(x, axis=axis, keepdims=True)
    v = jnp.var(x, axis=axis, keepdims=True)
    return (x - m) / jnp.sqrt(v + eps)

def _scatter_add(tgt, idx, src, axis=0):
    return tgt.at[idx].add(src)

def _segment_sum(src, seg, n):
    return jax.ops.segment_sum(src, seg, n)
kernel_name = 'mk_macaron_d2_jaxref_r8_ed6a13'

def setup_inputs(seed: int=0):
    np.random.seed(seed)
    _w = jnp.asarray

    def _L0_attn_setup():
        import jax, jax.numpy as jnp
        import numpy as np
        B, S, D = (2, 256, 256)
        H, KVH, DH = (16, 4, 128)
        WIN = 128
        THETA = 10000.0

        def _rotate_half(t):
            half = t.shape[-1] // 2
            return jnp.concatenate([-t[..., half:], t[..., :half]], axis=-1)

        def _rope_tables(seq_len, head_dim, theta, dtype):
            inv_freq = 1.0 / theta ** (jnp.arange(0, head_dim, 2, dtype=jnp.float32) / head_dim)
            freqs = jnp.arange(seq_len, dtype=jnp.float32)[:, None] * inv_freq[None, :]
            cos = jnp.repeat(jnp.cos(freqs), 2, axis=-1).astype(dtype)
            sin = jnp.repeat(jnp.sin(freqs), 2, axis=-1).astype(dtype)
            return (cos[None, :, None, :], sin[None, :, None, :])
        key = jax.random.key(seed)
        ks = jax.random.split(key, 5)
        return {'x': jax.random.normal(ks[0], (B, S, D), dtype=jnp.float32), 'Wq': jax.random.normal(ks[1], (H * DH, D), dtype=jnp.float32) * 0.02, 'Wk': jax.random.normal(ks[2], (KVH * DH, D), dtype=jnp.float32) * 0.02, 'Wv': jax.random.normal(ks[3], (KVH * DH, D), dtype=jnp.float32) * 0.02, 'Wo': jax.random.normal(ks[4], (D, H * DH), dtype=jnp.float32) * 0.02}
    _L0_attn_in = _L0_attn_setup()

    def _L0_ffn_setup():
        import jax, jax.numpy as jnp
        import numpy as np
        HIDDEN = 256
        INTER = 1024
        BATCH, LOCAL_SEQ = (2, 512)
        key = jax.random.key(seed)
        k1, k2, k3 = jax.random.split(key, 3)
        h_shard = jax.random.normal(k1, (BATCH, LOCAL_SEQ, HIDDEN), dtype=jnp.float32)
        w_gate_up = jax.random.normal(k2, (2 * INTER, HIDDEN), dtype=jnp.float32) * 0.02
        w_down = jax.random.normal(k3, (HIDDEN, INTER), dtype=jnp.float32) * 0.02
        return {'h_shard': h_shard, 'w_gate_up': w_gate_up, 'w_down': w_down}
    _L0_ffn_in = _L0_ffn_setup()

    def _L1_attn_setup():
        import jax, jax.numpy as jnp
        import numpy as np
        ROPE_THETA = 10000.0

        def _apply_rope(x, theta=ROPE_THETA):
            L, d_k = (x.shape[-2], x.shape[-1])
            inv_freq = 1.0 / theta ** (jnp.arange(0, d_k, 2, dtype=jnp.float32) / d_k)
            ang = jnp.arange(L, dtype=jnp.float32)[:, None] * inv_freq[None, :]
            ang = jnp.repeat(ang, 2, axis=-1)
            xr = x.reshape(x.shape[:-1] + (d_k // 2, 2))
            rot = jnp.stack((-xr[..., 1], xr[..., 0]), axis=-1).reshape(x.shape)
            return x * jnp.cos(ang) + rot * jnp.sin(ang)
        key = jax.random.key(seed)
        k1, k2, k3 = jax.random.split(key, 3)
        B, L, D = (2, 256, 256)
        std_qkv = np.sqrt(2.0 / (D + 3 * D)).astype(np.float32)
        std_o = np.sqrt(2.0 / (D + D)).astype(np.float32)
        return {'x': jax.random.normal(k1, (B, L, D), dtype=jnp.float32), 'W_qkv': jax.random.normal(k2, (3 * D, D), dtype=jnp.float32) * std_qkv, 'W_o': jax.random.normal(k3, (D, D), dtype=jnp.float32) * std_o}
    _L1_attn_in = _L1_attn_setup()

    def _L1_ffn_setup():
        import jax, jax.numpy as jnp
        import numpy as np
        B, S, H = (2, 128, 256)
        E, K = (8, 2)
        I = 176
        IS = 704
        WSCALE = 0.02
        key = jax.random.key(seed)
        ks = jax.random.split(key, 9)
        f32 = jnp.float32
        return {'hidden_states': jax.random.normal(ks[0], (B, S, H), dtype=f32), 'gate_w': jax.random.normal(ks[1], (E, H), dtype=f32) * WSCALE, 'w_gate': jax.random.normal(ks[2], (E, H, I), dtype=f32) * WSCALE, 'w_up': jax.random.normal(ks[3], (E, H, I), dtype=f32) * WSCALE, 'w_down': jax.random.normal(ks[4], (E, I, H), dtype=f32) * WSCALE, 'sw_gate': jax.random.normal(ks[5], (H, IS), dtype=f32) * WSCALE, 'sw_up': jax.random.normal(ks[6], (H, IS), dtype=f32) * WSCALE, 'sw_down': jax.random.normal(ks[7], (IS, H), dtype=f32) * WSCALE, 'shared_gate_w': jax.random.normal(ks[8], (H, 1), dtype=f32) * WSCALE}
    _L1_ffn_in = _L1_ffn_setup()
    _d = {'L0_attn_x': _L0_attn_in['x'], 'L0_attn_Wq': _L0_attn_in['Wq'], 'L0_attn_Wk': _L0_attn_in['Wk'], 'L0_attn_Wv': _L0_attn_in['Wv'], 'L0_attn_Wo': _L0_attn_in['Wo'], 'L0_ffn_w_gate_up': _L0_ffn_in['w_gate_up'], 'L0_ffn_w_down': _L0_ffn_in['w_down'], 'L1_attn_W_qkv': _L1_attn_in['W_qkv'], 'L1_attn_W_o': _L1_attn_in['W_o'], 'L1_ffn_gate_w': _L1_ffn_in['gate_w'], 'L1_ffn_w_gate': _L1_ffn_in['w_gate'], 'L1_ffn_w_up': _L1_ffn_in['w_up'], 'L1_ffn_w_down': _L1_ffn_in['w_down'], 'L1_ffn_sw_gate': _L1_ffn_in['sw_gate'], 'L1_ffn_sw_up': _L1_ffn_in['sw_up'], 'L1_ffn_sw_down': _L1_ffn_in['sw_down'], 'L1_ffn_shared_gate_w': _L1_ffn_in['shared_gate_w']}
    _x0 = _d['L0_attn_x']
    _d['L0_attn_x'] = jax.random.normal(jax.random.fold_in(jax.random.key(seed), 1), (4, 256, 256), dtype=_x0.dtype)
    del _x0
    return _d

def reference(L0_attn_x, L0_attn_Wq, L0_attn_Wk, L0_attn_Wv, L0_attn_Wo, L0_ffn_w_gate_up, L0_ffn_w_down, L1_attn_W_qkv, L1_attn_W_o, L1_ffn_gate_w, L1_ffn_w_gate, L1_ffn_w_up, L1_ffn_w_down, L1_ffn_sw_gate, L1_ffn_sw_up, L1_ffn_sw_down, L1_ffn_shared_gate_w):

    def _L0_attn_ref(x, Wq, Wk, Wv, Wo):
        import jax, jax.numpy as jnp
        import numpy as np
        B, S, D = (2, 256, 256)
        H, KVH, DH = (16, 4, 128)
        WIN = 128
        THETA = 10000.0

        def _rotate_half(t):
            half = t.shape[-1] // 2
            return jnp.concatenate([-t[..., half:], t[..., :half]], axis=-1)

        def _rope_tables(seq_len, head_dim, theta, dtype):
            inv_freq = 1.0 / theta ** (jnp.arange(0, head_dim, 2, dtype=jnp.float32) / head_dim)
            freqs = jnp.arange(seq_len, dtype=jnp.float32)[:, None] * inv_freq[None, :]
            cos = jnp.repeat(jnp.cos(freqs), 2, axis=-1).astype(dtype)
            sin = jnp.repeat(jnp.sin(freqs), 2, axis=-1).astype(dtype)
            return (cos[None, :, None, :], sin[None, :, None, :])
        b, s, _ = x.shape
        q = (x @ Wq.T).reshape(b, s, H, DH)
        k = (x @ Wk.T).reshape(b, s, KVH, DH)
        v = (x @ Wv.T).reshape(b, s, KVH, DH)
        cos, sin = _rope_tables(s, DH, THETA, x.dtype)
        q = q * cos + _rotate_half(q) * sin
        k = k * cos + _rotate_half(k) * sin
        groups = H // KVH
        k = jnp.repeat(k, groups, axis=2)
        v = jnp.repeat(v, groups, axis=2)
        q = q.transpose(0, 2, 1, 3)
        k = k.transpose(0, 2, 1, 3)
        v = v.transpose(0, 2, 1, 3)
        scale = DH ** (-0.5)
        scores = jnp.einsum('bhqd,bhkd->bhqk', q, k) * scale
        iq = jnp.arange(s)[:, None]
        ik = jnp.arange(s)[None, :]
        mask = iq >= ik - WIN
        scores = jnp.where(mask[None, None, :, :], scores, jnp.float32(-jnp.inf).astype(scores.dtype))
        attn = jax.nn.softmax(scores, axis=-1)
        out = jnp.einsum('bhqk,bhkd->bhqd', attn, v)
        out = out.transpose(0, 2, 1, 3).reshape(b, s, H * DH)
        return out @ Wo.T

    def _L0_ffn_ref(h_shard, w_gate_up, w_down):
        import jax, jax.numpy as jnp
        import numpy as np
        HIDDEN = 256
        INTER = 1024
        BATCH, LOCAL_SEQ = (2, 512)
        batch, local_seq, hidden = h_shard.shape
        gate_up = jnp.einsum('bsh,oh->bso', h_shard, w_gate_up)
        gate, up = jnp.split(gate_up, 2, axis=-1)
        h = jax.nn.silu(gate) * up
        out = jnp.einsum('bsi,hi->bsh', h, w_down)
        return out

    def _L1_attn_ref(x, W_qkv, W_o):
        import jax, jax.numpy as jnp
        import numpy as np
        ROPE_THETA = 10000.0

        def _apply_rope(x, theta=ROPE_THETA):
            L, d_k = (x.shape[-2], x.shape[-1])
            inv_freq = 1.0 / theta ** (jnp.arange(0, d_k, 2, dtype=jnp.float32) / d_k)
            ang = jnp.arange(L, dtype=jnp.float32)[:, None] * inv_freq[None, :]
            ang = jnp.repeat(ang, 2, axis=-1)
            xr = x.reshape(x.shape[:-1] + (d_k // 2, 2))
            rot = jnp.stack((-xr[..., 1], xr[..., 0]), axis=-1).reshape(x.shape)
            return x * jnp.cos(ang) + rot * jnp.sin(ang)
        B, L, D = x.shape
        H = 16
        dh = D // H
        qkv = jnp.einsum('bld,ed->ble', x, W_qkv)
        q, k, v = jnp.split(qkv, 3, axis=-1)
        q = q.reshape(B, L, H, dh).transpose(0, 2, 1, 3)
        k = k.reshape(B, L, H, dh).transpose(0, 2, 1, 3)
        v = v.reshape(B, L, H, dh).transpose(0, 2, 1, 3)
        q = _apply_rope(q)
        k = _apply_rope(k)
        scale = 1.0 / np.sqrt(dh).astype(np.float32)
        att = jnp.einsum('bhqd,bhkd->bhqk', q, k) * scale
        causal = jnp.tril(jnp.ones((L, L), dtype=bool))
        att = jnp.where(causal, att, -jnp.inf)
        p = jax.nn.softmax(att, axis=-1)
        y = jnp.einsum('bhqk,bhkd->bhqd', p, v)
        y = y.transpose(0, 2, 1, 3).reshape(B, L, D)
        return jnp.einsum('bld,ed->ble', y, W_o)

    def _L1_ffn_ref(hidden_states, gate_w, w_gate, w_up, w_down, sw_gate, sw_up, sw_down, shared_gate_w):
        import jax, jax.numpy as jnp
        import numpy as np
        B, S, H = (2, 128, 256)
        E, K = (8, 2)
        I = 176
        IS = 704
        WSCALE = 0.02
        x = hidden_states
        logits = jnp.einsum('bsh,eh->bse', x, gate_w)
        probs = jax.nn.softmax(logits, axis=-1)
        top_w, top_i = jax.lax.top_k(probs, K)
        top_w = top_w / jnp.sum(top_w, axis=-1, keepdims=True)
        onehot = jax.nn.one_hot(top_i, E, dtype=x.dtype)
        combine = jnp.einsum('bsk,bske->bse', top_w, onehot)
        g = jnp.einsum('bsh,ehi->besi', x, w_gate)
        u = jnp.einsum('bsh,ehi->besi', x, w_up)
        h = jax.nn.silu(g) * u
        expert_out = jnp.einsum('besi,eih->besh', h, w_down)
        moe_out = jnp.einsum('besh,bse->bsh', expert_out, combine)
        sh = jax.nn.silu(x @ sw_gate) * (x @ sw_up)
        shared_out = sh @ sw_down
        shared_gate = jax.nn.sigmoid(x @ shared_gate_w)
        return moe_out + shared_out * shared_gate
    x = L0_attn_x
    x = x + 0.5 * _L0_ffn_ref(_layernorm(x, axis=-1), L0_ffn_w_gate_up, L0_ffn_w_down)
    x = x + _L0_attn_ref(_layernorm(x, axis=-1), L0_attn_Wq, L0_attn_Wk, L0_attn_Wv, L0_attn_Wo)
    x = x + 0.5 * _L0_ffn_ref(_layernorm(x, axis=-1), L0_ffn_w_gate_up, L0_ffn_w_down)
    x = x + 0.5 * _L1_ffn_ref(_layernorm(x, axis=-1), L1_ffn_gate_w, L1_ffn_w_gate, L1_ffn_w_up, L1_ffn_w_down, L1_ffn_sw_gate, L1_ffn_sw_up, L1_ffn_sw_down, L1_ffn_shared_gate_w)
    x = x + _L1_attn_ref(_layernorm(x, axis=-1), L1_attn_W_qkv, L1_attn_W_o)
    x = x + 0.5 * _L1_ffn_ref(_layernorm(x, axis=-1), L1_ffn_gate_w, L1_ffn_w_gate, L1_ffn_w_up, L1_ffn_w_down, L1_ffn_sw_gate, L1_ffn_sw_up, L1_ffn_sw_down, L1_ffn_shared_gate_w)
    return x

_drawn_inputs = setup_inputs


def setup_inputs(seed=0):
    import zlib

    import numpy as np

    out = dict(_drawn_inputs(seed))
    spreads = {}
    factors = {'L0_attn_Wq': 8.0,
     'L0_attn_Wk': 8.0,
     'L1_ffn_gate_w': 6.73,
     'L1_ffn_w_gate': 5.908,
     'L1_ffn_w_up': 5.846,
     'L1_ffn_w_down': 5.842,
     'L1_ffn_sw_gate': 4.041,
     'L1_ffn_sw_up': 4.018,
     'L1_ffn_sw_down': 4.016,
     'L1_ffn_shared_gate_w': 8.0}
    for name, (base, spread) in spreads.items():
        noise = np.random.default_rng([zlib.crc32(name.encode()), seed]).standard_normal(out[name].shape)
        drawn = base * np.exp(spread * noise) if base else spread * noise
        out[name] = jnp.asarray(drawn.astype(out[name].dtype))
    for name, factor in factors.items():
        out[name] = (out[name] * factor).astype(out[name].dtype)
    return out
```

```python
import math
from contextlib import ExitStack

import concourse.bass as bass
from concourse import mybir

P = 128
D = 256
KD = D // P
NB = 4
S = 256
TOK = NB * S
TT = TOK // P
HALF = TOK // 2
TPH = HALF // P
INTER = 1024
JF = INTER // P
E, I_EXP, I_SH = 8, 176, 704
JM = -(-(E * I_EXP + I_SH) // P)
GATES = E + 1
GLU = 3 * D
H0, KV0 = 16, 4
GRP = H0 // KV0
SC0 = P ** -0.5
NS0 = NB * H0
H1, DH1 = 16, 16
SC1 = DH1 ** -0.5
VC1 = DH1 + 1
NG1 = 2 * H1
BLK1 = 3
EPS = 1e-5

SX = 2.0 ** 6
SW = 2.0 ** 10
SH = 2.0 ** 5
SQ = 2.0 ** 4
SP = 2.0 ** 10
SR = 2.0 ** 8

A_N, B_N, C_N, D_N = GLU + D, 4 * D, GLU, D

F32, F16, BF16 = mybir.dt.float32, mybir.dt.float16, mybir.dt.bfloat16
ALU = mybir.AluOpType
ACT = mybir.ActivationFunctionType
AX = mybir.AxisListType
PASSES = ((0, 0), (0, 1), (1, 0))


def macaron(nc, x_in, wa_in, wb_in, wc_in, wd_in, wg_in, rope0_in, rope1_in, mask_in, idf_in,
            tri_in, sel_in, out):
    ds = bass.ds
    ctx = ExitStack()
    with ctx:
        def sb(name, shape, dt):
            return ctx.enter_context(nc.sbuf_tensor(name, shape, dt))

        def sem(name):
            return ctx.enter_context(nc.semaphore(name))

        WA = sb("WA", [P, A_N * (JF + 1)], F32)
        WB = sb("WB", [P, B_N * (JF + 1)], F32)
        WC = sb("WC", [P, C_N * (JM + 1)], F32)
        WD = WB[:, 0:D_N * 9]
        WA16 = WA[:, 0:A_N * JF].bitcast(F16).rearrange("p (c s n) -> p c s n", c=JF, s=2)
        WB16 = WB[:, 0:B_N * JF].bitcast(F16).rearrange("p (h s n) -> p h s n", h=H0, s=2)
        WC16 = WC[:, 0:C_N * JM].bitcast(F16).rearrange("p (c s n) -> p c s n", c=JM, s=2)
        WD16 = WB[:, 0:D_N * 8].bitcast(F16).rearrange("p (c s n) -> p c s n", c=8, s=2)
        WGR = sb("WGR", [P, KD, 16], F32)
        WGS = sb("WGS", [P, 2, KD, 16], F16)

        X = sb("X", [P, TT, D], F32)
        XT = sb("XT", [P, 2, KD, TOK], F16)
        XN = sb("XN", [P, 2, 2, D], F32)
        BST = sb("BST", [P, NB, 2, 6], F32)
        MV = sb("MV", [P, NB, 2, 2], F32)
        RSTD = sb("RSTD", [P, NB, 2, 2], F32)
        NHALF = sb("NHALF", [P, 2], F32)
        T1 = sb("T1", [P, HALF], F32)
        T2 = sb("T2", [P, HALF], F32)
        T3 = sb("T3", [P, HALF], F32)

        KVR = sb("KVR", [P, 2 * KV0 * TOK + 2 * TT * KV0 * P], F16)
        KT0 = KVR[:, 0:2 * KV0 * TOK].rearrange("p (s g t) -> p s g t", s=2, g=KV0)
        V0 = KVR[:, 2 * KV0 * TOK:].rearrange("p (s t n) -> p s t n", s=2, t=TT)
        KZ1 = KVR[:, :].rearrange("p (h t) -> p h t", h=H1)

        ARENA = sb("ARENA", [P, 3584], F32)
        PR0 = ARENA[:, 0:1024].rearrange("p (a n) -> p a n", a=2)
        PT0 = ARENA[:, 1024:2048].bitcast(F16).rearrange("p (a s n) -> p a s n", a=2, s=2)
        OT0 = ARENA[:, 2048:2560].bitcast(F16).rearrange("p (a s n) -> p a s n", a=2, s=2)
        QT0 = ARENA[:, 2560:3584].bitcast(F16).rearrange("p (s n) -> p s n", s=2)
        HH = ARENA[:, 0:1024].bitcast(F16).rearrange("p (a s n) -> p a s n", a=2, s=2)
        QK1 = ARENA[:, 0:2048].bitcast(F16).rearrange("p (a h n) -> p a h n", a=2, h=2 * H1)
        PR1 = ARENA[:, 0:1536].rearrange("p (a n) -> p a n", a=2)
        PT1 = ARENA[:, 1536:3072].bitcast(F16).rearrange("p (a s n) -> p a s n", a=2, s=2)
        ST = sb("ST", [P, 2, 4, 2], F32)
        MB1 = sb("MB1", [P, 2, 4], BF16)
        R1 = sb("R1", [P, 2, 4], F32)

        QT1 = WB[:, D_N * 9:D_N * 9 + H1 // 4 * TOK].bitcast(F16).rearrange("p (h t) -> p h t", t=TOK)
        VB1 = WA[:, 0:TT * H1 * VC1].bitcast(F16).rearrange("p (s t h n) -> p s t h n", s=2, t=TT, h=H1)
        O1S = WA[:, 2304:2304 + TT * D].rearrange("p (t n) -> p t n", t=TT)
        CMB = WA[:, 4480:4480 + TT * P // 2].bitcast(F16).rearrange("p (t n) -> p t n", t=TT)
        CBT = WA[:, 5120:5120 + TOK // 2].bitcast(F16)
        RC = WA[:, 5760:5760 + 2 * TT * E * E].rearrange("p (a t e f) -> p a t e f", a=2, t=TT, e=E)
        RL = WA[:, 6912:6912 + TT * 16].rearrange("p (t n) -> p t n", t=TT)
        RE = WA[:, 7168:7168 + 8 * TT * 16].rearrange("p (a t n) -> p a t n", a=8, t=TT)

        ROPE0 = sb("ROPE0", [P, 2, S], F32)
        ROPE1 = sb("ROPE1", [P, 2, 2, DH1], F32)
        MASK = sb("MASK", [P, P], BF16)
        IDH = sb("IDH", [P, P], F16)
        IDB = sb("IDB", [P, P], BF16)
        IDF = sb("IDF", [P, P], F32)
        ZERO = sb("ZERO", [P, P], F16)
        LNSP = sb("LNSP", [P, 1], F32)
        TRI = sb("TRI", [P, E, E], F32)
        SEL = sb("SEL", [P, JM * P], F16)

        PS = ctx.enter_context(nc.psum_tensor("PS", [P, 8, 512], F32))
        GATE, UP, COMB = 4, 5, 6
        QB, SB, PTB, OB = 4, 5, 6, 7

        dma_x = [sem(f"dma_x{i}") for i in range(2)]
        dma_a = [sem(f"dma_a{i}") for i in range(3)]
        dma_b = [sem(f"dma_b{i}") for i in range(2)]
        dma_c = [sem(f"dma_c{i}") for i in range(2)]
        dma_d, dma_out = sem("dma_d"), sem("dma_out")
        dma_id, dma_wg, dma_const, dma_sel = (sem(n) for n in ("dma_id", "dma_wg", "dma_const", "dma_sel"))
        dma_mask, narrowed = sem("dma_mask"), sem("narrowed")
        zeroed, max_route = sem("zeroed"), sem("max_route")
        w_hi, w_lo, wg_hi, wg_lo = (sem(n) for n in ("w_hi", "w_lo", "wg_hi", "wg_lo"))
        x_sum, bn_half, bn_done = sem("x_sum"), sem("bn_half"), sem("bn_done")
        var_scaled, rstd_done, xn_done = sem("var_scaled"), sem("rstd_done"), sem("xn_done")
        turned, turned_hi, turned_lo = sem("turned"), sem("turned_hi"), sem("turned_lo")
        gate_done, up_done, comb_done = sem("gate_done"), sem("up_done"), sem("comb_done")
        tanh_done, gated, up_mul, comb_mul = sem("tanh_done"), sem("gated"), sem("up_mul"), sem("comb_mul")
        hid_hi, hid_lo, down_done = sem("hid_hi"), sem("hid_lo"), sem("down_done")
        cmb_zero, logits, route, route_act = sem("cmb_zero"), sem("logits"), sem("route"), sem("route_act")
        cmb_done, cmb_turned, cbt_done = sem("cmb_done"), sem("cmb_turned"), sem("cbt_done")
        rope_in, rope_mul, rope_sum = sem("rope_in"), sem("rope_mul"), sem("rope_sum")
        rope_hi, rope_lo = sem("rope_hi"), sem("rope_lo")
        v_in, v_hi, v_lo = sem("v_in"), sem("v_hi"), sem("v_lo")
        scores, max_done, shift_done = sem("scores"), sem("max_done"), sem("shift_done")
        exp_done, recip_done, norm_done = sem("exp_done"), sem("recip_done"), sem("norm_done")
        pt_done, pt_hi, pt_lo = sem("pt_done"), sem("pt_hi"), sem("pt_lo")
        pv_done, ot_hi, ot_lo, proj_done = sem("pv_done"), sem("ot_hi"), sem("ot_lo"), sem("proj_done")
        kz_zero, ones_set = sem("kz_zero"), sem("ones_set")
        qk1_in, v1_in, v1_hi, v1_lo = sem("qk1_in"), sem("v1_in"), sem("v1_hi"), sem("v1_lo")
        rope1_mul, rope1_sum, qk1_hi, qk1_lo = (sem(n) for n in ("rope1_mul", "rope1_sum", "qk1_hi", "qk1_lo"))
        qk1_turned, q1_copied, k1_copied = sem("qk1_turned"), sem("q1_copied"), sem("k1_copied")
        scores1, max1_done, shift1_done, shifted1 = (sem(n) for n in ("scores1", "max1_done", "shift1_done", "shifted1"))
        exp1_done, pt1_done, pt1_hi, pt1_lo = (sem(n) for n in ("exp1_done", "pt1_done", "pt1_hi", "pt1_lo"))
        pv1_done, recip1_done, o1_done, proj1_done = (sem(n) for n in ("pv1_done", "recip1_done", "o1_done", "proj1_done"))

        block = ctx.enter_context(nc.Block())

        def after(eng, semaphore, count):
            if not isinstance(count, int) or count > 0:
                eng.wait_ge(semaphore, count)

        def y_ready(eng, phase, u):
            if phase in GLU_OF:
                f = GLU_OF.index(phase)
                eng.wait_ge(down_done, STEPS[f] + 2 * TILES[f] - (1 if u < NB // 2 else 0))
            elif phase == 1:
                eng.wait_ge(proj_done, NS0 - NB + u + 1)
            else:
                eng.wait_ge(proj1_done, u + 1)

        GLU_OF, GLU_TURN, TILES = [0, 2, 3, 5], [0, 2, 3, 6], [JF, JF, JM, JM]
        STEPS = [0, 2 * JF, 4 * JF, 4 * JF + 2 * JM]
        MSTEPS = [0, 0, 0, 2 * JM]
        Y_SCALE = [0.5 / (SH * SW), 1.0 / (SQ * SW), 0.5 / (SH * SW), 0.5 / (SH * SW), 1.0 / (SQ * SW),
                   0.5 / (SH * SW)]
        W_OF_C = 2 * JF
        W_ALL = W_OF_C + 3 * JF + 1

        def weights(f):
            return WA16 if f < 2 else WC16

        def norm_of(n):
            return n if n < 6 else n - 1

        def y_tiles(u):
            return PS[:, u, :].rearrange("p (t n) -> p t n", t=2)

        def split_list(f, j):
            if f == 0:
                c = 2 * j + 1
                last = isinstance(j, int) and j == JF - 1
                if not last:
                    yield c, WA[:, ds((j + 2) * A_N, A_N)], WA16[:, j + 1, 0, :], WA16[:, j + 1, 1, :], 2
                raw = WB[:, ds((j + 1) * B_N, B_N)].rearrange("p (h n) -> p h n", h=2)
                yield (c + (not last), raw, WB16[:, ds(2 * j, 2), 0, :], WB16[:, ds(2 * j, 2), 1, :],
                       1 if last else 2)
            elif f == 1:
                c = W_OF_C + 3 * j
                yield c, WC[:, ds((2 * j + 1) * C_N, C_N)], WC16[:, 2 * j, 0, :], WC16[:, 2 * j, 1, :], 2
                yield c + 1, WC[:, ds((2 * j + 2) * C_N, C_N)], WC16[:, 2 * j + 1, 0, :], WC16[:, 2 * j + 1, 1, :], 1
                yield c + 2, WD[:, ds((j + 1) * D_N, D_N)], WD16[:, j, 0, :], WD16[:, j, 1, :], 3

        FIRST_SPLIT = (0, WA[:, A_N:2 * A_N], WA16[:, 0, 0, :], WA16[:, 0, 1, :], 2)
        LAST_SPLIT = (W_ALL - 1, WC[:, JM * C_N:], WC16[:, JM - 1, 0, :], WC16[:, JM - 1, 1, :], 2)

        def lagged(h, b, k, n_heads, per):
            if isinstance(h, int) and not 0 <= per * h + b - k < per * n_heads:
                return None
            return (h - 1 if b < k else h), (b - k) % per

        @block.sync
        def _(sp):
            x3 = x_in.rearrange("b (t p) d -> p (b t) d", p=P)
            o3 = out.rearrange("b (t p) d -> p (b t) d", p=P)
            sp.dma_start(X[:, 0:TPH, :], x3[:, 0:TPH, :]).then_inc(dma_x[0], 16)
            sp.dma_start(WA[:, A_N:2 * A_N], wa_in[:, 0:A_N]).then_inc(dma_a[0], 16)
            sp.dma_start(X[:, TPH:, :], x3[:, TPH:, :]).then_inc(dma_x[1], 16)
            sp.dma_start(WB[:, B_N:2 * B_N], wb_in[:, 0:B_N]).then_inc(dma_b[0], 16)
            sp.dma_start(WA[:, 2 * A_N:3 * A_N], wa_in[:, A_N:2 * A_N]).then_inc(dma_a[1], 16)
            sp.dma_start(WA[:, 3 * A_N:], wa_in[:, 2 * A_N:]).then_inc(dma_a[2], 16)
            sp.dma_start(WB[:, 2 * B_N:], wb_in[:, B_N:]).then_inc(dma_b[1], 16)
            sp.dma_start(WC[:, C_N:9 * C_N], wc_in[:, 0:8 * C_N]).then_inc(dma_c[0], 16)
            sp.dma_start(WC[:, 9 * C_N:], wc_in[:, 8 * C_N:]).then_inc(dma_c[1], 16)
            sp.wait_ge(proj_done, NS0)
            sp.dma_start(WD[:, D_N:], wd_in).then_inc(dma_d, 16)
            for u in range(NB):
                sp.wait_ge(x_sum, 5 * NB + u + 1)
                sp.dma_start(o3[:, 2 * u:2 * u + 2, :], X[:, 2 * u:2 * u + 2, :]).then_inc(dma_out, 16)
            sp.wait_ge(dma_out, 16 * NB)

        N_CONST = 3
        ROUTE_STEPS = 14

        @block.gpsimd
        def _(pool):
            pl = nc.gpsimd
            pl.memset(ZERO[:, :], 0.0).then_inc(zeroed, 1)
            pl.memset(NHALF[:, :], -0.5).then_inc(zeroed, 1)
            pl.memset(LNSP[:, :], math.log(SP)).then_inc(zeroed, 1)
            pl.memset(SEL[:, :], 0.0).then_inc(zeroed, 1)
            pool.wait_ge(zeroed, 4)
            pl.dma_start(SEL[0:32, :], sel_in).then_inc(dma_sel, 16)

            def turn(n):
                for u in range(NB):
                    c = norm_of(n) * NB + u
                    pool.wait_ge(bn_done, 2 * c + 2)
                    pl.tensor_scalar(RSTD[:, u, 0, :], MV[:, u, :, 1], SX ** -2, EPS * SX ** -2,
                                     ALU.mult, ALU.add).then_inc(var_scaled, 1)
                    pool.wait_ge(var_scaled, c + 1)
                    pl.tensor_tensor(RSTD[:, u, 1, :], RSTD[:, u, 0, :], NHALF[:, :],
                                     ALU.pow).then_inc(rstd_done, 1)

            def rope_add(r):
                pool.wait_ge(rope_mul, 3 * r + 3)
                after(pool, rope_hi, r)
                after(pool, rope_lo, r)
                pl.tensor_tensor(T3[:, :], T1[:, :], T2[:, :], ALU.add).then_inc(rope_sum, 1)

            def rope_low(r, lo, hi):
                pool.wait_ge(rope_hi, r + 1)
                pl.tensor_tensor(lo, T3[:, :], hi, ALU.subtract).then_inc(rope_lo, 1)

            def key_group(g):
                for hf in range(2):
                    rope_add(2 * g + hf)
                    rope_low(2 * g + hf, KT0[:, 1, g, hf * HALF:(hf + 1) * HALF],
                             KT0[:, 0, g, hf * HALF:(hf + 1) * HALF])

            def q_low(r, hf):
                rope_low(r, QT0[:, 1, hf * HALF:(hf + 1) * HALF], QT0[:, 0, hf * HALF:(hf + 1) * HALF])

            def head(h):
                for b in range(NB):
                    st = NB * h + b
                    unit = None
                    if b == 2 and not (isinstance(h, int) and h == H0 - 1):
                        unit = 2 * KV0 + 2 * h + 2
                    if b == 0 and not (isinstance(h, int) and h == 0):
                        unit = 2 * KV0 + 2 * h + 1
                    if unit is not None:
                        rope_add(unit)
                    pool.wait_ge(recip_done, st + 1)
                    pr = PR0[:, b % 2, :].rearrange("p (q k) -> p q k", q=2)
                    rs = ST[:, b % 2, 3, :].rearrange("p (q k) -> p q k", k=1)
                    pl.tensor_tensor(pr, pr, rs.broadcast_to([P, 2, S]), ALU.mult).then_inc(norm_done, 1)
                    if unit is not None:
                        q_low(unit, 1 if b == 0 else 0)

            def attention0():
                key_group(0)
                with pool.Fori(1, KV0) as g:
                    key_group(g)
                for hf in range(2):
                    rope_add(2 * KV0 + hf)
                    q_low(2 * KV0 + hf, hf)
                head(0)
                with pool.Fori(1, H0 - 1) as h:
                    head(h)
                head(H0 - 1)

            def tile1(tp):
                for a in range(2):
                    t = 2 * tp + a
                    pool.wait_ge(rope1_mul, 3 * t + 3)
                    after(pool, qk1_hi, 2 * t)
                    after(pool, qk1_lo, 2 * t)
                    pl.tensor_tensor(T3[:, :], T1[:, :], T2[:, :], ALU.add).then_inc(rope1_sum, 1)
                    t4 = T3[:, :].rearrange("p (h o n) -> p h o n", o=1, n=DH1)
                    pool.wait_ge(qk1_hi, 2 * t + 2)
                    q4 = QK1[:, a, 0:H1, :].rearrange("p h (c s n) -> p h c s n", c=2, s=2)
                    k4 = QK1[:, a, H1:, :].rearrange("p h (s c n) -> p h s c n", c=2, s=2)
                    pl.tensor_tensor(q4[:, :, :, 1, :], t4[:, 0:H1].broadcast_to([P, H1, 2, DH1]),
                                     q4[:, :, :, 0, :], ALU.subtract).then_inc(qk1_lo, 1)
                    pl.tensor_tensor(k4[:, :, 1, :, :], t4[:, H1:].broadcast_to([P, H1, 2, DH1]),
                                     k4[:, :, 0, :, :], ALU.subtract).then_inc(qk1_lo, 1)

            turn(0)
            turn(1)
            attention0()
            turn(2)
            turn(3)
            pool.wait_ge(down_done, STEPS[2])
            pl.memset(CMB[:, :, :], 0.0).then_inc(cmb_zero, 1)
            pool.wait_ge(proj_done, NS0)
            pool.wait_ge(cmb_zero, 1)
            k6 = KZ1.rearrange("p (h e) t -> p h e t", e=2)
            pl.memset(k6[P // 2:, :, 0, :], 0.0).then_inc(kz_zero, 1)
            pool.wait_ge(kz_zero, 1)
            pl.memset(k6[0:P // 2, :, 1, :], 0.0).then_inc(kz_zero, 1)
            pool.wait_ge(kz_zero, 2)
            pl.memset(VB1[:, 0, :, :, DH1:], 1.0).then_inc(ones_set, 1)
            pool.wait_ge(ones_set, 1)
            pl.memset(VB1[:, 1, :, :, DH1:], 0.0).then_inc(ones_set, 1)
            pool.wait_ge(ones_set, 2)
            turn(4)
            tile1(0)
            with pool.Fori(1, TT // 2) as tp:
                tile1(tp)
            turn(6)

        @block.scalar
        def _(act):
            sc = nc.scalar
            act.dma_start(IDF[:, :], idf_in).then_inc(dma_id, 16)
            act.dma_start(WGR[:, :, :], wg_in).then_inc(dma_wg, 16)
            act.dma_start(T3[:, 0:P], mask_in).then_inc(dma_mask, 16)
            for dst, src in ((ROPE0, rope0_in), (ROPE1, rope1_in), (TRI, tri_in)):
                act.dma_start(dst.ap(), src).then_inc(dma_const, 16)

            def split(c, raw, hi, lo, back):
                after(act, w_lo, c - back + 1)
                sc.activation(hi, raw, ACT.Copy, scale=SW).then_inc(w_hi, 1)

            def turn(n):
                for u in range(NB):
                    act.wait_ge(turned, n * NB + u + 1)
                    sc.activation(XT[:, 0, :, u * S:(u + 1) * S],
                                  PS[:, 7 - u % 2, :].rearrange("p (k t) -> p k t", k=KD),
                                  ACT.Copy).then_inc(turned_hi, 1)

            def glu_tile(f, j):
                splits = list(split_list(f, j))
                for hf in range(2):
                    st = STEPS[f] + 2 * j + hf
                    act.wait_ge(gate_done, st + 1)
                    after(act, gated, st)
                    sc.activation(T1[:, :], PS[:, GATE, :], ACT.Tanh,
                                  scale=0.5 / (SX * SW)).then_inc(tanh_done, 1)
                    if f < 2:
                        act.wait_ge(up_mul, st + 1)
                    else:
                        act.wait_ge(comb_mul, st - STEPS[f] + MSTEPS[f] + 1)
                    after(act, down_done, st - 1)
                    sc.activation(HH[:, hf, 0, :], T3[:, :], ACT.Copy).then_inc(hid_hi, 1)
                    for x in splits[(len(splits) + 1) // 2:] if hf else splits[:(len(splits) + 1) // 2]:
                        split(*x)

            def glu(f):
                glu_tile(f, 0)
                if f == 0:
                    act.wait_ge(dma_a[2], 16)
                    act.wait_ge(dma_b[1], 16)
                with act.Fori(1, TILES[f] - 1) as j:
                    glu_tile(f, j)
                glu_tile(f, TILES[f] - 1)

            def rope_high(r, hi):
                act.wait_ge(rope_sum, r + 1)
                sc.activation(hi, T3[:, :], ACT.Copy).then_inc(rope_hi, 1)

            def key_group(g):
                for hf in range(2):
                    i = 2 * g + hf
                    act.wait_ge(v_in, i + 1)
                    sc.activation(V0[:, 0, i, :], PS[:, 6 + hf, :], ACT.Copy,
                                  scale=SQ / (SX * SW)).then_inc(v_hi, 1)
                    rope_high(i, KT0[:, 0, g, hf * HALF:(hf + 1) * HALF])

            def step(h, b):
                st = NB * h + b
                if item := lagged(h, b, 2, H0, NB):
                    act.wait_ge(pt_done, st - 1)
                    after(act, pv_done, st - 3)
                    sc.activation(PT0[:, item[1] % 2, 0, :], PS[:, PTB, :], ACT.Copy,
                                  scale=SP).then_inc(pt_hi, 1)
                if item := lagged(h, b, 0, H0, NB):
                    act.wait_ge(shift_done, st + 1)
                    for qt in range(2):
                        sc.activation(PR0[:, b % 2, qt * S:(qt + 1) * S], PS[:, SB, qt * S:(qt + 1) * S],
                                      ACT.Exp, bias=ST[:, b % 2, 1, qt:qt + 1], scale=SC0 / SQ ** 2,
                                      accum_out=ST[:, b % 2, 2, qt:qt + 1]).then_inc(exp_done, 1)
                if item := lagged(h, b, 3, H0, NB):
                    act.wait_ge(pv_done, st - 2)
                    sc.activation(OT0[:, item[1] % 2, 0, :], PS[:, OB, 0:S], ACT.Copy,
                                  scale=1 / SP).then_inc(ot_hi, 1)
                if b == 2 and not (isinstance(h, int) and h >= H0 - 1):
                    act.wait_ge(scores, st)
                    rope_high(2 * KV0 + 2 * h + 2, QT0[:, 0, 0:HALF])
                if b == 0 and not (isinstance(h, int) and h in (0, H0)):
                    act.wait_ge(scores, st)
                    rope_high(2 * KV0 + 2 * h + 1, QT0[:, 0, HALF:])

            def head(h):
                for b in range(NB):
                    step(h, b)

            def attention0():
                key_group(0)
                with act.Fori(1, KV0) as g:
                    key_group(g)
                for hf in range(2):
                    rope_high(2 * KV0 + hf, QT0[:, 0, hf * HALF:(hf + 1) * HALF])
                head(0)
                with act.Fori(1, H0 - 1) as h:
                    head(h)
                head(H0 - 1)
                for b in range(3):
                    step(H0, b)

            def route1(n):
                base = 2 * n
                act.wait_ge(route, ROUTE_STEPS * n + 2)
                sc.activation(RE[:, 1, :, 0:E], RE[:, 0, :, 0:E], ACT.Exp).then_inc(route_act, 1)
                sc.activation(RE[:, 1, :, E:GATES], RL[:, :, E:GATES], ACT.Tanh, scale=0.5).then_inc(route_act, 1)

            def copies1(tp, a):
                t = 2 * tp + a
                act.wait_ge(qk1_turned, t + 1)
                q = PS[:, 4 + a, :].bitcast(F16).rearrange("p (h t) -> p h t", t=P)
                k = PS[P // 2:, 6 + a, :].bitcast(F16).rearrange("p (h t) -> p h t", t=P)
                sc.activation(QT1[:, :, ds(t * P, P)], q, ACT.Copy).then_inc(q1_copied, 1)
                if a == 0 and isinstance(tp, int) and tp == 0:
                    act.wait_ge(kz_zero, 2)
                act.wait_ge(k1_copied, t + 1)
                sc.activation(KZ1.rearrange("p (h e) t -> p h e t", e=2)[P // 2:, :, 1, ds(t * P, P)], k,
                              ACT.Copy).then_inc(q1_copied, 1)

            def tile1(tp):
                for a in range(2):
                    t = 2 * tp + a
                    act.wait_ge(v1_in, t + 1)
                    sc.activation(VB1[:, 0, t, :, 0:DH1], PS[:, 2 + a, 0:D].rearrange("p (h n) -> p h n", n=DH1),
                                  ACT.Copy, scale=SQ / (SX * SW)).then_inc(v1_hi, 1)
                    act.wait_ge(rope1_sum, t + 1)
                    after(act, qk1_turned, t - 1)
                    t4 = T3[:, :].rearrange("p (h o n) -> p h o n", o=1, n=DH1)
                    q4 = QK1[:, a, 0:H1, :].rearrange("p h (c s n) -> p h c s n", c=2, s=2)
                    k4 = QK1[:, a, H1:, :].rearrange("p h (s c n) -> p h s c n", c=2, s=2)
                    sc.activation(q4[:, :, :, 0, :], t4[:, 0:H1].broadcast_to([P, H1, 2, DH1]),
                                  ACT.Copy).then_inc(qk1_hi, 1)
                    sc.activation(k4[:, :, 0, :, :], t4[:, H1:].broadcast_to([P, H1, 2, DH1]),
                                  ACT.Copy).then_inc(qk1_hi, 1)
                    if a == 1:
                        copies1(tp, 0)
                    elif not isinstance(tp, int):
                        copies1(tp - 1, 1)

            def step1(p, q):
                g = 4 * p + q
                if item := lagged(p, q, 2, H1 // 2, 4):
                    act.wait_ge(pt1_done, g - 1)
                    after(act, pv1_done, g - 3)
                    sc.activation(PT1[:, item[1] % 2, 0, :], PS[:, 4:6, :].rearrange("p a n -> p (a n)")[:, 0:768],
                                  ACT.Copy).then_inc(pt1_hi, 1)
                if item := lagged(p, q, 0, H1 // 2, 4):
                    act.wait_ge(shifted1, g + 1)
                    sc.activation(PR1[:, q % 2, :].rearrange("p (b n) -> p b n", b=2),
                                  PS[:, 2 * (q % 2):2 * (q % 2) + 2, 0:384], ACT.Exp, bias=LNSP[:, :],
                                  scale=SC1 / SQ ** 2).then_inc(exp1_done, 1)

            def attention1():
                tile1(0)
                with act.Fori(1, TT // 2) as tp:
                    tile1(tp)
                copies1(TT // 2 - 1, 1)
                for q in range(4):
                    step1(0, q)
                with act.Fori(1, H1 // 2) as p:
                    for q in range(4):
                        step1(p, q)
                step1(H1 // 2, 0)
                step1(H1 // 2, 1)
                turn(5)

            act.wait_ge(dma_a[0], 16)
            split(*FIRST_SPLIT)
            turn(0)
            act.wait_ge(dma_wg, 16)
            sc.activation(WGS[:, 0, :, :], WGR[:, :, :], ACT.Copy, scale=SW).then_inc(wg_hi, 1)
            act.wait_ge(dma_b[0], 16)
            act.wait_ge(dma_a[1], 16)
            glu(0)
            turn(1)
            act.wait_ge(zeroed, 4)
            attention0()
            turn(2)
            for x in dma_c + [dma_d]:
                act.wait_ge(x, 16)
            glu(1)
            split(*LAST_SPLIT)
            turn(3)
            route1(0)
            glu(2)
            turn(4)
            attention1()
            turn(6)
            route1(1)
            glu(3)


        @block.vector
        def _(dve):
            v = nc.vector

            def split(c, raw, hi, lo, back):
                dve.wait_ge(w_hi, c + 1)
                after(dve, w_lo, c - back + 1)
                v.scalar_tensor_tensor(lo, raw, SW, hi, ALU.mult, ALU.subtract).then_inc(w_lo, 1)

            def add_phase(phase, u):
                y_ready(dve, phase, u)
                v.scalar_tensor_tensor(X[:, 2 * u:2 * u + 2, :], y_tiles(u), Y_SCALE[phase],
                                       X[:, 2 * u:2 * u + 2, :], ALU.mult, ALU.add).then_inc(x_sum, 1)

            def turn(n, phase=None):
                for i in range(NB + 2):
                    if i < NB and n != 5:
                        u, c = i, norm_of(n) * NB + i
                        if phase is None:
                            dve.wait_ge(dma_x[u // 2], 16)
                        else:
                            add_phase(phase, u)
                            dve.wait_ge(x_sum, phase * NB + u + 1)
                        for t in range(2):
                            v.bn_stats(BST[:, u, t, :], X[:, 2 * u + t, :]).then_inc(bn_half, 1)
                        dve.wait_ge(bn_half, 2 * c + 2)
                        for t in range(2):
                            v.bn_aggr(MV[:, u, t, :], BST[:, u, t, :]).then_inc(bn_done, 1)
                    if 1 <= i <= NB and n != 5:
                        u, c = i - 1, norm_of(n) * NB + i - 1
                        dve.wait_ge(rstd_done, c + 1)
                        if u >= 2:
                            dve.wait_ge(turned, n * NB + u - 1)
                        for t in range(2):
                            v.tensor_scalar(XN[:, u % 2, t, :], X[:, 2 * u + t, :], MV[:, u, t, 0:1],
                                            RSTD[:, u, 1, t:t + 1], ALU.subtract, ALU.mult).then_inc(xn_done, 1)
                    if i >= 2:
                        u = i - 2
                        dve.wait_ge(turned_hi, n * NB + u + 1)
                        v.tensor_tensor(XT[:, 1, :, u * S:(u + 1) * S],
                                        PS[:, 7 - u % 2, :].rearrange("p (k t) -> p k t", k=KD),
                                        XT[:, 0, :, u * S:(u + 1) * S], ALU.subtract).then_inc(turned_lo, 1)

            def glu_tile(f, j):
                splits = list(split_list(f, j))
                for hf in range(2):
                    st = STEPS[f] + 2 * j + hf
                    dve.wait_ge(tanh_done, st + 1)
                    after(dve, up_mul, st)
                    v.scalar_tensor_tensor(T2[:, :], T1[:, :], 1.0, PS[:, GATE, :], ALU.add,
                                           ALU.mult).then_inc(gated, 1)
                    dve.wait_ge(up_done, st + 1)
                    dve.wait_ge(gated, st + 1)
                    after(dve, hid_lo, st)
                    scale = 0.5 * SH / (SX * SW) ** 2 / (1 if f < 2 else SR)
                    v.scalar_tensor_tensor(T3[:, :], T2[:, :], scale, PS[:, UP, :], ALU.mult,
                                           ALU.mult).then_inc(up_mul, 1)
                    if f >= 2:
                        dve.wait_ge(comb_done, MSTEPS[f] + 2 * j + hf + 1)
                        dve.wait_ge(up_mul, st + 1)
                        v.tensor_tensor(T3[:, :], T3[:, :], PS[:, COMB, :], ALU.mult).then_inc(comb_mul, 1)
                    dve.wait_ge(hid_hi, st + 1)
                    v.tensor_tensor(HH[:, hf, 1, :], T3[:, :], HH[:, hf, 0, :], ALU.subtract).then_inc(hid_lo, 1)
                    for x in splits[(len(splits) + 1) // 2:] if hf else splits[:(len(splits) + 1) // 2]:
                        split(*x)

            def glu(f):
                glu_tile(f, 0)
                with dve.Fori(1, TILES[f] - 1) as j:
                    glu_tile(f, j)
                glu_tile(f, TILES[f] - 1)

            def rope_products(r, bank, parts=(0, 1, 2)):
                if 0 in parts:
                    dve.wait_ge(rope_in, r + 1)
                    after(dve, rope_sum, r)
                ps = PS[:, bank, :].rearrange("p (b t) -> p b t", b=2)
                t1, t2 = (x[:, :].rearrange("p (b t) -> p b t", b=2) for x in (T1, T2))
                lo, hi = slice(0, P // 2), slice(P // 2, P)
                for dst, src, table in [(t1, ps, ROPE0[:, 0:1, :]), (t2[lo], ps[hi], ROPE0[lo, 1:2, :]),
                                        (t2[hi], ps[lo], ROPE0[hi, 1:2, :])][parts[0]:parts[-1] + 1]:
                    v.tensor_tensor(dst, src, table.broadcast_to([dst.shape[0], 2, S]),
                                    ALU.mult).then_inc(rope_mul, 1)

            def key_group(g):
                for hf in range(2):
                    i = 2 * g + hf
                    rope_products(i, QB + hf)
                    dve.wait_ge(v_hi, i + 1)
                    v.scalar_tensor_tensor(V0[:, 1, i, :], PS[:, 6 + hf, :], SQ / (SX * SW), V0[:, 0, i, :],
                                           ALU.mult, ALU.subtract).then_inc(v_lo, 1)

            def step(h, b):
                st = NB * h + b
                if lagged(h, b, 0, H0, NB):
                    dve.wait_ge(scores, st + 1)
                    v.tensor_reduce(ST[:, b % 2, 0, :], PS[:, SB, :].rearrange("p (q k) -> p q k", q=2),
                                    AX.X, ALU.max).then_inc(max_done, 1)
                    dve.wait_ge(max_done, st + 1)
                    v.tensor_scalar(ST[:, b % 2, 1, :], ST[:, b % 2, 0, :], -SC0 / SQ ** 2, None,
                                    ALU.mult).then_inc(shift_done, 1)
                if item := lagged(h, b, 2, H0, NB):
                    a = item[1] % 2
                    dve.wait_ge(pt_hi, st - 1)
                    v.scalar_tensor_tensor(PT0[:, a, 1, :], PS[:, PTB, :], SP, PT0[:, a, 0, :], ALU.mult,
                                           ALU.subtract).then_inc(pt_lo, 1)
                if lagged(h, b, 0, H0, NB):
                    dve.wait_ge(exp_done, 2 * st + 2)
                    v.reciprocal(ST[:, b % 2, 3, :], ST[:, b % 2, 2, :]).then_inc(recip_done, 1)
                if item := lagged(h, b, 3, H0, NB):
                    a = item[1] % 2
                    dve.wait_ge(ot_hi, st - 2)
                    v.scalar_tensor_tensor(OT0[:, a, 1, :], PS[:, OB, 0:S], 1 / SP, OT0[:, a, 0, :], ALU.mult,
                                           ALU.subtract).then_inc(ot_lo, 1)
                if not (isinstance(h, int) and h >= H0 - 1):
                    rope_products(2 * KV0 + 2 * h + 2 + b // 2, QB, (1, 2) if b % 2 else (0,))

            def head(h):
                for b in range(NB):
                    step(h, b)

            def attention0():
                dve.wait_ge(dma_const, 16 * N_CONST)
                key_group(0)
                with dve.Fori(1, KV0) as g:
                    key_group(g)
                for hf in range(2):
                    rope_products(2 * KV0 + hf, QB)
                head(0)
                with dve.Fori(1, H0 - 1) as h:
                    head(h)
                head(H0 - 1)
                for b in range(3):
                    step(H0, b)

            def routing(n):
                made = [ROUTE_STEPS * n]

                def link(ins):
                    made[0] += 1
                    ins.then_inc(route, 1)
                    dve.wait_ge(route, made[0])

                def per_expert(x):
                    return x.rearrange("p t (o n) -> p t o n", o=1)[:, :, 0, 0:1].broadcast_to([P, TT, E])

                l, m = RL[:, :, 0:E], RE[:, 2, :, 0:1]
                dve.wait_ge(logits, n + 1)
                link(v.tensor_scalar(RL[:, :, 0:GATES], PS[:, 7, 0:TT * 16].rearrange("p (t n) -> p t n", t=TT)
                                     [:, :, 0:GATES], 1 / (SX * SW), None, ALU.mult))
                v.tensor_reduce(m, l, AX.X, ALU.max).then_inc(max_route, 1)
                dve.wait_ge(max_route, n + 1)
                link(v.tensor_tensor(RE[:, 0, :, 0:E], l, per_expert(m), ALU.subtract))
                lf = RL[:, :, 0:E].rearrange("p t (o e) -> p t o e", o=1).broadcast_to([P, TT, E, E])
                le = RL[:, :, 0:E].rearrange("p t (e o) -> p t e o", o=1).broadcast_to([P, TT, E, E])
                link(v.tensor_tensor(RC[:, 0], lf, le, ALU.is_equal))
                link(v.tensor_tensor(RC[:, 0], RC[:, 0], TRI[:, :, :].rearrange("p (o e) f -> p o e f", o=1)
                                     .broadcast_to([P, TT, E, E]), ALU.mult))
                link(v.tensor_tensor(RC[:, 1], lf, le, ALU.is_gt))
                link(v.tensor_tensor(RC[:, 0], RC[:, 0], RC[:, 1], ALU.add))
                link(v.tensor_reduce(RE[:, 3, :, 0:E], RC[:, 0], AX.X, ALU.add))
                dve.wait_ge(route_act, 2 * n + 2)
                link(v.scalar_tensor_tensor(RE[:, 4, :, 0:E], RE[:, 3, :, 0:E], 2.0, RE[:, 1, :, 0:E], ALU.is_lt,
                                            ALU.mult))
                link(v.tensor_reduce(RE[:, 5, :, 0:1], RE[:, 4, :, 0:E], AX.X, ALU.add))
                link(v.reciprocal(RE[:, 6, :, 0:1], RE[:, 5, :, 0:1]))
                link(v.scalar_tensor_tensor(RE[:, 7, :, 0:E], RE[:, 4, :, 0:E], SR, per_expert(RE[:, 6, :, 0:1]),
                                            ALU.mult, ALU.mult))
                link(v.tensor_scalar(RE[:, 7, :, E:GATES], RE[:, 1, :, E:GATES], 0.5 * SR, 0.5 * SR, ALU.mult,
                                     ALU.add))
                dve.wait_ge(cmb_zero, 1)
                link(v.tensor_copy(CMB[:, :, 0:GATES], RE[:, 7, :, 0:GATES]))
                link(v.tensor_tensor(CMB[:, :, GATES:2 * GATES], RE[:, 7, :, 0:GATES], CMB[:, :, 0:GATES],
                                     ALU.subtract))
                assert made[0] == ROUTE_STEPS * (n + 1), made
                dve.wait_ge(cmb_turned, n + 1)
                v.tensor_copy(CBT, PS[:, 7, :].bitcast(F16)).then_inc(cbt_done, 1)

            def copies1(tp, a):
                t = 2 * tp + a
                dve.wait_ge(qk1_turned, t + 1)
                if a == 0 and isinstance(tp, int) and tp == 0:
                    dve.wait_ge(kz_zero, 2)
                k = PS[0:P // 2, 6 + a, :].bitcast(F16).rearrange("p (h t) -> p h t", t=P)
                v.tensor_copy(KZ1.rearrange("p (h e) t -> p h e t", e=2)[0:P // 2, :, 0, ds(t * P, P)],
                              k).then_inc(k1_copied, 1)

            def tile1(tp):
                for a in range(2):
                    t = 2 * tp + a
                    dve.wait_ge(qk1_in, t + 1)
                    after(dve, rope1_sum, t)
                    ps = PS[:, a, :].rearrange("p (h n) -> p h n", n=DH1)
                    t1 = T1[:, :].rearrange("p (h n) -> p h n", n=DH1)
                    p2, t2 = (x.rearrange("p (h n e) -> p h n e", n=DH1 // 2, e=2) for x in (PS[:, a, :], T2[:, :]))
                    sn = ROPE1[:, a:a + 1, 1, :].rearrange("p o (n e) -> p o n e", e=2)
                    v.tensor_tensor(t1, ps, ROPE1[:, a:a + 1, 0, :].broadcast_to([P, 2 * H1, DH1]),
                                    ALU.mult).then_inc(rope1_mul, 1)
                    for e in range(2):
                        v.tensor_tensor(t2[:, :, :, e], p2[:, :, :, 1 - e],
                                        sn[:, :, :, e].broadcast_to([P, 2 * H1, DH1 // 2]),
                                        ALU.mult).then_inc(rope1_mul, 1)
                    dve.wait_ge(v1_hi, t + 1)
                    v.scalar_tensor_tensor(VB1[:, 1, t, :, 0:DH1], PS[:, 2 + a, 0:D].rearrange("p (h n) -> p h n", n=DH1),
                                           SQ / (SX * SW), VB1[:, 0, t, :, 0:DH1], ALU.mult,
                                           ALU.subtract).then_inc(v1_lo, 1)
                    if a == 1:
                        copies1(tp, 0)
                    elif not isinstance(tp, int):
                        copies1(tp - 1, 1)

            def step1(p, q):
                g = 4 * p + q
                if lagged(p, q, 0, H1 // 2, 4):
                    a = q % 2
                    dve.wait_ge(scores1, g + 1)
                    for qt, cols in ((0, slice(0, P)), (1, slice(P, 3 * P))):
                        v.tensor_reduce(ST[:, a, qt, :], PS[:, 2 * a:2 * a + 2, cols], AX.X,
                                        ALU.max).then_inc(max1_done, 1)
                    dve.wait_ge(max1_done, 2 * g + 2)
                    v.tensor_scalar(MB1[:, a, :], ST[:, a, 0:2, :].rearrange("p q b -> p (q b)"), -1.0, None,
                                    ALU.mult).then_inc(shift1_done, 1)
                if item := lagged(p, q, 2, H1 // 2, 4):
                    a = item[1] % 2
                    dve.wait_ge(pt1_hi, g - 1)
                    v.tensor_tensor(PT1[:, a, 1, :], PS[:, 4:6, :].rearrange("p a n -> p (a n)")[:, 0:768],
                                    PT1[:, a, 0, :], ALU.subtract).then_inc(pt1_lo, 1)
                if item := lagged(p, q, 3, H1 // 2, 4):
                    pp, qq = item
                    a = qq % 2
                    o = PS[:, 6 + a, 0:128].rearrange("p (t n) -> p t n", t=4)
                    dve.wait_ge(pv1_done, g - 2)
                    v.reciprocal(R1[:, a, :].rearrange("p (t n) -> p t n", n=1), o[:, :, DH1:VC1]).then_inc(recip1_done, 1)
                    dve.wait_ge(recip1_done, g - 2)
                    v.tensor_tensor(O1S[:, 4 * a:4 * a + 4, ds((2 * pp + qq // 2) * DH1, DH1)], o[:, :, 0:DH1],
                                    R1[:, a, :].rearrange("p (t n) -> p t n", n=1).broadcast_to([P, 4, DH1]),
                                    ALU.mult).then_inc(o1_done, 1)

            def attention1():
                tile1(0)
                with dve.Fori(1, TT // 2) as tp:
                    tile1(tp)
                copies1(TT // 2 - 1, 1)
                for q in range(4):
                    step1(0, q)
                with dve.Fori(1, H1 // 2) as p:
                    for q in range(4):
                        step1(p, q)
                for q in range(3):
                    step1(H1 // 2, q)
                turn(5)

            dve.wait_ge(dma_id, 16)
            v.tensor_copy(IDH[:, :], IDF[:, :]).then_inc(narrowed, 1)
            v.tensor_copy(IDB[:, :], IDF[:, :]).then_inc(narrowed, 1)
            dve.wait_ge(dma_mask, 16)
            v.tensor_copy(MASK[:, :], T3[:, 0:P]).then_inc(narrowed, 1)
            split(*FIRST_SPLIT)
            turn(0)
            dve.wait_ge(narrowed, 3)
            dve.wait_ge(wg_hi, 1)
            v.scalar_tensor_tensor(WGS[:, 1, :, :], WGR[:, :, :], SW, WGS[:, 0, :, :], ALU.mult,
                                   ALU.subtract).then_inc(wg_lo, 1)
            glu(0)
            turn(1, 0)
            attention0()
            turn(2, 1)
            glu(1)
            split(*LAST_SPLIT)
            turn(3, 2)
            routing(0)
            glu(2)
            turn(4, 3)
            attention1()
            turn(6, 4)
            routing(1)
            glu(3)
            for u in range(NB):
                add_phase(5, u)

        @block.tensor
        def _(pe):
            te = nc.tensor

            def product(dst, left, right, first=True, last=True):
                for n, (a, b) in enumerate(PASSES):
                    ins = te.matmul(dst, left(a), right(b), start=first and n == 0, stop=last and n == 2,
                                    skip_group_check=True)
                return ins

            def turn(n, clear=True):
                for u in range(NB):
                    if n == 5:
                        pe.wait_ge(o1_done, NG1)
                    else:
                        pe.wait_ge(xn_done, 2 * (norm_of(n) * NB + u) + 2)
                    if u >= 2:
                        pe.wait_ge(turned_lo, n * NB + u - 1)
                    for t in range(2):
                        for k in range(KD):
                            src = O1S[:, 2 * u + t, k * P:(k + 1) * P] if n == 5 else XN[:, u % 2, t, k * P:(k + 1) * P]
                            ins = te.transpose(PS[:, 7 - u % 2, k * S + t * P:k * S + (t + 1) * P], src, IDF[:, :])
                    ins.then_inc(turned, 1)
                    if clear:
                        te.matmul(PS[:, u, :], ZERO[:, :], SEL[:, 0:512], start=True, stop=False,
                                  skip_group_check=True)

            def down(f, j, hf, st):
                pe.wait_ge(hid_lo, st + 1)
                w = weights(f)
                for t in range(TPH):
                    u = (hf * TPH + t) // 2
                    ins = product(y_tiles(u)[:, t % 2, :], lambda s: HH[:, hf, s, t * P:(t + 1) * P],
                                  lambda s: w[:, j, s, 2 * D:3 * D], first=False, last=False)
                ins.then_inc(down_done, 1)

            def glu_tile(f, j):
                w = weights(f)
                for hf in range(2):
                    st = STEPS[f] + 2 * j + hf
                    tok = slice(hf * HALF, (hf + 1) * HALF)
                    if isinstance(j, int) and j == 0:
                        pe.wait_ge(turned_lo, GLU_TURN[f] * NB + 2 * hf + 2)
                    if f == 0 and hf == 0:
                        pe.wait_ge(w_lo, 1 if isinstance(j, int) and j == 0 else 2 * j)
                    after(pe, gated, st)
                    for k in range(KD):
                        ins = product(PS[:, GATE, :], lambda s: w[:, j, s, k * P:(k + 1) * P],
                                      lambda s: XT[:, s, k, tok], k == 0, k == KD - 1)
                    ins.then_inc(gate_done, 1)
                    after(pe, up_mul, st)
                    for k in range(KD):
                        ins = product(PS[:, UP, :], lambda s: w[:, j, s, D + k * P:D + (k + 1) * P],
                                      lambda s: XT[:, s, k, tok], k == 0, k == KD - 1)
                    ins.then_inc(up_done, 1)
                    if f >= 2:
                        if isinstance(j, int) and j == 0 and hf == 0:
                            combine_turn(f - 2)
                        after(pe, comb_mul, MSTEPS[f] + 2 * j + hf)
                        te.matmul(PS[:, COMB, :], SEL[:, ds(j * P, P)], CBT[:, tok], start=True,
                                  stop=True).then_inc(comb_done, 1)
                    if hf:
                        down(f, j, 0, st - 1)
                    elif not isinstance(j, int) or j:
                        down(f, j - 1, 1, st - 1)

            def glu(f):
                glu_tile(f, 0)
                with pe.Fori(1, TILES[f] - 1) as j:
                    glu_tile(f, j)
                glu_tile(f, TILES[f] - 1)
                down(f, TILES[f] - 1, 1, STEPS[f] + 2 * TILES[f] - 1)

            def route_logits(n, turn_n):
                pe.wait_ge(turned_lo, turn_n * NB + 4)
                for t in range(TT):
                    for k in range(KD):
                        ins = product(PS[:, 7, t * 16:(t + 1) * 16], lambda s: XT[:, s, k, t * P:(t + 1) * P],
                                      lambda s: WGS[:, s, k, :], k == 0, k == KD - 1)
                ins.then_inc(logits, 1)

            def combine_turn(n):
                pe.wait_ge(route, ROUTE_STEPS * (n + 1))
                for t in range(TT):
                    ins = te.transpose(PS[:, 7, :].bitcast(F16)[:, t * P:(t + 1) * P], CMB[:, t, :], IDH[:, :])
                ins.then_inc(cmb_turned, 1)
                pe.wait_ge(cbt_done, n + 1)

            def key_group(g):
                for hf in range(2):
                    i = 2 * g + hf
                    tok = slice(hf * HALF, (hf + 1) * HALF)
                    if isinstance(g, int) and g == 0:
                        pe.wait_ge(turned_lo, 1 * NB + 2 * hf + 2)
                    after(pe, rope_mul, 3 * i - 3)
                    for k in range(KD):
                        ins = product(PS[:, QB + hf, :], lambda s: WA16[:, g, s, GLU + k * P:GLU + (k + 1) * P],
                                      lambda s: XT[:, s, k, tok], k == 0, k == KD - 1)
                    ins.then_inc(rope_in, 1)
                    if isinstance(g, int) and g == 0 and hf == 0:
                        pe.wait_ge(turned_lo, 1 * NB + 4)
                    after(pe, v_lo, i - 1)
                    for k in range(KD):
                        ins = product(PS[:, 6 + hf, :].rearrange("p (c n) -> p c n", c=2),
                                      lambda s: XT[:, s, k, ds(i * P, P)],
                                      lambda s: WA16[:, 4 + 2 * k:6 + 2 * k, s, GLU:], k == 0, k == KD - 1)
                    ins.then_inc(v_in, 1)

            def queries(h, hf):
                r = 2 * KV0 + 2 * h + hf
                pe.wait_ge(rope_mul, 3 * r)
                for k in range(KD):
                    ins = product(PS[:, QB, :], lambda s: WB16[:, h, s, k * P:(k + 1) * P],
                                  lambda s: XT[:, s, k, hf * HALF:(hf + 1) * HALF], k == 0, k == KD - 1)
                ins.then_inc(rope_in, 1)

            def step(h, b):
                st = NB * h + b
                if lagged(h, b, 0, H0, NB):
                    g = h // GRP
                    if b % 2 == 0:
                        pe.wait_ge(rope_lo, 2 * KV0 + 2 * h + b // 2 + 1)
                    after(pe, exp_done, 2 * st)
                    for qt in range(2):
                        q0 = b * S + qt * P
                        ins = product(PS[:, SB, qt * S:(qt + 1) * S], lambda s: QT0[:, s, q0:q0 + P],
                                      lambda s: KT0[:, s, g, b * S:(b + 1) * S], True, qt == 1)
                        if qt == 0:
                            te.matmul(PS[:, SB, P:S], IDB[:, :], MASK[:, :], start=False, stop=True,
                                      skip_group_check=True)
                    ins.then_inc(scores, 1)
                if item := lagged(h, b, 2, H0, NB):
                    a = item[1] % 2
                    pe.wait_ge(norm_done, st - 1)
                    after(pe, pt_lo, st - 2)
                    for qt in range(2):
                        for kt in range(2):
                            ins = te.transpose(PS[:, PTB, kt * S + qt * P:kt * S + (qt + 1) * P],
                                               PR0[:, a, qt * S + kt * P:qt * S + (kt + 1) * P], IDF[:, :])
                    ins.then_inc(pt_done, 1)
                if b % 2 == 0 and not (isinstance(h, int) and h >= H0 - 1):
                    queries(h + 1, b // 2)
                if item := lagged(h, b, 3, H0, NB):
                    hh, bb = item
                    g = hh // GRP
                    pe.wait_ge(pt_lo, st - 2)
                    after(pe, ot_lo, st - 3)
                    for kt in range(2):
                        ins = product(PS[:, OB, 0:S], lambda s: V0[:, s, 2 * bb + kt, ds(g * P, P)],
                                      lambda s: PT0[:, bb % 2, s, kt * S:(kt + 1) * S], kt == 0, kt == 1)
                    ins.then_inc(pv_done, 1)
                if item := lagged(h, b, 4, H0, NB):
                    hh, bb = item
                    pe.wait_ge(ot_lo, st - 3)
                    for t in range(2):
                        ins = product(y_tiles(bb)[:, t, :], lambda s: OT0[:, bb % 2, s, t * P:(t + 1) * P],
                                      lambda s: WB16[:, hh, s, D:2 * D], False, False)
                    ins.then_inc(proj_done, 1)

            def head(h):
                for b in range(NB):
                    step(h, b)

            def attention0():
                pe.wait_ge(dma_const, 16 * N_CONST)
                key_group(0)
                with pe.Fori(1, KV0) as g:
                    key_group(g)
                queries(0, 0)
                queries(0, 1)
                head(0)
                with pe.Fori(1, H0 - 1) as h:
                    head(h)
                head(H0 - 1)
                for b in range(4):
                    step(H0, b)

            def turn_qk(tp, a):
                t = 2 * tp + a
                pe.wait_ge(qk1_lo, 2 * t + 2)
                after(pe, q1_copied, 2 * t - 2)
                for x in range(H1):
                    src = QK1[:, a, :, :].rearrange("p h n -> p (h n)")[:, x * P:(x + 1) * P]
                    dst = PS[:, (4 if x < H1 // 2 else 6) + a, :].bitcast(F16)
                    y = x % (H1 // 2)
                    ins = te.transpose(dst[:, y * P:(y + 1) * P], src, IDH[:, :])
                ins.then_inc(qk1_turned, 1)

            def tile1(tp):
                for a in range(2):
                    t = 2 * tp + a
                    after(pe, rope1_mul, 3 * t - 3)
                    for k in range(KD):
                        ins = product(PS[:, a, :].rearrange("p (c n) -> p c n", c=2),
                                      lambda s: XT[:, s, k, ds(t * P, P)],
                                      lambda s: WD16[:, 3 * k:3 * k + 2, s, :], k == 0, k == KD - 1)
                    ins.then_inc(qk1_in, 1)
                    after(pe, v1_lo, t - 1)
                    for k in range(KD):
                        ins = product(PS[:, 2 + a, 0:D], lambda s: XT[:, s, k, ds(t * P, P)],
                                      lambda s: WD16[:, 3 * k + 2, s, :], k == 0, k == KD - 1)
                    ins.then_inc(v1_in, 1)
                    if a == 1:
                        turn_qk(tp, 0)
                    elif not isinstance(tp, int):
                        turn_qk(tp - 1, 1)

            def step1(p, q):
                g = 4 * p + q
                if lagged(p, q, 0, H1 // 2, 4):
                    a, h = q % 2, 2 * p + q // 2
                    after(pe, exp1_done, g - 1)
                    for i in range(2):
                        b, bank = 2 * a + i, 2 * a + i
                        for qt, c0 in ((0, 0), (1, P)):
                            te.matmul(PS[:, bank, c0:c0 + (qt + 1) * P], QT1[:, p, b * S + qt * P:b * S + (qt + 1) * P],
                                      KZ1[:, h, b * S:b * S + (qt + 1) * P], start=qt == 0, stop=False,
                                      skip_group_check=True)
                            ins = te.matmul(PS[:, bank, 2 * c0:2 * c0 + P], IDB[:, :], MASK[:, :], start=False,
                                            stop=False, skip_group_check=True)
                    ins.then_inc(scores1, 1)
                if item := lagged(p, q, 2, H1 // 2, 4):
                    a = item[1] % 2
                    pe.wait_ge(exp1_done, g - 1)
                    after(pe, pt1_lo, g - 2)
                    for i in range(2 * BLK1):
                        ins = te.transpose(PS[:, 4 + i // 4, (i % 4) * P:(i % 4 + 1) * P],
                                           PR1[:, a, i * P:(i + 1) * P], IDF[:, :])
                    ins.then_inc(pt1_done, 1)
                if item := lagged(p, q, 3, H1 // 2, 4):
                    pp, qq = item
                    a, h = qq % 2, 2 * pp + qq // 2
                    pe.wait_ge(pt1_lo, g - 2)
                    for i in range(2):
                        for qt in range(2):
                            for kt in range(qt + 1):
                                blk = BLK1 * i + qt + kt
                                ins = product(PS[:, 6 + a, (2 * i + qt) * 32:(2 * i + qt) * 32 + VC1],
                                              lambda s: PT1[:, a, s, blk * P:(blk + 1) * P],
                                              lambda s: VB1[:, s, 4 * a + 2 * i + kt, h, :], kt == 0, kt == qt)
                    ins.then_inc(pv1_done, 1)
                if lagged(p, q, 0, H1 // 2, 4):
                    pe.wait_ge(shift1_done, g + 1)
                    for i in range(2):
                        for qt, c0 in ((0, 0), (1, P)):
                            n = (qt + 1) * P
                            ins = te.matmul(PS[:, 2 * a_of(q) + i, c0:c0 + n], IDB[:, :],
                                            MB1[:, a_of(q), 2 * qt + i:2 * qt + i + 1].broadcast_to([P, n]),
                                            start=False, stop=qt == 1, skip_group_check=True)
                    ins.then_inc(shifted1, 1)

            def a_of(q):
                return q % 2

            def attention1():
                pe.wait_ge(turned_lo, 4 * NB + 4)
                pe.wait_ge(ones_set, 2)
                tile1(0)
                with pe.Fori(1, TT // 2) as tp:
                    tile1(tp)
                turn_qk(TT // 2 - 1, 1)
                pe.wait_ge(q1_copied, 2 * TT)
                for q in range(4):
                    step1(0, q)
                with pe.Fori(1, H1 // 2) as p:
                    for q in range(4):
                        step1(p, q)
                for q in range(3):
                    step1(H1 // 2, q)
                turn(5, clear=False)
                for u in range(NB):
                    pe.wait_ge(turned_lo, 5 * NB + u + 1)
                    for t in range(2):
                        for k in range(KD):
                            ins = product(y_tiles(u)[:, t, :], lambda s: XT[:, s, k, (2 * u + t) * P:(2 * u + t + 1) * P],
                                          lambda s: WD16[:, 6 + k, s, :], k == 0, k == KD - 1)
                    ins.then_inc(proj1_done, 1)

            pe.wait_ge(dma_id, 16)
            pe.wait_ge(narrowed, 3)
            pe.wait_ge(zeroed, 4)
            pe.wait_ge(dma_sel, 16)
            turn(0)
            glu(0)
            turn(1)
            attention0()
            turn(2)
            glu(1)
            turn(3)
            pe.wait_ge(w_lo, W_ALL)
            pe.wait_ge(wg_lo, 1)
            route_logits(0, 3)
            glu(2)
            turn(4, clear=False)
            attention1()
            turn(6)
            route_logits(1, 6)
            glu(3)


def _pack(np, t):
    def feats(w):
        return np.stack([w[:P], w[P:]], axis=1)

    def glu(gate, up, down):
        n = -(-gate.shape[1] // P) * P
        g, u, d = np.zeros((D, n), np.float32), np.zeros((D, n), np.float32), np.zeros((n, D), np.float32)
        g[:, :gate.shape[1]], u[:, :gate.shape[1]], d[:gate.shape[1]] = gate, up, down
        return [np.concatenate([feats(g[:, c:c + P]).reshape(P, D), feats(u[:, c:c + P]).reshape(P, D),
                                d[c:c + P]], axis=1) for c in range(0, n, P)]

    gu, wk, wv = t["L0_ffn_w_gate_up"], t["L0_attn_Wk"], t["L0_attn_Wv"]
    a = glu(gu[:INTER].T, gu[INTER:].T, t["L0_ffn_w_down"].T)
    kv = [feats(wk[g * P:(g + 1) * P].T).reshape(P, D) for g in range(KV0)]
    kv += [wv[(i % 2) * D:(i % 2 + 1) * D, (i // 2) * P:(i // 2 + 1) * P].T for i in range(4)]
    wa = np.concatenate([x for pair in zip(a, kv) for x in pair], axis=1)
    wq, wo = t["L0_attn_Wq"], t["L0_attn_Wo"]
    wb = np.concatenate([x for h in range(H0) for x in (feats(wq[h * P:(h + 1) * P].T).reshape(P, D),
                                                        wo[:, h * P:(h + 1) * P].T)], axis=1)
    side = lambda n, s: np.concatenate([t["L1_ffn_w_" + n].transpose(1, 0, 2).reshape(D, E * I_EXP), t["L1_ffn_sw_" + s]], axis=1)
    wc = np.concatenate(glu(side("gate", "gate"), side("up", "up"),
                            np.concatenate([t["L1_ffn_w_down"].reshape(E * I_EXP, D), t["L1_ffn_sw_down"]])), axis=1)
    qkv, wo1 = t["L1_attn_W_qkv"].T, t["L1_attn_W_o"].T
    wd = np.concatenate([qkv[:P], qkv[P:], wo1[:P], wo1[P:]], axis=1)
    wg = np.zeros((D, 16), np.float32)
    wg[:, :E], wg[:, E:E + 1] = t["L1_ffn_gate_w"].T, t["L1_ffn_shared_gate_w"]
    return [wa, wb, wc, wd, feats(wg)]


def _tables(np):
    f = np.float32
    scale = f(SQ / (SX * SW))

    def angles(n, half):
        inv = f(1.0) / np.power(f(10000.0), (np.arange(0, 2 * half, 2, dtype=f) / f(2 * half)))
        return np.repeat(np.arange(n, dtype=f)[:, None] * inv[None, :], 2, axis=1)

    a0 = angles(S, P // 2).T
    sign0 = np.where(np.arange(P) < P // 2, f(-1), f(1))[:, None]
    rope0 = np.stack([np.cos(a0) * scale, np.sin(a0) * sign0 * scale], axis=1)
    a1 = angles(S, DH1 // 2).reshape(2, P, DH1).transpose(1, 0, 2)
    sign1 = np.where(np.arange(DH1) % 2 == 0, f(-1), f(1))
    rope1 = np.stack([np.cos(a1) * scale, np.sin(a1) * sign1 * scale], axis=2)
    i = np.arange(P)
    mask = np.where(i[None, :] <= i[:, None], f(0), f(-1e30))
    eye = np.eye(P, dtype=f)
    e = np.arange(E)
    tri = np.broadcast_to((e[None, :] < e[:, None]).astype(f), (P, E, E))
    sel = np.zeros((32, JM * P), np.float16)
    owner = np.minimum(np.arange(JM * P) // I_EXP, E)
    for part in range(2):
        sel[part * GATES + owner, np.arange(JM * P)] = 1
    return [rope0, rope1, mask, eye, tri, sel]


def kernel(**inputs):
    import numpy as np
    import concourse.bacc as bacc
    from concourse.bass_utils import run_bass_kernel_spmd as run

    t = {k: np.asarray(v) for k, v in inputs.items()}
    nc = bacc.Bacc("TRN2", target_bir_lowering=False, num_devices=1)
    names = ["x", "wa", "wb", "wc", "wd", "wg", "rope0", "rope1", "mask", "idf", "tri", "sel"]
    arrays, args = {}, []
    for name, a in zip(names, [t["L0_attn_x"]] + _pack(np, t) + _tables(np)):
        a = np.ascontiguousarray(a)
        arrays[name + "_dram"] = a
        args.append(nc.dram_tensor(name + "_dram", a.shape, mybir.dt.from_np(a.dtype), kind="ExternalInput").ap())
    args.append(nc.dram_tensor("out_dram", (NB, S, D), F32, kind="ExternalOutput").ap())
    macaron(nc, *args)
    return run(nc, [arrays], core_ids=[0]).results[0]["out_dram"]
```

```python
import math
from contextlib import ExitStack

import concourse.bass as bass
from concourse import mybir

P = 128
D = 256
KD = D // P
NB = 4
S = 256
TOK = NB * S
TT = TOK // P
HALF = TOK // 2
TPH = HALF // P
UPH = 2
INTER = 1024
JF = INTER // P
E, I_EXP, I_SH = 8, 176, 704
JM = -(-(E * I_EXP + I_SH) // P)
GATES = E + 1
GLU = 3 * D
H0, KV0 = 16, 4
GRP = H0 // KV0
SC0 = P ** -0.5
NS0 = 2 * H0
RU = KV0 + H0
H1, DH1 = 16, 16
SC1 = DH1 ** -0.5
VC1 = DH1 + 1
NG1 = H1
BLK1 = 3
EPS = 1e-5

SX = 2.0 ** 6
SW = 2.0 ** 10
SH = 2.0 ** 5
SQ = 2.0 ** 4
SP = 2.0 ** 10
SR = 2.0 ** 8

A_N, B_N, C_N, D_N = GLU + D, 4 * D, GLU, D

F32, F16, BF16 = mybir.dt.float32, mybir.dt.float16, mybir.dt.bfloat16
ALU = mybir.AluOpType
ACT = mybir.ActivationFunctionType
AX = mybir.AxisListType
PASSES = ((0, 0), (0, 1), (1, 0))


def macaron(nc, x_in, wa_in, wb_in, wc_in, wd_in, wg_in, rope0_in, rope1_in, mask_in, idf_in,
            tri_in, sel_in, out):
    ds = bass.ds
    ctx = ExitStack()
    with ctx:
        def sb(name, shape, dt):
            return ctx.enter_context(nc.sbuf_tensor(name, shape, dt))

        def sem(name):
            return ctx.enter_context(nc.semaphore(name))

        WA = sb("WA", [P, A_N * (JF + 1)], F32)
        WB = sb("WB", [P, B_N * (JF + 1)], F32)
        WC = sb("WC", [P, C_N * (JM + 1)], F32)
        WD = WB[:, 0:D_N * 9]
        WA16 = WA[:, 0:A_N * JF].bitcast(F16).rearrange("p (c s n) -> p c s n", c=JF, s=2)
        WB16 = WB[:, 0:B_N * JF].bitcast(F16).rearrange("p (h s n) -> p h s n", h=H0, s=2)
        WC16 = WC[:, 0:C_N * JM].bitcast(F16).rearrange("p (c s n) -> p c s n", c=JM, s=2)
        WD16 = WB[:, 0:D_N * 8].bitcast(F16).rearrange("p (c s n) -> p c s n", c=8, s=2)
        WGR = sb("WGR", [P, KD, 16], F32)
        WGS = sb("WGS", [P, 2, KD, 16], F16)

        X = sb("X", [P, TT, D], F32)
        XT = sb("XT", [P, 2, KD, TOK], F16)
        XN = sb("XN", [P, 2, 2, D], F32)
        BST = sb("BST", [P, NB, 2, 6], F32)
        MV = sb("MV", [P, NB, 2, 2], F32)
        RSTD = sb("RSTD", [P, NB, 2, 2], F32)
        NHALF = sb("NHALF", [P, 2], F32)
        T1 = sb("T1", [P, 2, HALF], F32)
        T2 = sb("T2", [P, 2, HALF], F32)
        T3 = sb("T3", [P, HALF], F32)

        NK0 = 2 * KV0 * HALF
        KVR = sb("KVR", [P, NK0 + 2 * TT * KV0 * P], F16)
        KT0 = KVR[:, 0:NK0].rearrange("p (s g t) -> p s g t", s=2, g=KV0)
        V0 = KVR[:, NK0:].rearrange("p (s t n) -> p s t n", s=2, t=TT)
        KZ1 = KVR[:, 0:H1 * HALF].rearrange("p (h t) -> p h t", h=H1)
        QT1 = KVR[:, H1 * HALF:].rearrange("p (h t) -> p h t", t=HALF)

        ARENA = sb("ARENA", [P, 3584], F32)
        PR0 = ARENA[:, 0:1024].rearrange("p (a n) -> p a n", a=2)
        PT0 = ARENA[:, 1024:2048].bitcast(F16).rearrange("p (a s n) -> p a s n", a=2, s=2)
        OT0 = ARENA[:, 2048:2560].bitcast(F16).rearrange("p (a s n) -> p a s n", a=2, s=2)
        QT0 = ARENA[:, 2560:3584].bitcast(F16).rearrange("p (a s n) -> p a s n", a=2, s=2)
        HH = ARENA[:, 0:1024].bitcast(F16).rearrange("p (a s n) -> p a s n", a=2, s=2)
        QK1 = ARENA[:, 0:2048].bitcast(F16).rearrange("p (a h n) -> p a h n", a=2, h=2 * H1)
        PR1 = ARENA[:, 0:1536].rearrange("p (a n) -> p a n", a=2)
        PT1 = ARENA[:, 1536:3072].bitcast(F16).rearrange("p (a s n) -> p a s n", a=2, s=2)
        RC = ARENA[:, 2048:2560].rearrange("p (a t e f) -> p a t e f", a=2, t=TPH, e=E)
        RL = ARENA[:, 2560:2624].rearrange("p (t n) -> p t n", t=TPH)
        RE = ARENA[:, 2624:3136].rearrange("p (a t n) -> p a t n", a=8, t=TPH)
        CMB = sb("CMB", [P, TPH, P], F16)
        CBT = sb("CBT", [P, 2, HALF], F16)
        ST = sb("ST", [P, 2, 4, 2], F32)
        MB1 = sb("MB1", [P, 2, 4], BF16)
        R1 = sb("R1", [P, 2, 4], F32)

        VB1 = WA[:, 0:TT * H1 * VC1].bitcast(F16).rearrange("p (s t h n) -> p s t h n", s=2, t=TT, h=H1)
        O1S = WA[:, 2304:2304 + TT * D].rearrange("p (t n) -> p t n", t=TT)

        ROPE0 = sb("ROPE0", [P, 2, S], F32)
        ROPE1 = sb("ROPE1", [P, 2, 2, DH1], F32)
        MASK = sb("MASK", [P, P], BF16)
        IDH = sb("IDH", [P, P], F16)
        IDB = sb("IDB", [P, P], BF16)
        IDF = sb("IDF", [P, P], F32)
        ZERO = sb("ZERO", [P, P], F16)
        SWT = sb("SWT", [P, 1], F32)
        LNSP = sb("LNSP", [P, 1], F32)
        TRI = sb("TRI", [P, E, E], F32)
        SEL = sb("SEL", [P, JM * P], F16)

        PS = ctx.enter_context(nc.psum_tensor("PS", [P, 8, 512], F32))
        GATE, UP, COMB = (4, 7), 5, 6
        QB, OB = 4, 7

        dma_x = [sem(f"dma_x{i}") for i in range(2)]
        dma_a = [sem(f"dma_a{i}") for i in range(5)]
        dma_b = [sem(f"dma_b{i}") for i in range(1)]
        dma_c = [sem(f"dma_c{i}") for i in range(2)]
        dma_d, dma_out = sem("dma_d"), sem("dma_out")
        dma_id, dma_wg, dma_const, dma_sel = (sem(n) for n in ("dma_id", "dma_wg", "dma_const", "dma_sel"))
        dma_mask, narrowed = sem("dma_mask"), sem("narrowed")
        zeroed = sem("zeroed")
        w_scaled, w_lo_pool = sem("w_scaled"), sem("w_lo_pool")
        w_hi, w_lo, wg_hi, wg_lo = (sem(n) for n in ("w_hi", "w_lo", "wg_hi", "wg_lo"))
        x_sum, bn_half, bn_done = sem("x_sum"), sem("bn_half"), sem("bn_done")
        var_scaled, rstd_done, xn_done = sem("var_scaled"), sem("rstd_done"), sem("xn_done")
        turned, turned_hi, turned_lo = sem("turned"), sem("turned_hi"), sem("turned_lo")
        gate_done, up_done, comb_done = sem("gate_done"), sem("up_done"), sem("comb_done")
        tanh_done, gated, up_mul, comb_mul = sem("tanh_done"), sem("gated"), sem("up_mul"), sem("comb_mul")
        hid_hi, hid_lo, down_done = sem("hid_hi"), sem("hid_lo"), sem("down_done")
        logits, max_route, route, route_act = sem("logits"), sem("max_route"), sem("route"), sem("route_act")
        cmb_turned, cbt_done = sem("cmb_turned"), sem("cbt_done")
        rope_in, rope_swap, rope_cos, rope_sin = (sem(n) for n in ("rope_in", "rope_swap", "rope_cos", "rope_sin"))
        rope_sum, rope_hi, rope_lo = sem("rope_sum"), sem("rope_hi"), sem("rope_lo")
        v_in, v_hi, v_lo = sem("v_in"), sem("v_hi"), sem("v_lo")
        scores, max_done, shift_done = sem("scores"), sem("max_done"), sem("shift_done")
        exp_done, recip_done, norm_done = sem("exp_done"), sem("recip_done"), sem("norm_done")
        pt_done, pt_hi, pt_lo = sem("pt_done"), sem("pt_hi"), sem("pt_lo")
        pv_done, ot_hi, ot_lo, proj_done = sem("pv_done"), sem("ot_hi"), sem("ot_lo"), sem("proj_done")
        kz_zero, ones_set = sem("kz_zero"), sem("ones_set")
        qk1_in, v1_in, v1_hi, v1_lo = sem("qk1_in"), sem("v1_in"), sem("v1_hi"), sem("v1_lo")
        rope1_mul, rope1_sum, qk1_hi, qk1_lo = (sem(n) for n in ("rope1_mul", "rope1_sum", "qk1_hi", "qk1_lo"))
        qk1_turned, q1_copied, k1_copied = sem("qk1_turned"), sem("q1_copied"), sem("k1_copied")
        scores1, max1_done, shift1_done, shifted1 = (sem(n) for n in ("scores1", "max1_done", "shift1_done", "shifted1"))
        exp1_done, pt1_done, pt1_hi, pt1_lo = (sem(n) for n in ("exp1_done", "pt1_done", "pt1_hi", "pt1_lo"))
        pv1_done, recip1_done, o1_done, proj1_done = (sem(n) for n in ("pv1_done", "recip1_done", "o1_done", "proj1_done"))

        block = ctx.enter_context(nc.Block())

        def after(eng, semaphore, count):
            if not isinstance(count, int) or count > 0:
                eng.wait_ge(semaphore, count)

        TILES = [JF, JF, JM, JM]
        STEPS = [0, 2 * JF, 4 * JF, 4 * JF + 2 * JM, 4 * JF + 4 * JM]
        GLU_TURN, GLU_OF = [0, 2, 3, 6], [0, 2, 3, 5]
        Y_SCALE = [0.5 / (SH * SW), 1.0 / (SQ * SW), 0.5 / (SH * SW), 0.5 / (SH * SW), 1.0 / (SQ * SW),
                   0.5 / (SH * SW)]
        TURNS = [(n, h) for n in range(5) for h in range(2)] + [(5, 0), (6, 0), (5, 1), (6, 1)]
        NORMS = [t for t in TURNS if t[0] != 5]
        ROUTED = [(3, 0), (3, 1), (6, 0), (6, 1)]

        def turn_count(n, u):
            return UPH * TURNS.index((n, u // UPH)) + u % UPH

        def norm_count(n, u):
            return UPH * NORMS.index((n, u // UPH)) + u % UPH

        def steps_before(f, hf):
            return STEPS[f] + hf * TILES[f]

        def y_ready(eng, phase, u):
            hf = u // UPH
            if phase in GLU_OF:
                f = GLU_OF.index(phase)
                eng.wait_ge(down_done, steps_before(f, hf) + TILES[f])
            elif phase == 1:
                eng.wait_ge(proj_done, NS0 * hf + NS0 - 1 + u % UPH)
            else:
                eng.wait_ge(proj1_done, u + 1)

        def weights(f):
            return WA16 if f < 2 else WC16

        def y_tiles(u):
            return PS[:, u, :].rearrange("p (t n) -> p t n", t=2)

        def split_a(j):
            return j, WA[:, ds((j + 1) * A_N, A_N)], WA16[:, j, 0, :], WA16[:, j, 1, :], 1

        def split_b(j):
            raw = WB[:, ds((j + 1) * B_N, B_N)].rearrange("p (h n) -> p h n", h=2)
            return JF + j, raw, WB16[:, ds(2 * j, 2), 0, :], WB16[:, ds(2 * j, 2), 1, :], 1

        def split_c(number, c):
            return number, WC[:, ds((c + 1) * C_N, C_N)], WC16[:, c, 0, :], WC16[:, c, 1, :], 1

        def split_d(j):
            return 3 * JF + 2 * j + 1, WD[:, ds((j + 1) * D_N, D_N)], WD16[:, j, 0, :], WD16[:, j, 1, :], 2

        W_ALL = 5 * JF + 1

        def share(x, i):
            if len(x.shape) == 3:
                return x[:, i, :]
            n = x.shape[1] // 2
            return x[:, i * n:(i + 1) * n]

        def wait_split(eng, count):
            eng.wait_ge(w_lo, count)
            eng.wait_ge(w_lo_pool, count)

        def splits(f, hf, j):
            if (f, hf) == (0, 0):
                return [] if isinstance(j, int) and j >= JF - 2 else [split_a(j + 2)]
            if (f, hf) == (0, 1):
                return [split_b(j)]
            if (f, hf) == (1, 0):
                return [split_c(2 * JF + j, j)]
            if (f, hf) == (1, 1):
                return [split_c(3 * JF + 2 * j, JF + j), split_d(j)]
            if (f, hf) == (2, 0) and isinstance(j, int) and j == 0:
                return [split_c(W_ALL - 1, JM - 1)]
            return []

        HOSTED = {(0, 0): (0, 1), (0, 1): (1, 0), (1, 0): (2, 1), (1, 1): (3, 0), (2, 0): (3, 1),
                  (2, 1): (4, 0), (3, 0): (6, 1), (3, 1): None}

        def run_glu(eng, f, hf, step, side):
            first = 5 if HOSTED[f, hf] in ROUTED else 3
            for j in range(first):
                step(f, hf, j, j % 2)
                side(f, hf, j)
            pairs = (TILES[f] - 1) // 2 - ((f, hf) == (0, 0))
            with eng.Fori((first - 1) // 2, pairs) as pair:
                for e in range(2):
                    step(f, hf, 2 * pair + 1 + e, 1 - e)
            for j in range(2 * pairs + 1, TILES[f]):
                step(f, hf, j, j % 2)

        def lagged(i, x, k, n):
            if isinstance(i, int) and not 0 <= 4 * i + x - k < 4 * n:
                return None
            return (i - 1 if x < k else i), (x - k) % 4

        P0, P1 = H0 // 2, H1 // 4
        N_CONST = 3
        ROUTE_STEPS = 14

        def half_of(q, hf):
            return slice(hf * HALF, (hf + 1) * HALF)

        def odd_bank(hf):
            return 2 * (1 - hf)

        def value_bank(hf, i):
            return 2 * hf + i if i < 2 else 4 + i

        @block.sync
        def _(sp):
            x3 = x_in.rearrange("b (t p) d -> p (b t) d", p=P)
            o3 = out.rearrange("b (t p) d -> p (b t) d", p=P)
            sp.dma_start(X[:, 0:TPH, :], x3[:, 0:TPH, :]).then_inc(dma_x[0], 16)
            sp.dma_start(WA[:, A_N:2 * A_N], wa_in[:, 0:A_N]).then_inc(dma_a[0], 16)
            sp.dma_start(WA[:, 2 * A_N:3 * A_N], wa_in[:, A_N:2 * A_N]).then_inc(dma_a[1], 16)
            sp.dma_start(X[:, TPH:, :], x3[:, TPH:, :]).then_inc(dma_x[1], 16)
            sp.dma_start(WA[:, 3 * A_N:4 * A_N], wa_in[:, 2 * A_N:3 * A_N]).then_inc(dma_a[2], 16)
            sp.dma_start(WA[:, 4 * A_N:5 * A_N], wa_in[:, 3 * A_N:4 * A_N]).then_inc(dma_a[3], 16)
            sp.dma_start(WA[:, 5 * A_N:], wa_in[:, 4 * A_N:]).then_inc(dma_a[4], 16)
            sp.dma_start(WB[:, B_N:], wb_in).then_inc(dma_b[0], 16)
            sp.dma_start(WC[:, C_N:9 * C_N], wc_in[:, 0:8 * C_N]).then_inc(dma_c[0], 16)
            sp.dma_start(WC[:, 9 * C_N:], wc_in[:, 8 * C_N:]).then_inc(dma_c[1], 16)
            sp.wait_ge(proj_done, 2 * NS0)
            sp.dma_start(WD[:, D_N:], wd_in).then_inc(dma_d, 16)
            for u in range(NB):
                sp.wait_ge(x_sum, 5 * NB + u + 1)
                sp.dma_start(o3[:, 2 * u:2 * u + 2, :], X[:, 2 * u:2 * u + 2, :]).then_inc(dma_out, 16)
            sp.wait_ge(dma_out, 16 * NB)

        @block.gpsimd
        def _(pool):
            pl = nc.gpsimd
            pl.memset(ZERO[:, :], 0.0).then_inc(zeroed, 1)
            pl.memset(NHALF[:, :], -0.5).then_inc(zeroed, 1)
            pl.memset(LNSP[:, :], math.log(SP)).then_inc(zeroed, 1)
            pl.memset(SEL[:, :], 0.0).then_inc(zeroed, 1)
            pl.memset(CMB[:, :, :], 0.0).then_inc(zeroed, 1)
            pl.memset(SWT[:, :], SW).then_inc(zeroed, 1)
            pool.wait_ge(zeroed, 6)
            pl.dma_start(SEL[0:32, :], sel_in).then_inc(dma_sel, 16)

            def turn(n, hf):
                for u in range(UPH * hf, UPH * hf + UPH):
                    c = norm_count(n, u)
                    pool.wait_ge(bn_done, 2 * c + 2)
                    pl.tensor_scalar(RSTD[:, u, 0, :], MV[:, u, :, 1], SX ** -2, EPS * SX ** -2,
                                     ALU.mult, ALU.add).then_inc(var_scaled, 1)
                    pool.wait_ge(var_scaled, c + 1)
                    pl.tensor_tensor(RSTD[:, u, 1, :], RSTD[:, u, 0, :], NHALF[:, :],
                                     ALU.pow).then_inc(rstd_done, 1)

            def split(c, raw, hi, lo, back):
                r = share(raw, 1)
                pool.wait_ge(w_hi, c + 1)
                pl.tensor_tensor(r, r, SWT[:, :].broadcast_to(list(r.shape)), ALU.mult).then_inc(w_scaled, 1)
                pool.wait_ge(w_scaled, c + 1)
                pl.tensor_tensor(share(lo, 1), r, share(hi, 1), ALU.subtract).then_inc(w_lo_pool, 1)

            def glu_step(f, hf, j, a):
                for x in splits(f, hf, j):
                    split(*x)

            def glu_side(f, hf, j):
                if j == 0:
                    turn(*HOSTED[f, hf])

            def rope_sine(r, a):
                pool.wait_ge(rope_swap, 2 * r + 2)
                t2 = T2[:, a, :].rearrange("p (b t) -> p b t", b=2)
                pl.tensor_tensor(t2, t2, ROPE0[:, 1:2, :].broadcast_to([P, 2, S]), ALU.mult).then_inc(rope_sin, 1)

            def rope_add(r, a):
                pool.wait_ge(rope_cos, r + 1)
                pool.wait_ge(rope_sin, r + 1)
                after(pool, rope_lo, r)
                pl.tensor_tensor(T3[:, :], T1[:, a, :], T2[:, a, :], ALU.add).then_inc(rope_sum, 1)

            def step0(hf, p, x):
                st, r = NS0 * hf + 4 * p + x, RU * hf + KV0 + 2 * p
                more, before = not (isinstance(p, int) and p == P0 - 1), not (isinstance(p, int) and p == 0)
                if x == 0 and before:
                    rope_add(r + 1, 1)
                if x == 2 and more:
                    rope_add(r + 2, 0)
                pool.wait_ge(recip_done, st + 1)
                pr = PR0[:, x % 2, :].rearrange("p (q k) -> p q k", q=2)
                rs = ST[:, x % 2, 3, :].rearrange("p (q k) -> p q k", k=1)
                pl.tensor_tensor(pr, pr, rs.broadcast_to([P, 2, S]), ALU.mult).then_inc(norm_done, 1)
                if x % 2 and more:
                    rope_sine(r + 2 + x // 2, x // 2)

            def attention0(hf, n, th):
                for i in range(KV0 + 2):
                    if i == KV0:
                        rope_add(RU * hf + i - 1, 1)
                    rope_sine(RU * hf + i, i % 2)
                    if i not in (0, KV0):
                        rope_add(RU * hf + i - 1, 1 - i % 2)
                    if i == (3 if hf else 2):
                        turn(n, th)
                rope_add(RU * hf + KV0 + 1, 1)
                for x in range(4):
                    step0(hf, 0, x)
                with pool.Fori(1, P0 - 1) as p:
                    for x in range(4):
                        step0(hf, p, x)
                for x in range(4):
                    step0(hf, P0 - 1, x)

            def attention1(hf, n, th):
                for i in range(TPH):
                    t, a = TPH * hf + i, i % 2
                    pool.wait_ge(rope1_mul, 3 * t + 3)
                    after(pool, qk1_hi, 2 * t)
                    after(pool, qk1_lo, 2 * t)
                    pl.tensor_tensor(T3[:, :], T1[:, a, :], T2[:, a, :], ALU.add).then_inc(rope1_sum, 1)
                    t4 = T3[:, :].rearrange("p (h o n) -> p h o n", o=1, n=DH1)
                    pool.wait_ge(qk1_hi, 2 * t + 2)
                    q4 = QK1[:, a, 0:H1, :].rearrange("p h (c s n) -> p h c s n", c=2, s=2)
                    k4 = QK1[:, a, H1:, :].rearrange("p h (s c n) -> p h s c n", c=2, s=2)
                    pl.tensor_tensor(q4[:, :, :, 1, :], t4[:, 0:H1].broadcast_to([P, H1, 2, DH1]),
                                     q4[:, :, :, 0, :], ALU.subtract).then_inc(qk1_lo, 1)
                    pl.tensor_tensor(k4[:, :, 1, :, :], t4[:, H1:].broadcast_to([P, H1, 2, DH1]),
                                     k4[:, :, 0, :, :], ALU.subtract).then_inc(qk1_lo, 1)
                    if i == 1:
                        turn(n, th)

            turn(0, 0)
            split(*split_a(0))
            split(*split_a(1))
            run_glu(pool, 0, 0, glu_step, glu_side)
            run_glu(pool, 0, 1, glu_step, glu_side)
            pool.wait_ge(dma_const, 16 * N_CONST)
            attention0(0, 1, 1)
            attention0(1, 2, 0)
            run_glu(pool, 1, 0, glu_step, glu_side)
            run_glu(pool, 1, 1, glu_step, glu_side)
            run_glu(pool, 2, 0, glu_step, lambda f, hf, j: None)
            pool.wait_ge(proj_done, 2 * NS0)
            pool.wait_ge(w_lo_pool, W_ALL)
            k6 = KZ1.rearrange("p (h e) t -> p h e t", e=2)
            pl.memset(k6[P // 2:, :, 0, :], 0.0).then_inc(kz_zero, 1)
            pool.wait_ge(kz_zero, 1)
            pl.memset(k6[0:P // 2, :, 1, :], 0.0).then_inc(kz_zero, 1)
            pool.wait_ge(kz_zero, 2)
            pool.wait_ge(down_done, STEPS[2])
            pl.memset(VB1[:, 0, :, :, DH1:], 1.0).then_inc(ones_set, 1)
            pool.wait_ge(ones_set, 1)
            pl.memset(VB1[:, 1, :, :, DH1:], 0.0).then_inc(ones_set, 1)
            pool.wait_ge(ones_set, 2)
            turn(3, 1)
            turn(4, 0)
            attention1(0, 4, 1)
            attention1(1, 6, 0)
            turn(6, 1)

        @block.scalar
        def _(act):
            sc = nc.scalar
            act.dma_start(IDF[:, :], idf_in).then_inc(dma_id, 16)
            act.dma_start(WGR[:, :, :], wg_in).then_inc(dma_wg, 16)
            act.dma_start(T3[:, 0:P], mask_in).then_inc(dma_mask, 16)
            for dst, src in ((ROPE0, rope0_in), (ROPE1, rope1_in), (TRI, tri_in)):
                act.dma_start(dst.ap(), src).then_inc(dma_const, 16)

            def split(c, raw, hi, lo, back):
                after(act, w_lo, c - back + 1)
                after(act, w_lo_pool, c - back + 1)
                sc.activation(hi, raw, ACT.Copy, scale=SW).then_inc(w_hi, 1)

            def turn_high(n, hf):
                for u in range(UPH * hf, UPH * hf + UPH):
                    act.wait_ge(turned, turn_count(n, u) + 1)
                    sc.activation(XT[:, 0, :, u * S:(u + 1) * S],
                                  PS[:, u, :].rearrange("p (k t) -> p k t", k=KD), ACT.Copy).then_inc(turned_hi, 1)

            def routing(n, hf):
                m = ROUTED.index((n, hf))
                act.wait_ge(route, ROUTE_STEPS * m + 2)
                sc.activation(RE[:, 1, :, 0:E], RE[:, 0, :, 0:E], ACT.Exp).then_inc(route_act, 1)
                sc.activation(RE[:, 1, :, E:GATES], RL[:, :, E:GATES], ACT.Tanh, scale=0.5).then_inc(route_act, 1)

            def glu_step(f, hf, j, a):
                st = steps_before(f, hf) + j
                if (f, hf) == (0, 0) and isinstance(j, int) and j < 3:
                    act.wait_ge(dma_a[j + 2], 16)
                act.wait_ge(gate_done, st + 1)
                after(act, gated, st)
                sc.activation(T1[:, 0, :], PS[:, GATE[a], :], ACT.Tanh, scale=0.5 / (SX * SW)).then_inc(tanh_done, 1)
                for x in splits(f, hf, j):
                    split(*x)
                if f < 2:
                    act.wait_ge(up_mul, st + 1)
                else:
                    act.wait_ge(comb_mul, st - STEPS[2] + 1)
                after(act, down_done, st if isinstance(j, int) and j == 0 else st - 1)
                sc.activation(HH[:, a, 0, :], T3[:, :], ACT.Copy).then_inc(hid_hi, 1)

            def glu_side(f, hf, j):
                t = HOSTED[f, hf]
                if t and j == 2:
                    turn_high(*t)
                if t in ROUTED and j == 3:
                    routing(*t)

            def rope_swapped(r, bank, a):
                act.wait_ge(rope_in, r + 1)
                after(act, rope_sum, r - 1)
                lo, hi = slice(0, P // 2), slice(P // 2, P)
                sc.activation(T2[lo, a, :], PS[hi, bank, :], ACT.Copy).then_inc(rope_swap, 1)
                sc.activation(T2[hi, a, :], PS[lo, bank, :], ACT.Copy).then_inc(rope_swap, 1)

            def rope_high(r, hi):
                act.wait_ge(rope_sum, r + 1)
                sc.activation(hi, T3[:, :], ACT.Copy).then_inc(rope_hi, 1)

            def step0(hf, p, x):
                st, r = NS0 * hf + 4 * p + x, RU * hf + KV0 + 2 * p
                more, before = not (isinstance(p, int) and p >= P0 - 1), not (isinstance(p, int) and p in (0, P0))
                if lagged(p, x, 2, P0):
                    act.wait_ge(pt_done, st - 1)
                    after(act, pv_done, st - 3)
                    bank = odd_bank(hf) + 1 if x % 2 else 6
                    sc.activation(PT0[:, x % 2, 0, :], PS[:, bank, :], ACT.Copy, scale=SP).then_inc(pt_hi, 1)
                if lagged(p, x, 0, P0):
                    act.wait_ge(shift_done, st + 1)
                    bank = odd_bank(hf) if x % 2 else 5
                    for qt in range(2):
                        sc.activation(PR0[:, x % 2, qt * S:(qt + 1) * S], PS[:, bank, qt * S:(qt + 1) * S],
                                      ACT.Exp, bias=ST[:, x % 2, 1, qt:qt + 1], scale=SC0 / SQ ** 2,
                                      accum_out=ST[:, x % 2, 2, qt:qt + 1]).then_inc(exp_done, 1)
                if lagged(p, x, 3, P0):
                    act.wait_ge(pv_done, st - 2)
                    sc.activation(OT0[:, 1 - x % 2, 0, :], PS[:, OB, 0:S], ACT.Copy, scale=1 / SP).then_inc(ot_hi, 1)
                if x % 2 and more:
                    rope_swapped(r + 2 + x // 2, QB, x // 2)
                if x == 0 and before:
                    act.wait_ge(scores, st)
                    rope_high(r + 1, QT0[:, 1, 0, :])
                if x == 2 and more:
                    act.wait_ge(scores, st)
                    rope_high(r + 2, QT0[:, 0, 0, :])

            def attention0(hf, n, th):
                r = RU * hf
                def value_high(i):
                    t = TPH * hf + i
                    act.wait_ge(v_in, t + 1)
                    sc.activation(V0[:, 0, t, :], PS[:, value_bank(hf, i), :], ACT.Copy,
                                  scale=SQ / (SX * SW)).then_inc(v_hi, 1)

                for i in range(KV0):
                    rope_swapped(r + i, QB + i % 2, i % 2)
                    if i:
                        rope_high(r + i - 1, KT0[:, 0, i - 1, :])
                    if hf and i < 3:
                        step0(0, P0, i)
                    if not hf and i >= 2:
                        value_high(i - 2)
                if hf:
                    value_high(0)
                    value_high(1)
                rope_high(r + KV0 - 1, KT0[:, 0, KV0 - 1, :])
                value_high(2)
                rope_swapped(r + KV0, QB, 0)
                value_high(3)
                if hf:
                    rope_swapped(r + KV0 + 1, QB + 1, 1)
                turn_high(n, th)
                if not hf:
                    rope_swapped(r + KV0 + 1, QB + 1, 1)
                for i in range(2):
                    rope_high(r + KV0 + i, QT0[:, i, 0, :])
                for x in range(4):
                    step0(hf, 0, x)
                with act.Fori(1, P0 - 1) as p:
                    for x in range(4):
                        step0(hf, p, x)
                for x in range(4):
                    step0(hf, P0 - 1, x)

            def copies1(hf, i):
                t = TPH * hf + i
                act.wait_ge(qk1_turned, t + 1)
                q = PS[:, 6, :].bitcast(F16).rearrange("p (h t) -> p h t", t=P)
                k = PS[P // 2:, 7, :].bitcast(F16).rearrange("p (h t) -> p h t", t=P)
                after(act, pv1_done, NG1 * hf)
                sc.activation(QT1[:, :, i * P:(i + 1) * P], q, ACT.Copy).then_inc(q1_copied, 1)
                act.wait_ge(kz_zero, 2)
                act.wait_ge(k1_copied, t + 1)
                sc.activation(KZ1.rearrange("p (h e) t -> p h e t", e=2)[P // 2:, :, 1, i * P:(i + 1) * P], k,
                              ACT.Copy).then_inc(q1_copied, 1)

            def step1(hf, p, q):
                g = NG1 * hf + 4 * p + q
                if lagged(p, q, 2, P1):
                    act.wait_ge(pt1_done, g - 1)
                    after(act, pv1_done, g - 3)
                    sc.activation(PT1[:, q % 2, 0, :], PS[:, 6:8, :].rearrange("p a n -> p (a n)")[:, 0:768],
                                  ACT.Copy).then_inc(pt1_hi, 1)
                if lagged(p, q, 0, P1):
                    act.wait_ge(shifted1, g + 1)
                    bank = 4 if q % 2 else 2 * hf
                    sc.activation(PR1[:, q % 2, :].rearrange("p (b n) -> p b n", b=2),
                                  PS[:, bank:bank + 2, 0:384], ACT.Exp, bias=LNSP[:, :],
                                  scale=SC1 / SQ ** 2).then_inc(exp1_done, 1)

            def attention1(hf, n, th):
                for i in range(TPH):
                    t, a = TPH * hf + i, i % 2
                    act.wait_ge(v1_in, t + 1)
                    sc.activation(VB1[:, 0, t, :, 0:DH1], PS[:, 4 + a, 0:D].rearrange("p (h n) -> p h n", n=DH1),
                                  ACT.Copy, scale=SQ / (SX * SW)).then_inc(v1_hi, 1)
                    act.wait_ge(rope1_sum, t + 1)
                    if i >= 2:
                        act.wait_ge(qk1_turned, t - 1)
                    t4 = T3[:, :].rearrange("p (h o n) -> p h o n", o=1, n=DH1)
                    q4 = QK1[:, a, 0:H1, :].rearrange("p h (c s n) -> p h c s n", c=2, s=2)
                    k4 = QK1[:, a, H1:, :].rearrange("p h (s c n) -> p h s c n", c=2, s=2)
                    sc.activation(q4[:, :, :, 0, :], t4[:, 0:H1].broadcast_to([P, H1, 2, DH1]),
                                  ACT.Copy).then_inc(qk1_hi, 1)
                    sc.activation(k4[:, :, 0, :, :], t4[:, H1:].broadcast_to([P, H1, 2, DH1]),
                                  ACT.Copy).then_inc(qk1_hi, 1)
                    if i:
                        copies1(hf, i - 1)
                copies1(hf, TPH - 1)
                turn_high(n, th)
                if (n, th) in ROUTED:
                    routing(n, th)
                for q in range(4):
                    step1(hf, 0, q)
                with act.Fori(1, P1) as p:
                    for q in range(4):
                        step1(hf, p, q)
                step1(hf, P1, 0)
                step1(hf, P1, 1)
                turn_high(5, hf)

            act.wait_ge(dma_a[0], 16)
            split(*split_a(0))
            turn_high(0, 0)
            act.wait_ge(dma_wg, 16)
            sc.activation(WGS[:, 0, :, :], WGR[:, :, :], ACT.Copy, scale=SW).then_inc(wg_hi, 1)
            act.wait_ge(dma_a[1], 16)
            split(*split_a(1))
            run_glu(act, 0, 0, glu_step, glu_side)
            act.wait_ge(dma_b[0], 16)
            run_glu(act, 0, 1, glu_step, glu_side)
            act.wait_ge(zeroed, 6)
            attention0(0, 1, 1)
            attention0(1, 2, 0)
            for x in range(3):
                step0(1, P0, x)
            act.wait_ge(dma_c[0], 16)
            run_glu(act, 1, 0, glu_step, glu_side)
            act.wait_ge(dma_c[1], 16)
            act.wait_ge(dma_d, 16)
            run_glu(act, 1, 1, glu_step, glu_side)
            run_glu(act, 2, 0, glu_step, glu_side)
            run_glu(act, 2, 1, glu_step, glu_side)
            attention1(0, 4, 1)
            attention1(1, 6, 0)
            run_glu(act, 3, 0, glu_step, glu_side)
            run_glu(act, 3, 1, glu_step, glu_side)

        @block.vector
        def _(dve):
            v = nc.vector

            def split(c, raw, hi, lo, back):
                dve.wait_ge(w_hi, c + 1)
                v.scalar_tensor_tensor(share(lo, 0), share(raw, 0), SW, share(hi, 0), ALU.mult,
                                       ALU.subtract).then_inc(w_lo, 1)

            def add_phase(phase, u):
                y_ready(dve, phase, u)
                v.scalar_tensor_tensor(X[:, 2 * u:2 * u + 2, :], y_tiles(u), Y_SCALE[phase],
                                       X[:, 2 * u:2 * u + 2, :], ALU.mult, ALU.add).then_inc(x_sum, 1)

            def turn_stats(n, hf, units=range(UPH)):
                phase = n - 1 if n < 5 else 4
                for u in (UPH * hf + i for i in units):
                    c = norm_count(n, u)
                    if n:
                        add_phase(phase, u)
                        dve.wait_ge(x_sum, phase * NB + u + 1)
                    else:
                        dve.wait_ge(dma_x[hf], 16)
                    for t in range(2):
                        v.bn_stats(BST[:, u, t, :], X[:, 2 * u + t, :]).then_inc(bn_half, 1)
                    dve.wait_ge(bn_half, 2 * c + 2)
                    for t in range(2):
                        v.bn_aggr(MV[:, u, t, :], BST[:, u, t, :]).then_inc(bn_done, 1)

            def turn_norm(n, hf):
                for u in range(UPH * hf, UPH * hf + UPH):
                    dve.wait_ge(rstd_done, norm_count(n, u) + 1)
                    for t in range(2):
                        v.tensor_scalar(XN[:, u % 2, t, :], X[:, 2 * u + t, :], MV[:, u, t, 0:1],
                                        RSTD[:, u, 1, t:t + 1], ALU.subtract, ALU.mult).then_inc(xn_done, 1)

            def turn_low(n, hf):
                for u in range(UPH * hf, UPH * hf + UPH):
                    dve.wait_ge(turned_hi, turn_count(n, u) + 1)
                    v.tensor_tensor(XT[:, 1, :, u * S:(u + 1) * S], PS[:, u, :].rearrange("p (k t) -> p k t", k=KD),
                                    XT[:, 0, :, u * S:(u + 1) * S], ALU.subtract).then_inc(turned_lo, 1)

            made = [0]

            def link(ins):
                made[0] += 1
                ins.then_inc(route, 1)
                dve.wait_ge(route, made[0])

            def per_expert(x):
                return x.broadcast_to([P, TPH, E])

            def routing_ranks(n, hf):
                l, m = RL[:, :, 0:E], RE[:, 2, :, 0:1]
                dve.wait_ge(logits, ROUTED.index((n, hf)) + 1)
                link(v.tensor_scalar(RL[:, :, 0:GATES], PS[:, 2 * hf, 0:TPH * 16].rearrange("p (t n) -> p t n", t=TPH)
                                     [:, :, 0:GATES], 1 / (SX * SW), None, ALU.mult))
                v.tensor_reduce(m, l, AX.X, ALU.max).then_inc(max_route, 1)
                dve.wait_ge(max_route, ROUTED.index((n, hf)) + 1)
                link(v.tensor_tensor(RE[:, 0, :, 0:E], l, per_expert(m), ALU.subtract))
                lf = l.rearrange("p t (o e) -> p t o e", o=1).broadcast_to([P, TPH, E, E])
                le = l.rearrange("p t (e o) -> p t e o", o=1).broadcast_to([P, TPH, E, E])
                link(v.tensor_tensor(RC[:, 0], lf, le, ALU.is_equal))
                link(v.tensor_tensor(RC[:, 0], RC[:, 0], TRI[:, :, :].rearrange("p (o e) f -> p o e f", o=1)
                                     .broadcast_to([P, TPH, E, E]), ALU.mult))
                link(v.tensor_tensor(RC[:, 1], lf, le, ALU.is_gt))
                link(v.tensor_tensor(RC[:, 0], RC[:, 0], RC[:, 1], ALU.add))
                link(v.tensor_reduce(RE[:, 3, :, 0:E], RC[:, 0], AX.X, ALU.add))

            def routing_weights(n, hf):
                dve.wait_ge(route_act, 2 * ROUTED.index((n, hf)) + 2)
                link(v.scalar_tensor_tensor(RE[:, 4, :, 0:E], RE[:, 3, :, 0:E], 2.0, RE[:, 1, :, 0:E], ALU.is_lt,
                                            ALU.mult))
                link(v.tensor_reduce(RE[:, 5, :, 0:1], RE[:, 4, :, 0:E], AX.X, ALU.add))
                link(v.reciprocal(RE[:, 6, :, 0:1], RE[:, 5, :, 0:1]))
                link(v.scalar_tensor_tensor(RE[:, 7, :, 0:E], RE[:, 4, :, 0:E], SR, per_expert(RE[:, 6, :, 0:1]),
                                            ALU.mult, ALU.mult))
                link(v.tensor_scalar(RE[:, 7, :, E:GATES], RE[:, 1, :, E:GATES], 0.5 * SR, 0.5 * SR, ALU.mult,
                                     ALU.add))
                link(v.tensor_copy(CMB[:, :, 0:GATES], RE[:, 7, :, 0:GATES]))
                link(v.tensor_tensor(CMB[:, :, GATES:2 * GATES], RE[:, 7, :, 0:GATES], CMB[:, :, 0:GATES],
                                     ALU.subtract))
                assert made[0] % ROUTE_STEPS == 0, made

            def routing_turned(n, hf):
                dve.wait_ge(cmb_turned, ROUTED.index((n, hf)) + 1)
                v.tensor_copy(CBT[:, hf, :], PS[:, 2 * hf + 1, 0:HALF // 2].bitcast(F16)).then_inc(cbt_done, 1)

            def glu_step(f, hf, j, a):
                st = steps_before(f, hf) + j
                dve.wait_ge(tanh_done, st + 1)
                after(dve, up_mul, st)
                v.scalar_tensor_tensor(T2[:, 0, :], T1[:, 0, :], 1.0, PS[:, GATE[a], :], ALU.add,
                                       ALU.mult).then_inc(gated, 1)
                dve.wait_ge(up_done, st + 1)
                dve.wait_ge(gated, st + 1)
                after(dve, hid_lo, st)
                scale = 0.5 * SH / (SX * SW) ** 2 / (1 if f < 2 else SR)
                v.scalar_tensor_tensor(T3[:, :], T2[:, 0, :], scale, PS[:, UP, :], ALU.mult,
                                       ALU.mult).then_inc(up_mul, 1)
                if f >= 2:
                    dve.wait_ge(comb_done, st - STEPS[2] + 1)
                    dve.wait_ge(up_mul, st + 1)
                    v.tensor_tensor(T3[:, :], T3[:, :], PS[:, COMB, :], ALU.mult).then_inc(comb_mul, 1)
                for x in splits(f, hf, j):
                    split(*x)
                dve.wait_ge(hid_hi, st + 1)
                v.tensor_tensor(HH[:, a, 1, :], T3[:, :], HH[:, a, 0, :], ALU.subtract).then_inc(hid_lo, 1)

            def glu_side(f, hf, j):
                t = HOSTED[f, hf]
                if t is None:
                    if j == 1:
                        add_phase(5, 0)
                        add_phase(5, 1)
                    return
                if j < 3:
                    (turn_stats, turn_norm, turn_low)[j](*t)
                if t in ROUTED and j >= 3:
                    (routing_ranks, routing_weights)[j - 3](*t)

            def glu(f, hf):
                run_glu(dve, f, hf, glu_step, glu_side)
                if HOSTED[f, hf] in ROUTED:
                    routing_turned(*HOSTED[f, hf])

            def rope_cosine(r, bank, a):
                dve.wait_ge(rope_swap, 2 * r + 2)
                after(dve, rope_sum, r - 1)
                v.tensor_tensor(T1[:, a, :].rearrange("p (b t) -> p b t", b=2),
                                PS[:, bank, :].rearrange("p (b t) -> p b t", b=2),
                                ROPE0[:, 0:1, :].broadcast_to([P, 2, S]), ALU.mult).then_inc(rope_cos, 1)

            def rope_low(r, lo, hi):
                dve.wait_ge(rope_hi, r + 1)
                v.tensor_tensor(lo, T3[:, :], hi, ALU.subtract).then_inc(rope_lo, 1)

            def step0(hf, p, x):
                st, r = NS0 * hf + 4 * p + x, RU * hf + KV0 + 2 * p
                more, before = not (isinstance(p, int) and p >= P0 - 1), not (isinstance(p, int) and p in (0, P0))
                if lagged(p, x, 0, P0):
                    dve.wait_ge(scores, st + 1)
                    bank = odd_bank(hf) if x % 2 else 5
                    v.tensor_reduce(ST[:, x % 2, 0, :], PS[:, bank, :].rearrange("p (q k) -> p q k", q=2),
                                    AX.X, ALU.max).then_inc(max_done, 1)
                    dve.wait_ge(max_done, st + 1)
                    v.tensor_scalar(ST[:, x % 2, 1, :], ST[:, x % 2, 0, :], -SC0 / SQ ** 2, None,
                                    ALU.mult).then_inc(shift_done, 1)
                if x == 0 and before:
                    rope_cosine(r + 1, QB, 1)
                if x == 2 and more:
                    rope_cosine(r + 2, QB, 0)
                if x == 1 and before:
                    rope_low(r + 1, QT0[:, 1, 1, :], QT0[:, 1, 0, :])
                if x == 3 and more:
                    rope_low(r + 2, QT0[:, 0, 1, :], QT0[:, 0, 0, :])
                if lagged(p, x, 2, P0):
                    dve.wait_ge(pt_hi, st - 1)
                    bank = odd_bank(hf) + 1 if x % 2 else 6
                    v.scalar_tensor_tensor(PT0[:, x % 2, 1, :], PS[:, bank, :], SP, PT0[:, x % 2, 0, :], ALU.mult,
                                           ALU.subtract).then_inc(pt_lo, 1)
                if lagged(p, x, 0, P0):
                    dve.wait_ge(exp_done, 2 * st + 2)
                    v.reciprocal(ST[:, x % 2, 3, :], ST[:, x % 2, 2, :]).then_inc(recip_done, 1)
                if lagged(p, x, 3, P0):
                    dve.wait_ge(ot_hi, st - 2)
                    v.scalar_tensor_tensor(OT0[:, 1 - x % 2, 1, :], PS[:, OB, 0:S], 1 / SP, OT0[:, 1 - x % 2, 0, :],
                                           ALU.mult, ALU.subtract).then_inc(ot_lo, 1)

            def attention0(hf, n, th):
                r = RU * hf
                def value_low(i):
                    t = TPH * hf + i
                    dve.wait_ge(v_hi, t + 1)
                    v.scalar_tensor_tensor(V0[:, 1, t, :], PS[:, value_bank(hf, i), :], SQ / (SX * SW),
                                           V0[:, 0, t, :], ALU.mult, ALU.subtract).then_inc(v_lo, 1)

                for i in range(KV0):
                    rope_cosine(r + i, QB + i % 2, i % 2)
                    if i:
                        rope_low(r + i - 1, KT0[:, 1, i - 1, :], KT0[:, 0, i - 1, :])
                    if hf and i < 3:
                        step0(0, P0, i)
                    if not hf:
                        turn_stats(n, th, (i,)) if i < 2 else value_low(i - 2)
                if hf:
                    turn_stats(n, th)
                    value_low(0)
                    value_low(1)
                turn_norm(n, th)
                rope_low(r + KV0 - 1, KT0[:, 1, KV0 - 1, :], KT0[:, 0, KV0 - 1, :])
                value_low(2)
                rope_cosine(r + KV0, QB, 0)
                value_low(3)
                if hf:
                    rope_cosine(r + KV0 + 1, QB + 1, 1)
                turn_low(n, th)
                if not hf:
                    rope_cosine(r + KV0 + 1, QB + 1, 1)
                for i in range(2):
                    rope_low(r + KV0 + i, QT0[:, i, 1, :], QT0[:, i, 0, :])
                for x in range(4):
                    step0(hf, 0, x)
                with dve.Fori(1, P0 - 1) as p:
                    for x in range(4):
                        step0(hf, p, x)
                for x in range(4):
                    step0(hf, P0 - 1, x)

            def copies1(hf, i):
                t = TPH * hf + i
                dve.wait_ge(qk1_turned, t + 1)
                dve.wait_ge(kz_zero, 2)
                after(dve, pv1_done, NG1 * hf)
                k = PS[0:P // 2, 7, :].bitcast(F16).rearrange("p (h t) -> p h t", t=P)
                v.tensor_copy(KZ1.rearrange("p (h e) t -> p h e t", e=2)[0:P // 2, :, 0, i * P:(i + 1) * P],
                              k).then_inc(k1_copied, 1)

            def step1(hf, p, q):
                g = NG1 * hf + 4 * p + q
                a = q % 2
                if lagged(p, q, 0, P1):
                    dve.wait_ge(scores1, g + 1)
                    bank = 4 if a else 2 * hf
                    for qt, cols in ((0, slice(0, P)), (1, slice(P, 3 * P))):
                        v.tensor_reduce(ST[:, a, qt, :], PS[:, bank:bank + 2, cols], AX.X,
                                        ALU.max).then_inc(max1_done, 1)
                    dve.wait_ge(max1_done, 2 * g + 2)
                    v.tensor_scalar(MB1[:, a, :], ST[:, a, 0:2, :].rearrange("p q b -> p (q b)"), -1.0, None,
                                    ALU.mult).then_inc(shift1_done, 1)
                if lagged(p, q, 2, P1):
                    dve.wait_ge(pt1_hi, g - 1)
                    v.tensor_tensor(PT1[:, a, 1, :], PS[:, 6:8, :].rearrange("p a n -> p (a n)")[:, 0:768],
                                    PT1[:, a, 0, :], ALU.subtract).then_inc(pt1_lo, 1)
                if item := lagged(p, q, 3, P1):
                    a = 1 - a
                    o = PS[:, odd_bank(hf) + a, 0:128].rearrange("p (t n) -> p t n", t=4)
                    dve.wait_ge(pv1_done, g - 2)
                    v.reciprocal(R1[:, a, :].rearrange("p (t n) -> p t n", n=1), o[:, :, DH1:VC1]).then_inc(recip1_done, 1)
                    dve.wait_ge(recip1_done, g - 2)
                    v.tensor_tensor(O1S[:, TPH * hf:TPH * hf + 4, ds((4 * item[0] + item[1]) * DH1, DH1)], o[:, :, 0:DH1],
                                    R1[:, a, :].rearrange("p (t n) -> p t n", n=1).broadcast_to([P, 4, DH1]),
                                    ALU.mult).then_inc(o1_done, 1)

            def attention1(hf, n, th):
                for i in range(TPH):
                    t, a = TPH * hf + i, i % 2
                    dve.wait_ge(qk1_in, t + 1)
                    after(dve, rope1_sum, t - 1)
                    ps = PS[:, 2 * hf + a, :]
                    p2, t2 = (x.rearrange("p (h n e) -> p h n e", n=DH1 // 2, e=2) for x in (ps, T2[:, a, :]))
                    sn = ROPE1[:, a:a + 1, 1, :].rearrange("p o (n e) -> p o n e", e=2)
                    v.tensor_tensor(T1[:, a, :].rearrange("p (h n) -> p h n", n=DH1),
                                    ps.rearrange("p (h n) -> p h n", n=DH1),
                                    ROPE1[:, a:a + 1, 0, :].broadcast_to([P, 2 * H1, DH1]),
                                    ALU.mult).then_inc(rope1_mul, 1)
                    for e in range(2):
                        v.tensor_tensor(t2[:, :, :, e], p2[:, :, :, 1 - e],
                                        sn[:, :, :, e].broadcast_to([P, 2 * H1, DH1 // 2]),
                                        ALU.mult).then_inc(rope1_mul, 1)
                    dve.wait_ge(v1_hi, t + 1)
                    v.scalar_tensor_tensor(VB1[:, 1, t, :, 0:DH1], PS[:, 4 + a, 0:D].rearrange("p (h n) -> p h n", n=DH1),
                                           SQ / (SX * SW), VB1[:, 0, t, :, 0:DH1], ALU.mult,
                                           ALU.subtract).then_inc(v1_lo, 1)
                    if i:
                        copies1(hf, i - 1)
                    if i == 0:
                        turn_stats(n, th)
                    if i == 2:
                        turn_norm(n, th)
                copies1(hf, TPH - 1)
                turn_low(n, th)
                if (n, th) in ROUTED:
                    routing_ranks(n, th)
                    routing_weights(n, th)
                    routing_turned(n, th)
                for q in range(4):
                    step1(hf, 0, q)
                with dve.Fori(1, P1) as p:
                    for q in range(4):
                        step1(hf, p, q)
                for q in range(3):
                    step1(hf, P1, q)
                turn_low(5, hf)

            dve.wait_ge(dma_id, 16)
            v.tensor_copy(IDH[:, :], IDF[:, :]).then_inc(narrowed, 1)
            v.tensor_copy(IDB[:, :], IDF[:, :]).then_inc(narrowed, 1)
            turn_stats(0, 0)
            split(*split_a(0))
            turn_norm(0, 0)
            dve.wait_ge(dma_mask, 16)
            v.tensor_copy(MASK[:, :], T3[:, 0:P]).then_inc(narrowed, 1)
            turn_low(0, 0)
            dve.wait_ge(narrowed, 3)
            dve.wait_ge(wg_hi, 1)
            v.scalar_tensor_tensor(WGS[:, 1, :, :], WGR[:, :, :], SW, WGS[:, 0, :, :], ALU.mult,
                                   ALU.subtract).then_inc(wg_lo, 1)
            split(*split_a(1))
            glu(0, 0)
            glu(0, 1)
            dve.wait_ge(dma_const, 16 * N_CONST)
            attention0(0, 1, 1)
            attention0(1, 2, 0)
            for x in range(3):
                step0(1, P0, x)
            glu(1, 0)
            glu(1, 1)
            glu(2, 0)
            glu(2, 1)
            attention1(0, 4, 1)
            attention1(1, 6, 0)
            glu(3, 0)
            glu(3, 1)
            for u in range(UPH, NB):
                add_phase(5, u)

        @block.tensor
        def _(pe):
            te = nc.tensor

            def product(dst, left, right, first=True, last=True):
                for n, (a, b) in enumerate(PASSES):
                    ins = te.matmul(dst, left(a), right(b), start=first and n == 0, stop=last and n == 2,
                                    skip_group_check=True)
                return ins

            def turn(n, hf):
                for u in range(UPH * hf, UPH * hf + UPH):
                    if n == 5:
                        pe.wait_ge(o1_done, NG1 * (hf + 1))
                    else:
                        pe.wait_ge(xn_done, 2 * norm_count(n, u) + 2)
                    for t in range(2):
                        for k in range(KD):
                            src = O1S[:, 2 * u + t, k * P:(k + 1) * P] if n == 5 else XN[:, u % 2, t, k * P:(k + 1) * P]
                            ins = te.transpose(PS[:, u, k * S + t * P:k * S + (t + 1) * P], src, IDF[:, :])
                    ins.then_inc(turned, 1)

            def clear(hf):
                for u in range(UPH * hf, UPH * hf + UPH):
                    te.matmul(PS[:, u, :], ZERO[:, :], SEL[:, 0:512], start=True, stop=False, skip_group_check=True)

            def route_logits(n, hf):
                pe.wait_ge(turned_lo, turn_count(n, UPH * hf + 1) + 1)
                if (n, hf) == (3, 0):
                    pe.wait_ge(wg_lo, 1)
                for t in range(TPH):
                    tok = slice((TPH * hf + t) * P, (TPH * hf + t + 1) * P)
                    for k in range(KD):
                        ins = product(PS[:, 2 * hf, t * 16:(t + 1) * 16], lambda s: XT[:, s, k, tok],
                                      lambda s: WGS[:, s, k, :], k == 0, k == KD - 1)
                ins.then_inc(logits, 1)

            def route_turn(n, hf):
                m = ROUTED.index((n, hf))
                pe.wait_ge(route, ROUTE_STEPS * (m + 1))
                for t in range(TPH):
                    ins = te.transpose(PS[:, 2 * hf + 1, :].bitcast(F16)[:, t * P:(t + 1) * P], CMB[:, t, :], IDH[:, :])
                ins.then_inc(cmb_turned, 1)

            def down(f, hf, j, a, st):
                pe.wait_ge(hid_lo, st + 1)
                w = weights(f)
                for t in range(TPH):
                    ins = product(y_tiles(UPH * hf + t // 2)[:, t % 2, :], lambda s: HH[:, a, s, t * P:(t + 1) * P],
                                  lambda s: w[:, j, s, 2 * D:3 * D], first=False, last=False)
                ins.then_inc(down_done, 1)

            def last_down(f, hf):
                j = TILES[f] - 1
                down(f, hf, j, j % 2, steps_before(f, hf) + j)

            def glu(f, hf, tail):
                w, n = weights(f), GLU_TURN[f]
                tok = slice(hf * HALF, (hf + 1) * HALF)

                def step(f, hf, j, a):
                    st = steps_before(f, hf) + j
                    start = isinstance(j, int) and j == 0
                    if start:
                        pe.wait_ge(turned_lo, turn_count(n, UPH * hf + 1) + 1)
                    if (f, hf) == (0, 0):
                        wait_split(pe, j + 1)
                    if (f, hf) == (2, 0) and isinstance(j, int) and j in (0, 4):
                        wait_split(pe, W_ALL if j else W_ALL - 1)
                    after(pe, gated, st if start else st - 1)
                    for k in range(KD):
                        ins = product(PS[:, GATE[a], :], lambda s: w[:, j, s, k * P:(k + 1) * P],
                                      lambda s: XT[:, s, k, tok], k == 0, k == KD - 1)
                    ins.then_inc(gate_done, 1)
                    if start:
                        tail[0]()
                    after(pe, up_mul, st)
                    for k in range(KD):
                        ins = product(PS[:, UP, :], lambda s: w[:, j, s, D + k * P:D + (k + 1) * P],
                                      lambda s: XT[:, s, k, tok], k == 0, k == KD - 1)
                    ins.then_inc(up_done, 1)
                    if f >= 2:
                        if start:
                            pe.wait_ge(cbt_done, ROUTED.index((n, hf)) + 1)
                        after(pe, comb_mul, st - STEPS[2])
                        te.matmul(PS[:, COMB, :], SEL[:, ds(j * P, P)], CBT[:, hf, :], start=True,
                                  stop=True).then_inc(comb_done, 1)
                    if start:
                        tail[1]()
                        clear(hf)
                    else:
                        down(f, hf, j - 1, 1 - a, st - 1)

                def side(f, hf, j):
                    t = HOSTED[f, hf]
                    if t and j == 2:
                        turn(*t)
                    if t in ROUTED and j == 3:
                        route_logits(*t)

                run_glu(pe, f, hf, step, side)
                if HOSTED[f, hf] in ROUTED:
                    route_turn(*HOSTED[f, hf])

            def queries(hf, h, bank, r, read):
                pe.wait_ge(rope_cos, read)
                for k in range(KD):
                    ins = product(PS[:, bank, :], lambda s: WB16[:, h, s, k * P:(k + 1) * P],
                                  lambda s: XT[:, s, k, hf * HALF:(hf + 1) * HALF], k == 0, k == KD - 1)
                ins.then_inc(rope_in, 1)

            def step0(hf, p, x):
                st, r = NS0 * hf + 4 * p + x, RU * hf + KV0 + 2 * p
                a = x % 2
                if lagged(p, x, 0, P0):
                    g = p // (GRP // 2)
                    if x % 2 == 0:
                        pe.wait_ge(rope_lo, r + x // 2 + 1)
                    after(pe, exp_done, 2 * st - 2)
                    bank = odd_bank(hf) if a else 5
                    for qt in range(2):
                        q0 = a * S + qt * P
                        ins = product(PS[:, bank, qt * S:(qt + 1) * S], lambda s: QT0[:, x // 2, s, q0:q0 + P],
                                      lambda s: KT0[:, s, g, a * S:(a + 1) * S], True, qt == 1)
                        if qt == 0:
                            te.matmul(PS[:, bank, P:S], IDB[:, :], MASK[:, :], start=False, stop=True,
                                      skip_group_check=True)
                    ins.then_inc(scores, 1)
                if lagged(p, x, 2, P0):
                    pe.wait_ge(norm_done, st - 1)
                    after(pe, pt_lo, st - 3)
                    bank = odd_bank(hf) + 1 if a else 6
                    for qt in range(2):
                        for kt in range(2):
                            ins = te.transpose(PS[:, bank, kt * S + qt * P:kt * S + (qt + 1) * P],
                                               PR0[:, a, qt * S + kt * P:qt * S + (kt + 1) * P], IDF[:, :])
                    ins.then_inc(pt_done, 1)
                if item := lagged(p, x, 3, P0):
                    pp, xx = item
                    g = pp // (GRP // 2)
                    pe.wait_ge(pt_lo, st - 2)
                    after(pe, ot_lo, st - 3)
                    for kt in range(2):
                        ins = product(PS[:, OB, 0:S], lambda s: V0[:, s, TPH * hf + 2 * (xx % 2) + kt, ds(g * P, P)],
                                      lambda s: PT0[:, xx % 2, s, kt * S:(kt + 1) * S], kt == 0, kt == 1)
                    ins.then_inc(pv_done, 1)
                if item := lagged(p, x, 4, P0):
                    pp, xx = item
                    pe.wait_ge(ot_lo, st - 3)
                    for t in range(2):
                        ins = product(y_tiles(UPH * hf + xx % 2)[:, t, :], lambda s: OT0[:, xx % 2, s, t * P:(t + 1) * P],
                                      lambda s: WB16[:, 2 * pp + xx // 2, s, D:2 * D], False, False)
                    ins.then_inc(proj_done, 1)
                if x % 2 == 0 and not (isinstance(p, int) and p >= P0 - 1):
                    queries(hf, 2 * p + 2 + x // 2, QB, r + 2 + x // 2, r + 2 + x // 2)

            def attention0(hf, n, th):
                r = RU * hf
                tok = slice(hf * HALF, (hf + 1) * HALF)

                def values(i):
                    t = TPH * hf + i
                    for k in range(KD):
                        ins = product(PS[:, value_bank(hf, i), :].rearrange("p (c n) -> p c n", c=2),
                                      lambda s: XT[:, s, k, t * P:(t + 1) * P],
                                      lambda s: WA16[:, 4 + 2 * k:6 + 2 * k, s, GLU:], k == 0, k == KD - 1)
                    ins.then_inc(v_in, 1)

                pe.wait_ge(turned_lo, turn_count(1, UPH * hf + 1) + 1)
                for i in range(KV0):
                    after(pe, rope_cos, r + i - 1)
                    for k in range(KD):
                        ins = product(PS[:, QB + i % 2, :], lambda s: WA16[:, i, s, GLU + k * P:GLU + (k + 1) * P],
                                      lambda s: XT[:, s, k, tok], k == 0, k == KD - 1)
                    ins.then_inc(rope_in, 1)
                    if hf:
                        step0(0, P0, i)
                    elif i == 0:
                        last_down(0, 1)
                    else:
                        values(i - 1)
                for i in range(0 if hf else KV0 - 1, TPH):
                    values(i)
                if hf == 0:
                    wait_split(pe, 2 * JF)
                queries(hf, 0, QB, r + KV0, r + KV0 - 1)
                if hf:
                    queries(hf, 1, QB + 1, r + KV0 + 1, r + KV0)
                turn(n, th)
                if not hf:
                    queries(hf, 1, QB + 1, r + KV0 + 1, r + KV0)
                pe.wait_ge(v_lo, TPH * (hf + 1))
                clear(hf)
                pe.wait_ge(turned_lo, turn_count(n, UPH * th + 1) + 1)
                for x in range(4):
                    step0(hf, 0, x)
                with pe.Fori(1, P0 - 1) as p:
                    for x in range(4):
                        step0(hf, p, x)
                for x in range(4):
                    step0(hf, P0 - 1, x)

            def turn_qk(hf, i):
                t, a = TPH * hf + i, i % 2
                pe.wait_ge(qk1_lo, 2 * t + 2)
                after(pe, q1_copied, 2 * t)
                for x in range(H1):
                    src = QK1[:, a, :, :].rearrange("p h n -> p (h n)")[:, x * P:(x + 1) * P]
                    dst = PS[:, 6 if x < H1 // 2 else 7, :].bitcast(F16)
                    y = x % (H1 // 2)
                    ins = te.transpose(dst[:, y * P:(y + 1) * P], src, IDH[:, :])
                ins.then_inc(qk1_turned, 1)

            def step1(hf, p, q):
                g = NG1 * hf + 4 * p + q
                a = q % 2
                bank = 4 if a else 2 * hf
                if lagged(p, q, 0, P1):
                    after(pe, exp1_done, g - 1)
                    for i in range(2):
                        for qt, c0 in ((0, 0), (1, P)):
                            te.matmul(PS[:, bank + i, c0:c0 + (qt + 1) * P],
                                      QT1[:, 2 * p + q // 2, i * S + qt * P:i * S + (qt + 1) * P],
                                      KZ1[:, 4 * p + q, i * S:i * S + (qt + 1) * P], start=qt == 0, stop=False,
                                      skip_group_check=True)
                            ins = te.matmul(PS[:, bank + i, 2 * c0:2 * c0 + P], IDB[:, :], MASK[:, :], start=False,
                                            stop=False, skip_group_check=True)
                    ins.then_inc(scores1, 1)
                if lagged(p, q, 2, P1):
                    pe.wait_ge(exp1_done, g - 1)
                    after(pe, pt1_lo, g - 2)
                    for i in range(2 * BLK1):
                        ins = te.transpose(PS[:, 6 + i // 4, (i % 4) * P:(i % 4 + 1) * P],
                                           PR1[:, a, i * P:(i + 1) * P], IDF[:, :])
                    ins.then_inc(pt1_done, 1)
                if item := lagged(p, q, 3, P1):
                    h, b = 4 * item[0] + item[1], 1 - a
                    pe.wait_ge(pt1_lo, g - 2)
                    for i in range(2):
                        for qt in range(2):
                            for kt in range(qt + 1):
                                blk = BLK1 * i + qt + kt
                                c0 = (2 * i + qt) * 32
                                ins = product(PS[:, odd_bank(hf) + b, c0:c0 + VC1],
                                              lambda s: PT1[:, b, s, blk * P:(blk + 1) * P],
                                              lambda s: VB1[:, s, TPH * hf + 2 * i + kt, h, :], kt == 0, kt == qt)
                    ins.then_inc(pv1_done, 1)
                if lagged(p, q, 0, P1):
                    pe.wait_ge(shift1_done, g + 1)
                    for i in range(2):
                        for qt, c0 in ((0, 0), (1, P)):
                            n = (qt + 1) * P
                            ins = te.matmul(PS[:, bank + i, c0:c0 + n], IDB[:, :],
                                            MB1[:, a, 2 * qt + i:2 * qt + i + 1].broadcast_to([P, n]),
                                            start=False, stop=qt == 1, skip_group_check=True)
                    ins.then_inc(shifted1, 1)

            def attention1(hf, n, th):
                pe.wait_ge(turned_lo, turn_count(4, UPH * hf + 1) + 1)
                for i in range(TPH):
                    t, a = TPH * hf + i, i % 2
                    tok = slice(t * P, (t + 1) * P)
                    if i >= 2:
                        pe.wait_ge(rope1_mul, 3 * t - 3)
                    for k in range(KD):
                        ins = product(PS[:, 2 * hf + a, :].rearrange("p (c n) -> p c n", c=2),
                                      lambda s: XT[:, s, k, tok], lambda s: WD16[:, 3 * k:3 * k + 2, s, :],
                                      k == 0, k == KD - 1)
                    ins.then_inc(qk1_in, 1)
                    if (hf, i) == (0, 0):
                        last_down(2, 1)
                    if i >= 2:
                        pe.wait_ge(v1_lo, t - 1)
                    for k in range(KD):
                        ins = product(PS[:, 4 + a, 0:D], lambda s: XT[:, s, k, tok],
                                      lambda s: WD16[:, 3 * k + 2, s, :], k == 0, k == KD - 1)
                    ins.then_inc(v1_in, 1)
                    if i:
                        turn_qk(hf, i - 1)
                turn_qk(hf, TPH - 1)
                turn(n, th)
                pe.wait_ge(turned_lo, turn_count(n, UPH * th + 1) + 1)
                if (n, th) in ROUTED:
                    route_logits(n, th)
                    route_turn(n, th)
                    pe.wait_ge(cbt_done, ROUTED.index((n, th)) + 1)
                pe.wait_ge(ones_set, 2)
                pe.wait_ge(q1_copied, 2 * TPH * (hf + 1))
                for q in range(4):
                    step1(hf, 0, q)
                with pe.Fori(1, P1) as p:
                    for q in range(4):
                        step1(hf, p, q)
                for q in range(3):
                    step1(hf, P1, q)
                turn(5, hf)
                for u in range(UPH * hf, UPH * hf + UPH):
                    pe.wait_ge(turned_lo, turn_count(5, u) + 1)
                    for t in range(2):
                        for k in range(KD):
                            ins = product(y_tiles(u)[:, t, :], lambda s: XT[:, s, k, (2 * u + t) * P:(2 * u + t + 1) * P],
                                          lambda s: WD16[:, 6 + k, s, :], k == 0, k == KD - 1)
                    ins.then_inc(proj1_done, 1)

            nothing = (lambda: None, lambda: None)

            def left_down(f, hf):
                return lambda: None, lambda: last_down(f, hf)

            def last_steps0():
                step0(1, P0, 1)
                step0(1, P0, 2)
                step0(1, P0, 3)

            pe.wait_ge(dma_id, 16)
            turn(0, 0)
            pe.wait_ge(narrowed, 3)
            pe.wait_ge(zeroed, 6)
            pe.wait_ge(dma_sel, 16)
            glu(0, 0, nothing)
            glu(0, 1, left_down(0, 0))
            attention0(0, 1, 1)
            attention0(1, 2, 0)
            glu(1, 0, (lambda: step0(1, P0, 0), last_steps0))
            glu(1, 1, left_down(1, 0))
            glu(2, 0, left_down(1, 1))
            glu(2, 1, left_down(2, 0))
            attention1(0, 4, 1)
            attention1(1, 6, 0)
            glu(3, 0, nothing)
            glu(3, 1, left_down(3, 0))
            last_down(3, 1)


def _pack(np, t):
    def feats(w):
        return np.stack([w[:P], w[P:]], axis=1)

    def glu(gate, up, down):
        n = -(-gate.shape[1] // P) * P
        g, u, d = np.zeros((D, n), np.float32), np.zeros((D, n), np.float32), np.zeros((n, D), np.float32)
        g[:, :gate.shape[1]], u[:, :gate.shape[1]], d[:gate.shape[1]] = gate, up, down
        return [np.concatenate([feats(g[:, c:c + P]).reshape(P, D), feats(u[:, c:c + P]).reshape(P, D),
                                d[c:c + P]], axis=1) for c in range(0, n, P)]

    gu, wk, wv = t["L0_ffn_w_gate_up"], t["L0_attn_Wk"], t["L0_attn_Wv"]
    a = glu(gu[:INTER].T, gu[INTER:].T, t["L0_ffn_w_down"].T)
    kv = [feats(wk[g * P:(g + 1) * P].T).reshape(P, D) for g in range(KV0)]
    kv += [wv[(i % 2) * D:(i % 2 + 1) * D, (i // 2) * P:(i // 2 + 1) * P].T for i in range(4)]
    wa = np.concatenate([x for pair in zip(a, kv) for x in pair], axis=1)
    wq, wo = t["L0_attn_Wq"], t["L0_attn_Wo"]
    wb = np.concatenate([x for h in range(H0) for x in (feats(wq[h * P:(h + 1) * P].T).reshape(P, D),
                                                        wo[:, h * P:(h + 1) * P].T)], axis=1)
    side = lambda n, s: np.concatenate([t["L1_ffn_w_" + n].transpose(1, 0, 2).reshape(D, E * I_EXP), t["L1_ffn_sw_" + s]], axis=1)
    wc = np.concatenate(glu(side("gate", "gate"), side("up", "up"),
                            np.concatenate([t["L1_ffn_w_down"].reshape(E * I_EXP, D), t["L1_ffn_sw_down"]])), axis=1)
    qkv, wo1 = t["L1_attn_W_qkv"].T, t["L1_attn_W_o"].T
    wd = np.concatenate([qkv[:P], qkv[P:], wo1[:P], wo1[P:]], axis=1)
    wg = np.zeros((D, 16), np.float32)
    wg[:, :E], wg[:, E:E + 1] = t["L1_ffn_gate_w"].T, t["L1_ffn_shared_gate_w"]
    return [wa, wb, wc, wd, feats(wg)]


def _tables(np):
    f = np.float32
    scale = f(SQ / (SX * SW))

    def angles(n, half):
        inv = f(1.0) / np.power(f(10000.0), (np.arange(0, 2 * half, 2, dtype=f) / f(2 * half)))
        return np.repeat(np.arange(n, dtype=f)[:, None] * inv[None, :], 2, axis=1)

    a0 = angles(S, P // 2).T
    sign0 = np.where(np.arange(P) < P // 2, f(-1), f(1))[:, None]
    rope0 = np.stack([np.cos(a0) * scale, np.sin(a0) * sign0 * scale], axis=1)
    a1 = angles(S, DH1 // 2).reshape(2, P, DH1).transpose(1, 0, 2)
    sign1 = np.where(np.arange(DH1) % 2 == 0, f(-1), f(1))
    rope1 = np.stack([np.cos(a1) * scale, np.sin(a1) * sign1 * scale], axis=2)
    i = np.arange(P)
    mask = np.where(i[None, :] <= i[:, None], f(0), f(-1e30))
    eye = np.eye(P, dtype=f)
    e = np.arange(E)
    tri = np.broadcast_to((e[None, :] < e[:, None]).astype(f), (P, E, E))
    sel = np.zeros((32, JM * P), np.float16)
    owner = np.minimum(np.arange(JM * P) // I_EXP, E)
    for part in range(2):
        sel[part * GATES + owner, np.arange(JM * P)] = 1
    return [rope0, rope1, mask, eye, tri, sel]


def kernel(**inputs):
    import numpy as np
    import concourse.bacc as bacc
    from concourse.bass_utils import run_bass_kernel_spmd as run

    t = {k: np.asarray(v) for k, v in inputs.items()}
    nc = bacc.Bacc("TRN2", target_bir_lowering=False, num_devices=1)
    names = ["x", "wa", "wb", "wc", "wd", "wg", "rope0", "rope1", "mask", "idf", "tri", "sel"]
    arrays, args = {}, []
    for name, a in zip(names, [t["L0_attn_x"]] + _pack(np, t) + _tables(np)):
        a = np.ascontiguousarray(a)
        arrays[name + "_dram"] = a
        args.append(nc.dram_tensor(name + "_dram", a.shape, mybir.dt.from_np(a.dtype), kind="ExternalInput").ap())
    args.append(nc.dram_tensor("out_dram", (NB, S, D), F32, kind="ExternalOutput").ap())
    macaron(nc, *args)
    return run(nc, [arrays], core_ids=[0]).results[0]["out_dram"]
```

```python
import math
from contextlib import ExitStack

import concourse.bass as bass
from concourse import mybir

P = 128
D = 256
KD = D // P
NB = 4
S = 256
TOK = NB * S
TT = TOK // P
HALF = TOK // 2
TPH = HALF // P
UPH = 2
INTER = 1024
JF = INTER // P
E, I_EXP, I_SH = 8, 176, 704
JM = -(-(E * I_EXP + I_SH) // P)
assert (E * I_EXP + I_SH) % P == P // 2
JR = 13
assert (JR - 1) * P >= E * I_EXP
GATES = E + 1
GLU = 3 * D
H0, KV0 = 16, 4
GRP = H0 // KV0
SC0 = P ** -0.5
NS0 = 2 * H0
RU = KV0 + H0
H1, DH1 = 16, 16
SC1 = DH1 ** -0.5
VC1 = DH1 + 1
NG1 = H1
BLK1 = 3
EPS = 1e-5

SX = 2.0 ** 6
SW = 2.0 ** 10
SH = 2.0 ** 5
SQ = 2.0 ** 4
SP = 2.0 ** 10
SR = 2.0 ** 8

A_N, B_N, C_N, D_N = GLU + D, 4 * D, GLU, D

F32, F16, BF16 = mybir.dt.float32, mybir.dt.float16, mybir.dt.bfloat16
ALU = mybir.AluOpType
ACT = mybir.ActivationFunctionType
AX = mybir.AxisListType
PASSES = ((0, 0), (0, 1), (1, 0))


def macaron(nc, x_in, wa_in, wb_in, wc_in, wd_in, wg_in, rope0_in, rope1_in, mask_in, idf_in,
            tri_in, sel_in, out):
    ds = bass.ds
    ctx = ExitStack()
    with ctx:
        def sb(name, shape, dt):
            return ctx.enter_context(nc.sbuf_tensor(name, shape, dt))

        def sem(name):
            return ctx.enter_context(nc.semaphore(name))

        WA = sb("WA", [P, A_N * (JF + 1)], F32)
        WB = sb("WB", [P, B_N * (JF + 1)], F32)
        WC = sb("WC", [P, C_N * (JM + 1)], F32)
        WD = WB[:, 0:D_N * 9]
        WA16 = WA[:, 0:A_N * JF].bitcast(F16).rearrange("p (c s n) -> p c s n", c=JF, s=2)
        WB16 = WB[:, 0:B_N * JF].bitcast(F16).rearrange("p (h s n) -> p h s n", h=H0, s=2)
        WC16 = WC[:, 0:C_N * JM].bitcast(F16).rearrange("p (c s n) -> p c s n", c=JM, s=2)
        WD16 = WB[:, 0:D_N * 8].bitcast(F16).rearrange("p (c s n) -> p c s n", c=8, s=2)
        WGR = sb("WGR", [P, KD, 16], F32)
        WGS = sb("WGS", [P, 2, KD, 16], F16)

        X = sb("X", [P, TT, D], F32)
        XT = sb("XT", [P, 2, KD, TOK], F16)
        XN = sb("XN", [P, 2, 2, D], F32)
        BST = sb("BST", [P, NB, 2, 6], F32)
        MV = sb("MV", [P, NB, 2, 2], F32)
        RSTD = sb("RSTD", [P, NB, 2, 2], F32)
        NHALF = sb("NHALF", [P, 2], F32)
        T1 = sb("T1", [P, 2, HALF], F32)
        T2 = sb("T2", [P, 2, HALF], F32)
        T3 = sb("T3", [P, HALF], F32)

        NK0 = 2 * KV0 * HALF
        KVR = sb("KVR", [P, NK0 + 2 * TT * KV0 * P], F16)
        KT0 = KVR[:, 0:NK0].rearrange("p (s g t) -> p s g t", s=2, g=KV0)
        V0 = KVR[:, NK0:].rearrange("p (s t n) -> p s t n", s=2, t=TT)
        KZ1 = KVR[:, 0:H1 * HALF].rearrange("p (h t) -> p h t", h=H1)
        QT1 = KVR[:, H1 * HALF:].rearrange("p (h t) -> p h t", t=HALF)

        ARENA = sb("ARENA", [P, 3584], F32)
        PR0 = ARENA[:, 0:1024].rearrange("p (a n) -> p a n", a=2)
        PT0 = ARENA[:, 1024:2048].bitcast(F16).rearrange("p (a s n) -> p a s n", a=2, s=2)
        OT0 = ARENA[:, 2048:2560].bitcast(F16).rearrange("p (a s n) -> p a s n", a=2, s=2)
        QT0 = ARENA[:, 2560:3584].bitcast(F16).rearrange("p (a s n) -> p a s n", a=2, s=2)
        HH = ARENA[:, 0:1024].bitcast(F16).rearrange("p (a s n) -> p a s n", a=2, s=2)
        QK1 = ARENA[:, 0:2048].bitcast(F16).rearrange("p (a h n) -> p a h n", a=2, h=2 * H1)
        PR1 = ARENA[:, 0:1536].rearrange("p (a n) -> p a n", a=2)
        PT1 = ARENA[:, 1536:3072].bitcast(F16).rearrange("p (a s n) -> p a s n", a=2, s=2)
        RC = ARENA[:, 2048:2560].rearrange("p (a t e f) -> p a t e f", a=2, t=TPH, e=E)
        RL = ARENA[:, 2560:2624].rearrange("p (t n) -> p t n", t=TPH)
        RE = ARENA[:, 2624:3136].rearrange("p (a t n) -> p a t n", a=8, t=TPH)
        CMB = sb("CMB", [P, TPH, P], F16)
        CBT = sb("CBT", [P, 2, HALF], F16)
        ST = sb("ST", [P, 2, 4, 2], F32)
        MB1 = sb("MB1", [P, 2, 4], BF16)
        R1 = sb("R1", [P, 2, 4], F32)

        VB1 = WA[:, 0:TT * H1 * VC1].bitcast(F16).rearrange("p (s t h n) -> p s t h n", s=2, t=TT, h=H1)
        O1S = WA[:, 2304:2304 + TT * D].rearrange("p (t n) -> p t n", t=TT)

        ROPE0 = sb("ROPE0", [P, 2, S], F32)
        ROPE1 = sb("ROPE1", [P, 2, 2, DH1], F32)
        MASK = sb("MASK", [P, P], BF16)
        IDH = sb("IDH", [P, P], F16)
        IDB = sb("IDB", [P, P], BF16)
        IDF = sb("IDF", [P, P], F32)
        ZERO = sb("ZERO", [P, P], F16)
        SWT = sb("SWT", [P, 1], F32)
        LNSP = sb("LNSP", [P, 1], F32)
        LNSP2 = sb("LNSP2", [P, 1], F32)
        TRI = sb("TRI", [P, E, E], F32)
        SEL = sb("SEL", [P, JM * P], F16)

        PS = ctx.enter_context(nc.psum_tensor("PS", [P, 8, 512], F32))
        GATE, UP, COMB = (4, 7), 5, 6
        QB, OB = 4, 7

        dma_x = [sem(f"dma_x{i}") for i in range(2)]
        dma_a = [sem(f"dma_a{i}") for i in range(5)]
        dma_b = [sem(f"dma_b{i}") for i in range(1)]
        dma_c = [sem(f"dma_c{i}") for i in range(2)]
        dma_d, dma_out = sem("dma_d"), sem("dma_out")
        dma_id, dma_wg, dma_const, dma_sel = (sem(n) for n in ("dma_id", "dma_wg", "dma_const", "dma_sel"))
        dma_mask, narrowed = sem("dma_mask"), sem("narrowed")
        zeroed, table = sem("zeroed"), sem("table")
        w_scaled, w_lo_pool = sem("w_scaled"), sem("w_lo_pool")
        w_hi, w_lo, wg_hi, wg_lo = (sem(n) for n in ("w_hi", "w_lo", "wg_hi", "wg_lo"))
        x_sum, bn_half, bn_done = sem("x_sum"), sem("bn_half"), sem("bn_done")
        var_scaled, rstd_done, xn_done = sem("var_scaled"), sem("rstd_done"), sem("xn_done")
        turned, turned_hi, turned_lo = sem("turned"), sem("turned_hi"), sem("turned_lo")
        gate_done, up_done, comb_done = sem("gate_done"), sem("up_done"), sem("comb_done")
        tanh_done, gated, up_mul, comb_mul = sem("tanh_done"), sem("gated"), sem("up_mul"), sem("comb_mul")
        hid_hi, hid_lo, down_done = sem("hid_hi"), sem("hid_lo"), sem("down_done")
        logits, max_route, route, route_act = sem("logits"), sem("max_route"), sem("route"), sem("route_act")
        cmb_turned, cbt_done = sem("cmb_turned"), sem("cbt_done")
        rope_in, rope_swap, rope_cos, rope_sin = (sem(n) for n in ("rope_in", "rope_swap", "rope_cos", "rope_sin"))
        rope_sum, rope_hi, rope_lo = sem("rope_sum"), sem("rope_hi"), sem("rope_lo")
        v_in, v_hi, v_lo = sem("v_in"), sem("v_hi"), sem("v_lo")
        scores, max_done, shift_done = sem("scores"), sem("max_done"), sem("shift_done")
        exp_done, recip_done, norm_done = sem("exp_done"), sem("recip_done"), sem("norm_done")
        pt_done, pt_hi, pt_lo = sem("pt_done"), sem("pt_hi"), sem("pt_lo")
        pv_done, ot_hi, ot_lo, proj_done = sem("pv_done"), sem("ot_hi"), sem("ot_lo"), sem("proj_done")
        kz_zero, ones_set = sem("kz_zero"), sem("ones_set")
        qk1_in, v1_in, v1_hi, v1_lo = sem("qk1_in"), sem("v1_in"), sem("v1_hi"), sem("v1_lo")
        rope1_mul, rope1_sum, qk1_hi, qk1_lo = (sem(n) for n in ("rope1_mul", "rope1_sum", "qk1_hi", "qk1_lo"))
        qk1_turned, q1_copied, k1_copied = sem("qk1_turned"), sem("q1_copied"), sem("k1_copied")
        scores1, shift1_done, shifted1 = (sem(n) for n in ("scores1", "shift1_done", "shifted1"))
        exp1_done, pt1_done, pt1_hi, pt1_lo = (sem(n) for n in ("exp1_done", "pt1_done", "pt1_hi", "pt1_lo"))
        pv1_done, recip1_done, o1_done, proj1_done = (sem(n) for n in ("pv1_done", "recip1_done", "o1_done", "proj1_done"))

        block = ctx.enter_context(nc.Block())

        def after(eng, semaphore, count):
            if not isinstance(count, int) or count > 0:
                eng.wait_ge(semaphore, count)

        TILES = [JF, JF, JM, JM]
        STEPS = [0, 2 * JF, 4 * JF, 4 * JF + 2 * JM, 4 * JF + 4 * JM]
        GLU_TURN, GLU_OF = [0, 2, 3, 6], [0, 2, 3, 5]
        Y_SCALE = [0.5 / (SH * SW), 1.0 / (SQ * SW), 0.5 / (SH * SW), 0.5 / (SH * SW), 1.0 / (SQ * SW),
                   0.5 / (SH * SW)]
        TURNS = [(n, h) for n in range(5) for h in range(2)] + [(5, 0), (6, 0), (5, 1), (6, 1)]
        NORMS = [t for t in TURNS if t[0] != 5]
        ROUTED = [(3, 0), (3, 1), (6, 0), (6, 1)]

        def turn_count(n, u):
            return UPH * TURNS.index((n, u // UPH)) + u % UPH

        def norm_count(n, u):
            return UPH * NORMS.index((n, u // UPH)) + u % UPH

        def steps_before(f, hf):
            return STEPS[f] + hf * TILES[f]

        def y_ready(eng, phase, u):
            hf = u // UPH
            if phase in GLU_OF:
                f = GLU_OF.index(phase)
                eng.wait_ge(down_done, steps_before(f, hf) + TILES[f])
            elif phase == 1:
                eng.wait_ge(proj_done, NS0 * hf + NS0 - 1 + u % UPH)
            else:
                eng.wait_ge(proj1_done, u + 1)

        def last_tile(f, j):
            return f >= 2 and isinstance(j, int) and j == JM - 1

        def rows(f, j):
            return slice(0, P // 2 if last_tile(f, j) else P)

        def combs(f, hf, j):
            before = sum(JM if x == (2, 1) else JR for x in ((2, 0), (2, 1), (3, 0)) if x < (f, hf))
            return before + (min(j, JR - 1) if isinstance(j, int) and (f, hf) != (2, 1) else j) + 1

        def weights(f):
            return WA16 if f < 2 else WC16

        def y_tiles(u):
            return PS[:, u, :].rearrange("p (t n) -> p t n", t=2)

        def split_a(j):
            return j, WA[:, ds((j + 1) * A_N, A_N)], WA16[:, j, 0, :], WA16[:, j, 1, :], 1

        def split_b(j):
            raw = WB[:, ds((j + 1) * B_N, B_N)].rearrange("p (h n) -> p h n", h=2)
            return JF + j, raw, WB16[:, ds(2 * j, 2), 0, :], WB16[:, ds(2 * j, 2), 1, :], 1

        def split_c(number, c):
            return number, WC[:, ds((c + 1) * C_N, C_N)], WC16[:, c, 0, :], WC16[:, c, 1, :], 1

        def split_d(j):
            return 3 * JF + 2 * j + 1, WD[:, ds((j + 1) * D_N, D_N)], WD16[:, j, 0, :], WD16[:, j, 1, :], 2

        W_ALL = 5 * JF + 1

        def share(x, i):
            if len(x.shape) == 3:
                return x[:, i, :]
            n = x.shape[1] // 2
            return x[:, i * n:(i + 1) * n]

        def wait_split(eng, count):
            eng.wait_ge(w_lo, count)
            eng.wait_ge(w_lo_pool, count)

        def splits(f, hf, j):
            if (f, hf) == (0, 0):
                return [] if isinstance(j, int) and j >= JF - 2 else [split_a(j + 2)]
            if (f, hf) == (0, 1):
                return [split_b(j)]
            if (f, hf) == (1, 0):
                return [split_c(2 * JF + j, j)]
            if (f, hf) == (1, 1):
                return [split_c(3 * JF + 2 * j, JF + j), split_d(j)]
            if (f, hf) == (2, 0) and isinstance(j, int) and j == 0:
                return [split_c(W_ALL - 1, JM - 1)]
            return []

        HOSTED = {(0, 0): (0, 1), (0, 1): (1, 0), (1, 0): (2, 1), (1, 1): (3, 0), (2, 0): (3, 1),
                  (2, 1): (4, 0), (3, 0): (6, 1), (3, 1): None}

        def run_glu(eng, f, hf, step, side, tile=None):
            if (f, hf) == (2, 1):
                for j in range(4):
                    step(f, hf, j, j % 2)
                    side(f, hf, j)
                with eng.Fori(0, TPH // 2) as b:
                    for e in range(2):
                        for x in range(3):
                            tile(2 * b + e, e, x)
                            step(f, hf, 4 + 6 * b + 3 * e + x, (e + x) % 2)
                        tile(2 * b + e, e, 3)
                for j in range(4 + 3 * TPH, JM):
                    step(f, hf, j, j % 2)
                return
            first = 5 if HOSTED[f, hf] in ROUTED else 3
            for j in range(first):
                step(f, hf, j, j % 2)
                side(f, hf, j)
            pairs = (JR - 1) // 2 if f >= 2 else (TILES[f] - 1) // 2 - ((f, hf) == (0, 0))
            with eng.Fori((first - 1) // 2, pairs) as pair:
                for e in range(2):
                    step(f, hf, 2 * pair + 1 + e, 1 - e)
            for j in range(2 * pairs + 1, TILES[f]):
                step(f, hf, j, j % 2)

        def lagged(i, x, k, n):
            if isinstance(i, int) and not 0 <= 4 * i + x - k < 4 * n:
                return None
            return (i - 1 if x < k else i), (x - k) % 4

        P0, P1 = H0 // 2, H1 // 4
        N_CONST = 3
        ROUTE_STEPS = 14

        def half_of(q, hf):
            return slice(hf * HALF, (hf + 1) * HALF)

        def odd_bank(hf):
            return 2 * (1 - hf)

        def qk_bank(hf, i):
            return 4 + i % 2 if hf else 0

        def v_bank(hf, i):
            return 2 + i % 2 if hf else 1

        def turned_bank(hf):
            return 6 if hf else 0

        def place(hf, i):
            return i % 2 if hf else 1

        def pt1_part(a, s, i):
            return PT1[:, a, s, i * BLK1 * P:(i + 1) * BLK1 * P]

        def up_bank(f, a):
            return UP + (a if f < 2 else 0)

        def value_bank(hf, i):
            return 2 * hf + i if i < 2 else 4 + i

        @block.sync
        def _(sp):
            x3 = x_in.rearrange("b (t p) d -> p (b t) d", p=P)
            o3 = out.rearrange("b (t p) d -> p (b t) d", p=P)
            sp.dma_start(X[:, 0:TPH, :], x3[:, 0:TPH, :]).then_inc(dma_x[0], 16)
            sp.dma_start(WA[:, A_N:2 * A_N], wa_in[:, 0:A_N]).then_inc(dma_a[0], 16)
            sp.dma_start(WA[:, 2 * A_N:3 * A_N], wa_in[:, A_N:2 * A_N]).then_inc(dma_a[1], 16)
            sp.dma_start(X[:, TPH:, :], x3[:, TPH:, :]).then_inc(dma_x[1], 16)
            sp.dma_start(WA[:, 3 * A_N:4 * A_N], wa_in[:, 2 * A_N:3 * A_N]).then_inc(dma_a[2], 16)
            sp.dma_start(WA[:, 4 * A_N:5 * A_N], wa_in[:, 3 * A_N:4 * A_N]).then_inc(dma_a[3], 16)
            sp.dma_start(WA[:, 5 * A_N:], wa_in[:, 4 * A_N:]).then_inc(dma_a[4], 16)
            for dst, src in ((ROPE0, rope0_in), (ROPE1, rope1_in), (TRI, tri_in)):
                sp.dma_start(dst.ap(), src).then_inc(dma_const, 16)
            sp.dma_start(WB[:, B_N:], wb_in).then_inc(dma_b[0], 16)
            sp.dma_start(WC[:, C_N:9 * C_N], wc_in[:, 0:8 * C_N]).then_inc(dma_c[0], 16)
            sp.dma_start(WC[:, 9 * C_N:], wc_in[:, 8 * C_N:]).then_inc(dma_c[1], 16)
            sp.wait_ge(proj_done, 2 * NS0)
            sp.dma_start(WD[:, D_N:], wd_in).then_inc(dma_d, 16)
            for u in range(NB):
                sp.wait_ge(x_sum, 5 * NB + u + 1)
                sp.dma_start(o3[:, 2 * u:2 * u + 2, :], X[:, 2 * u:2 * u + 2, :]).then_inc(dma_out, 16)
            sp.wait_ge(dma_out, 16 * NB)

        @block.gpsimd
        def _(pool):
            pl = nc.gpsimd
            pl.memset(ZERO[:, :], 0.0).then_inc(zeroed, 1)
            pl.memset(CMB[:, :, :], 0.0).then_inc(zeroed, 1)
            pl.memset(NHALF[:, :], -0.5).then_inc(zeroed, 1)
            pl.memset(LNSP[:, :], math.log(SP)).then_inc(zeroed, 1)
            pl.memset(SEL[:, :], 0.0).then_inc(zeroed, 1)
            pl.memset(SWT[:, :], SW).then_inc(zeroed, 1)
            pool.wait_ge(zeroed, 6)
            pl.dma_start(SEL[0:32, :], sel_in).then_inc(dma_sel, 16)

            def turn(n, hf, units=range(UPH)):
                for u in (UPH * hf + i for i in units):
                    c = norm_count(n, u)
                    pool.wait_ge(bn_done, 2 * c + 2)
                    pl.tensor_scalar(RSTD[:, u, 0, :], MV[:, u, :, 1], SX ** -2, EPS * SX ** -2,
                                     ALU.mult, ALU.add).then_inc(var_scaled, 1)
                    pool.wait_ge(var_scaled, c + 1)
                    pl.tensor_tensor(RSTD[:, u, 1, :], RSTD[:, u, 0, :], NHALF[:, :],
                                     ALU.pow).then_inc(rstd_done, 1)

            def split(c, raw, hi, lo, back):
                r = share(raw, 1)
                pool.wait_ge(w_hi, c + 1)
                pl.tensor_tensor(r, r, SWT[:, :].broadcast_to(list(r.shape)), ALU.mult).then_inc(w_scaled, 1)
                pool.wait_ge(w_scaled, c + 1)
                pl.tensor_tensor(share(lo, 1), r, share(hi, 1), ALU.subtract).then_inc(w_lo_pool, 1)

            def glu_step(f, hf, j, a):
                st = steps_before(f, hf) + j
                for x in splits(f, hf, j):
                    split(*x)
                if f >= 2:
                    pool.wait_ge(hid_hi, st + 1)
                    r = rows(f, j)
                    pl.tensor_tensor(HH[r, a, 1, :], T3[r, :], HH[r, a, 0, :], ALU.subtract).then_inc(hid_lo, 1)

            def glu_side(f, hf, j):
                if HOSTED[f, hf] and j < 2:
                    turn(*HOSTED[f, hf], (j,))
                if (f, hf) == (2, 0) and j > 0:
                    prepare1(j - 1)

            def prepare1(i):
                pool.wait_ge(proj_done, 2 * NS0)
                pool.wait_ge(hid_lo, STEPS[2] + i + 2)
                pool.wait_ge(w_lo_pool, W_ALL)
                pool.wait_ge(rstd_done, norm_count(3, NB - 1) + 1)
                k6 = KZ1.rearrange("p (h e) t -> p h e t", e=2)
                rows = slice(P // 2, P) if i % 2 == 0 else slice(0, P // 2)
                heads = slice(i // 2 * H1 // 4, (i // 2 + 1) * H1 // 4)
                pl.memset(k6[rows, heads, i % 2, :], 0.0).then_inc(kz_zero, 1)
                pool.wait_ge(kz_zero, i + 1)
                if i == 3:
                    pool.wait_ge(down_done, STEPS[2])
                    pl.memset(VB1[:, 0, :, :, DH1:], 1.0).then_inc(ones_set, 1)
                    pool.wait_ge(ones_set, 1)
                    pl.memset(VB1[:, 1, :, :, DH1:], 0.0).then_inc(ones_set, 1)
                    pool.wait_ge(ones_set, 2)

            def rope_sine(r, a):
                pool.wait_ge(rope_swap, 2 * r + 2)
                t2 = T2[:, a, :].rearrange("p (b t) -> p b t", b=2)
                pl.tensor_tensor(t2, t2, ROPE0[:, 1:2, :].broadcast_to([P, 2, S]), ALU.mult).then_inc(rope_sin, 1)

            def rope_add(r, a):
                pool.wait_ge(rope_cos, r + 1)
                pool.wait_ge(rope_sin, r + 1)
                pl.tensor_tensor(T1[:, a, :], T1[:, a, :], T2[:, a, :], ALU.add).then_inc(rope_sum, 1)

            def step0(hf, p, x):
                st, r = NS0 * hf + 4 * p + x, RU * hf + KV0 + 2 * p
                more, before = not (isinstance(p, int) and p == P0 - 1), not (isinstance(p, int) and p == 0)
                if x == 0 and before:
                    rope_add(r + 1, 1)
                if x == 2 and more:
                    rope_add(r + 2, 0)
                pool.wait_ge(recip_done, st + 1)
                pr = PR0[:, x % 2, :].rearrange("p (q k) -> p q k", q=2)
                rs = ST[:, x % 2, 3, :].rearrange("p (q k) -> p q k", k=1)
                pl.tensor_tensor(pr, pr, rs.broadcast_to([P, 2, S]), ALU.mult).then_inc(norm_done, 1)
                if x % 2 and more:
                    rope_sine(r + 2 + x // 2, x // 2)

            def attention0(hf, n, th):
                for i in range(KV0 + 2):
                    rope_sine(RU * hf + i, i % 2)
                    rope_add(RU * hf + i, i % 2)
                    if i == (4 if hf else 2):
                        turn(n, th)
                for x in range(4):
                    step0(hf, 0, x)
                with pool.Fori(1, P0 - 1) as p:
                    for x in range(4):
                        step0(hf, p, x)
                for x in range(4):
                    step0(hf, P0 - 1, x)

            def rotated1(t, a):
                pool.wait_ge(rope1_mul, 3 * t + 3)
                pl.tensor_tensor(T1[:, a, :], T1[:, a, :], T2[:, a, :], ALU.add).then_inc(rope1_sum, 1)

            def qk1_low(t, a):
                pool.wait_ge(qk1_hi, 2 * t + 2)
                t4 = T1[:, a, :].rearrange("p (h o n) -> p h o n", o=1, n=DH1)
                q4 = QK1[:, a, 0:H1, :].rearrange("p h (c s n) -> p h c s n", c=2, s=2)
                k4 = QK1[:, a, H1:, :].rearrange("p h (s c n) -> p h s c n", c=2, s=2)
                pl.tensor_tensor(q4[:, :, :, 1, :], t4[:, 0:H1].broadcast_to([P, H1, 2, DH1]),
                                 q4[:, :, :, 0, :], ALU.subtract).then_inc(qk1_lo, 1)
                pl.tensor_tensor(k4[:, :, 1, :, :], t4[:, H1:].broadcast_to([P, H1, 2, DH1]),
                                 k4[:, :, 0, :, :], ALU.subtract).then_inc(qk1_lo, 1)

            def tile1(t, e, x):
                if x == 0:
                    rotated1(t, place(0, e))
                if x == 1:
                    qk1_low(t, place(0, e))

            turn(0, 0)
            split(*split_a(0))
            split(*split_a(1))
            run_glu(pool, 0, 0, glu_step, glu_side)
            run_glu(pool, 0, 1, glu_step, glu_side)
            pool.wait_ge(dma_const, 16 * N_CONST)
            attention0(0, 1, 1)
            attention0(1, 2, 0)
            run_glu(pool, 1, 0, glu_step, glu_side)
            run_glu(pool, 1, 1, glu_step, glu_side)
            run_glu(pool, 2, 0, glu_step, glu_side)
            run_glu(pool, 2, 1, glu_step, glu_side, tile1)
            turn(4, 1)
            for i in range(TPH):
                rotated1(TPH + i, place(1, i))
                qk1_low(TPH + i, place(1, i))
                if i == 1:
                    turn(6, 0)
            run_glu(pool, 3, 0, glu_step, glu_side)
            run_glu(pool, 3, 1, glu_step, glu_side)

        @block.scalar
        def _(act):
            sc = nc.scalar
            act.dma_start(IDF[:, :], idf_in).then_inc(dma_id, 16)
            act.dma_start(WGR[:, :, :], wg_in).then_inc(dma_wg, 16)
            act.dma_start(T3[:, 0:P], mask_in).then_inc(dma_mask, 16)

            def split(c, raw, hi, lo, back):
                after(act, w_lo, c - back + 1)
                after(act, w_lo_pool, c - back + 1)
                sc.activation(hi, raw, ACT.Copy, scale=SW).then_inc(w_hi, 1)

            def turn_high(n, hf):
                for u in range(UPH * hf, UPH * hf + UPH):
                    act.wait_ge(turned, turn_count(n, u) + 1)
                    sc.activation(XT[:, 0, :, u * S:(u + 1) * S],
                                  PS[:, u, :].rearrange("p (k t) -> p k t", k=KD), ACT.Copy).then_inc(turned_hi, 1)

            def routing(n, hf):
                m = ROUTED.index((n, hf))
                act.wait_ge(route, ROUTE_STEPS * m + 2)
                sc.activation(RE[:, 1, :, 0:E], RE[:, 0, :, 0:E], ACT.Exp).then_inc(route_act, 1)
                sc.activation(RE[:, 1, :, E:GATES], RL[:, :, E:GATES], ACT.Tanh, scale=0.5).then_inc(route_act, 1)

            def glu_step(f, hf, j, a):
                st = steps_before(f, hf) + j
                if (f, hf) == (0, 0) and isinstance(j, int) and j < 3:
                    act.wait_ge(dma_a[j + 2], 16)
                act.wait_ge(gate_done, st + 1)
                after(act, gated, st)
                r = rows(f, j)
                sc.activation(T1[r, 0, :], PS[r, GATE[a], :], ACT.Tanh, scale=0.5 / (SX * SW)).then_inc(tanh_done, 1)
                if last_tile(f, j):
                    sc.activation(T1[r, 1, :], PS[P // 2:, GATE[a], :], ACT.Copy).then_inc(up_done, 1)
                for x in splits(f, hf, j):
                    split(*x)
                if f < 2:
                    act.wait_ge(up_mul, st + 1)
                else:
                    act.wait_ge(comb_mul, st - STEPS[2] + 1)
                after(act, down_done, st if isinstance(j, int) and j == 0 else st - 1)
                sc.activation(HH[r, a, 0, :], T3[r, :], ACT.Copy).then_inc(hid_hi, 1)

            def glu_side(f, hf, j):
                t = HOSTED[f, hf]
                if t and j == 2:
                    turn_high(*t)
                if t in ROUTED and j == 3:
                    routing(*t)

            def rope_swapped(r, bank, a):
                act.wait_ge(rope_in, r + 1)
                after(act, rope_sum, r - 1)
                lo, hi = slice(0, P // 2), slice(P // 2, P)
                sc.activation(T2[lo, a, :], PS[hi, bank, :], ACT.Copy).then_inc(rope_swap, 1)
                sc.activation(T2[hi, a, :], PS[lo, bank, :], ACT.Copy).then_inc(rope_swap, 1)

            def rope_high(r, a, hi):
                act.wait_ge(rope_sum, r + 1)
                sc.activation(hi, T1[:, a, :], ACT.Copy).then_inc(rope_hi, 1)

            def step0(hf, p, x):
                st, r = NS0 * hf + 4 * p + x, RU * hf + KV0 + 2 * p
                more, before = not (isinstance(p, int) and p >= P0 - 1), not (isinstance(p, int) and p in (0, P0))
                if lagged(p, x, 2, P0):
                    act.wait_ge(pt_done, st - 1)
                    after(act, pv_done, st - 3)
                    bank = odd_bank(hf) + 1 if x % 2 else 6
                    sc.activation(PT0[:, x % 2, 0, :], PS[:, bank, :], ACT.Copy, scale=SP).then_inc(pt_hi, 1)
                if lagged(p, x, 0, P0):
                    act.wait_ge(shift_done, st + 1)
                    bank = odd_bank(hf) if x % 2 else 5
                    for qt in range(2):
                        sc.activation(PR0[:, x % 2, qt * S:(qt + 1) * S], PS[:, bank, qt * S:(qt + 1) * S],
                                      ACT.Exp, bias=ST[:, x % 2, 1, qt:qt + 1], scale=SC0 / SQ ** 2,
                                      accum_out=ST[:, x % 2, 2, qt:qt + 1]).then_inc(exp_done, 1)
                if lagged(p, x, 3, P0):
                    act.wait_ge(pv_done, st - 2)
                    sc.activation(OT0[:, 1 - x % 2, 0, :], PS[:, OB, 0:S], ACT.Copy, scale=1 / SP).then_inc(ot_hi, 1)
                if x % 2 and more:
                    rope_swapped(r + 2 + x // 2, QB, x // 2)
                if x == 0 and before:
                    act.wait_ge(scores, st)
                    rope_high(r + 1, 1, QT0[:, 1, 0, :])
                if x == 2 and more:
                    act.wait_ge(scores, st)
                    rope_high(r + 2, 0, QT0[:, 0, 0, :])

            def attention0(hf, n, th):
                r = RU * hf
                def value_high(i):
                    t = TPH * hf + i
                    act.wait_ge(v_in, t + 1)
                    sc.activation(V0[:, 0, t, :], PS[:, value_bank(hf, i), :], ACT.Copy,
                                  scale=SQ / (SX * SW)).then_inc(v_hi, 1)

                for i in range(KV0):
                    rope_swapped(r + i, QB + i % 2, i % 2)
                    if i:
                        rope_high(r + i - 1, 1 - i % 2, KT0[:, 0, i - 1, :])
                    if hf and i < 3:
                        step0(0, P0, i)
                    if not hf and i >= 2:
                        value_high(i - 2)
                rope_swapped(r + KV0, QB, 0)
                if hf:
                    value_high(0)
                rope_high(r + KV0 - 1, 1, KT0[:, 0, KV0 - 1, :])
                if hf:
                    value_high(1)
                value_high(2)
                rope_swapped(r + KV0 + 1, QB + 1, 1)
                value_high(3)
                rope_high(r + KV0, 0, QT0[:, 0, 0, :])
                turn_high(n, th)
                rope_high(r + KV0 + 1, 1, QT0[:, 1, 0, :])
                for x in range(4):
                    step0(hf, 0, x)
                with act.Fori(1, P0 - 1) as p:
                    for x in range(4):
                        step0(hf, p, x)
                for x in range(4):
                    step0(hf, P0 - 1, x)

            def values1_high(hf, i, t):
                act.wait_ge(v1_in, t + 1)
                sc.activation(VB1[:, 0, t, :, 0:DH1], PS[:, v_bank(hf, i), 0:D].rearrange("p (h n) -> p h n", n=DH1),
                              ACT.Copy, scale=SQ / (SX * SW)).then_inc(v1_hi, 1)

            def qk1_high(hf, t, a):
                act.wait_ge(rope1_sum, t + 1)
                t4 = T1[:, a, :].rearrange("p (h o n) -> p h o n", o=1, n=DH1)
                q4 = QK1[:, a, 0:H1, :].rearrange("p h (c s n) -> p h c s n", c=2, s=2)
                k4 = QK1[:, a, H1:, :].rearrange("p h (s c n) -> p h s c n", c=2, s=2)
                sc.activation(q4[:, :, :, 0, :], t4[:, 0:H1].broadcast_to([P, H1, 2, DH1]),
                              ACT.Copy).then_inc(qk1_hi, 1)
                sc.activation(k4[:, :, 0, :, :], t4[:, H1:].broadcast_to([P, H1, 2, DH1]),
                              ACT.Copy).then_inc(qk1_hi, 1)

            def copies1(hf, i, t):
                act.wait_ge(qk1_turned, t + 1)
                q = PS[:, turned_bank(hf), :].bitcast(F16).rearrange("p (h t) -> p h t", t=P)
                k = PS[P // 2:, turned_bank(hf) + 1, :].bitcast(F16).rearrange("p (h t) -> p h t", t=P)
                sc.activation(QT1[:, :, ds(i * P, P)], q, ACT.Copy).then_inc(q1_copied, 1)
                act.wait_ge(k1_copied, t + 1)
                sc.activation(KZ1.rearrange("p (h e) t -> p h e t", e=2)[P // 2:, :, 1, ds(i * P, P)], k,
                              ACT.Copy).then_inc(q1_copied, 1)

            def tile1(t, e, x):
                if x == 0:
                    values1_high(0, e, t)
                if x == 1:
                    qk1_high(0, t, place(0, e))
                if x == 2:
                    copies1(0, t, t)

            def step1(hf, p, q):
                g = NG1 * hf + 4 * p + q
                if lagged(p, q, 2, P1):
                    after(act, pv1_done, g - 3)
                    for i in range(2):
                        act.wait_ge(pt1_done, 2 * g - 3 + i)
                        sc.activation(pt1_part(q % 2, 0, i), PS[:, 6 + i, 0:BLK1 * P], ACT.Copy).then_inc(pt1_hi, 1)
                if lagged(p, q, 0, P1):
                    act.wait_ge(shifted1, g + 1)
                    bank = 4 if q % 2 else 2 * hf
                    sc.activation(PR1[:, q % 2, :].rearrange("p (b n) -> p b n", b=2),
                                  PS[:, bank:bank + 2, 0:384], ACT.Exp, bias=LNSP[:, :],
                                  scale=SC1 / SQ ** 2).then_inc(exp1_done, 1)

            def attention1():
                def half(hf):
                    for q in range(4):
                        step1(hf, 0, q)
                        if q == 2 and hf == 0:
                            turn_high(4, 1)
                    with act.Fori(1, P1) as p:
                        for q in range(4):
                            step1(hf, p, q)
                    step1(hf, P1, 0)
                    step1(hf, P1, 1)
                    turn_high(5, hf)

                def high(i):
                    values1_high(1, i, TPH + i)
                    qk1_high(1, TPH + i, place(1, i))

                half(0)
                high(0)
                high(1)
                copies1(1, 0, TPH)
                high(2)
                copies1(1, 1, TPH + 1)
                values1_high(1, 3, TPH + 3)
                turn_high(6, 0)
                qk1_high(1, TPH + 3, place(1, 3))
                copies1(1, 2, TPH + 2)
                routing(6, 0)
                copies1(1, 3, TPH + 3)
                half(1)

            act.wait_ge(zeroed, 6)
            sc.activation(LNSP2[:, :], LNSP[:, :], ACT.Tanh).then_inc(table, 1)
            act.wait_ge(dma_a[0], 16)
            split(*split_a(0))
            turn_high(0, 0)
            act.wait_ge(dma_wg, 16)
            sc.activation(WGS[:, 0, :, :], WGR[:, :, :], ACT.Copy, scale=SW).then_inc(wg_hi, 1)
            act.wait_ge(dma_a[1], 16)
            split(*split_a(1))
            run_glu(act, 0, 0, glu_step, glu_side)
            act.wait_ge(dma_b[0], 16)
            run_glu(act, 0, 1, glu_step, glu_side)
            act.wait_ge(zeroed, 6)
            attention0(0, 1, 1)
            attention0(1, 2, 0)
            for x in range(3):
                step0(1, P0, x)
            act.wait_ge(dma_c[0], 16)
            run_glu(act, 1, 0, glu_step, glu_side)
            act.wait_ge(dma_c[1], 16)
            act.wait_ge(dma_d, 16)
            run_glu(act, 1, 1, glu_step, glu_side)
            run_glu(act, 2, 0, glu_step, glu_side)
            act.wait_ge(kz_zero, 4)
            run_glu(act, 2, 1, glu_step, glu_side, tile1)
            attention1()
            run_glu(act, 3, 0, glu_step, glu_side)
            run_glu(act, 3, 1, glu_step, glu_side)

        @block.vector
        def _(dve):
            v = nc.vector

            def split(c, raw, hi, lo, back):
                dve.wait_ge(w_hi, c + 1)
                v.scalar_tensor_tensor(share(lo, 0), share(raw, 0), SW, share(hi, 0), ALU.mult,
                                       ALU.subtract).then_inc(w_lo, 1)

            def add_phase(phase, u):
                y_ready(dve, phase, u)
                v.scalar_tensor_tensor(X[:, 2 * u:2 * u + 2, :], y_tiles(u), Y_SCALE[phase],
                                       X[:, 2 * u:2 * u + 2, :], ALU.mult, ALU.add).then_inc(x_sum, 1)

            def turn_add(n, u):
                if n:
                    add_phase(n - 1 if n < 5 else 4, u)

            def turn_variance(n, u):
                c, phase = norm_count(n, u), n - 1 if n < 5 else 4
                if n:
                    dve.wait_ge(x_sum, phase * NB + u + 1)
                else:
                    dve.wait_ge(dma_x[u // UPH], 16)
                for t in range(2):
                    v.bn_stats(BST[:, u, t, :], X[:, 2 * u + t, :]).then_inc(bn_half, 1)
                dve.wait_ge(bn_half, 2 * c + 2)
                for t in range(2):
                    v.bn_aggr(MV[:, u, t, :], BST[:, u, t, :]).then_inc(bn_done, 1)

            def turn_stats(n, hf, units=range(UPH)):
                for u in (UPH * hf + i for i in units):
                    turn_add(n, u)
                    turn_variance(n, u)

            def turn_norm(n, hf):
                for u in range(UPH * hf, UPH * hf + UPH):
                    dve.wait_ge(rstd_done, norm_count(n, u) + 1)
                    for t in range(2):
                        v.tensor_scalar(XN[:, u % 2, t, :], X[:, 2 * u + t, :], MV[:, u, t, 0:1],
                                        RSTD[:, u, 1, t:t + 1], ALU.subtract, ALU.mult).then_inc(xn_done, 1)

            def turn_low(n, hf):
                for u in range(UPH * hf, UPH * hf + UPH):
                    dve.wait_ge(turned_hi, turn_count(n, u) + 1)
                    v.tensor_tensor(XT[:, 1, :, u * S:(u + 1) * S], PS[:, u, :].rearrange("p (k t) -> p k t", k=KD),
                                    XT[:, 0, :, u * S:(u + 1) * S], ALU.subtract).then_inc(turned_lo, 1)

            made = [0]

            def link(ins):
                made[0] += 1
                ins.then_inc(route, 1)
                dve.wait_ge(route, made[0])

            def per_expert(x):
                return x.broadcast_to([P, TPH, E])

            def routing_ranks(n, hf):
                l, m = RL[:, :, 0:E], RE[:, 2, :, 0:1]
                dve.wait_ge(logits, ROUTED.index((n, hf)) + 1)
                link(v.tensor_scalar(RL[:, :, 0:GATES], PS[:, 2 * hf, 0:TPH * 16].rearrange("p (t n) -> p t n", t=TPH)
                                     [:, :, 0:GATES], 1 / (SX * SW), None, ALU.mult))
                v.tensor_reduce(m, l, AX.X, ALU.max).then_inc(max_route, 1)
                dve.wait_ge(max_route, ROUTED.index((n, hf)) + 1)
                link(v.tensor_tensor(RE[:, 0, :, 0:E], l, per_expert(m), ALU.subtract))
                lf = l.rearrange("p t (o e) -> p t o e", o=1).broadcast_to([P, TPH, E, E])
                le = l.rearrange("p t (e o) -> p t e o", o=1).broadcast_to([P, TPH, E, E])
                link(v.tensor_tensor(RC[:, 0], lf, le, ALU.is_equal))
                link(v.tensor_tensor(RC[:, 0], RC[:, 0], TRI[:, :, :].rearrange("p (o e) f -> p o e f", o=1)
                                     .broadcast_to([P, TPH, E, E]), ALU.mult))
                link(v.tensor_tensor(RC[:, 1], lf, le, ALU.is_gt))
                link(v.tensor_tensor(RC[:, 0], RC[:, 0], RC[:, 1], ALU.add))
                link(v.tensor_reduce(RE[:, 3, :, 0:E], RC[:, 0], AX.X, ALU.add))

            def routing_weights(n, hf):
                dve.wait_ge(route_act, 2 * ROUTED.index((n, hf)) + 2)
                link(v.scalar_tensor_tensor(RE[:, 4, :, 0:E], RE[:, 3, :, 0:E], 2.0, RE[:, 1, :, 0:E], ALU.is_lt,
                                            ALU.mult))
                link(v.tensor_reduce(RE[:, 5, :, 0:1], RE[:, 4, :, 0:E], AX.X, ALU.add))
                link(v.reciprocal(RE[:, 6, :, 0:1], RE[:, 5, :, 0:1]))
                link(v.scalar_tensor_tensor(RE[:, 7, :, 0:E], RE[:, 4, :, 0:E], SR, per_expert(RE[:, 6, :, 0:1]),
                                            ALU.mult, ALU.mult))
                link(v.tensor_scalar(RE[:, 7, :, E:GATES], RE[:, 1, :, E:GATES], 0.5 * SR, 0.5 * SR, ALU.mult,
                                     ALU.add))
                link(v.tensor_copy(CMB[:, :, 0:GATES], RE[:, 7, :, 0:GATES]))
                link(v.tensor_tensor(CMB[:, :, GATES:2 * GATES], RE[:, 7, :, 0:GATES], CMB[:, :, 0:GATES],
                                     ALU.subtract))
                assert made[0] % ROUTE_STEPS == 0, made

            def routing_turned(n, hf):
                dve.wait_ge(cmb_turned, ROUTED.index((n, hf)) + 1)
                v.tensor_copy(CBT[:, hf, :], PS[:, 2 * hf + 1, 0:HALF // 2].bitcast(F16)).then_inc(cbt_done, 1)

            def glu_step(f, hf, j, a):
                st = steps_before(f, hf) + j
                dve.wait_ge(tanh_done, st + 1)
                after(dve, up_mul, st)
                r = rows(f, j)
                v.scalar_tensor_tensor(T2[r, 0, :], T1[r, 0, :], 1.0, PS[r, GATE[a], :], ALU.add,
                                       ALU.mult).then_inc(gated, 1)
                dve.wait_ge(up_done, st + 1)
                dve.wait_ge(gated, st + 1)
                after(dve, hid_lo, st)
                scale = 0.5 * SH / (SX * SW) ** 2 / (1 if f < 2 else SR)
                up = T1[r, 1, :] if last_tile(f, j) else PS[:, up_bank(f, a), :]
                v.scalar_tensor_tensor(T3[r, :], T2[r, 0, :], scale, up, ALU.mult,
                                       ALU.mult).then_inc(up_mul, 1)
                if f >= 2:
                    dve.wait_ge(comb_done, combs(f, hf, j))
                    dve.wait_ge(up_mul, st + 1)
                    v.tensor_tensor(T3[r, :], T3[r, :], PS[r, COMB, :], ALU.mult).then_inc(comb_mul, 1)
                for x in splits(f, hf, j):
                    split(*x)
                if HOSTED[f, hf] and isinstance(j, int) and j == 1:
                    n, th = HOSTED[f, hf]
                    turn_variance(n, UPH * th + 1)
                if f < 2:
                    dve.wait_ge(hid_hi, st + 1)
                    v.tensor_tensor(HH[:, a, 1, :], T3[:, :], HH[:, a, 0, :], ALU.subtract).then_inc(hid_lo, 1)

            def glu_side(f, hf, j):
                t = HOSTED[f, hf]
                if t is None:
                    if j == 1:
                        add_phase(5, 0)
                        add_phase(5, 1)
                    return
                if j == 0:
                    turn_stats(*t, (0,))
                    turn_add(t[0], UPH * t[1] + 1)
                if j in (1, 2):
                    (turn_norm, turn_low)[j - 1](*t)
                if t in ROUTED and j >= 3:
                    (routing_ranks, routing_weights)[j - 3](*t)

            def glu(f, hf, tile=None):
                run_glu(dve, f, hf, glu_step, glu_side, tile)
                if HOSTED[f, hf] in ROUTED:
                    routing_turned(*HOSTED[f, hf])

            def rope_cosine(r, bank, a):
                dve.wait_ge(rope_swap, 2 * r + 2)
                after(dve, rope_lo, r - 1)
                v.tensor_tensor(T1[:, a, :].rearrange("p (b t) -> p b t", b=2),
                                PS[:, bank, :].rearrange("p (b t) -> p b t", b=2),
                                ROPE0[:, 0:1, :].broadcast_to([P, 2, S]), ALU.mult).then_inc(rope_cos, 1)

            def rope_low(r, a, lo, hi):
                dve.wait_ge(rope_hi, r + 1)
                v.tensor_tensor(lo, T1[:, a, :], hi, ALU.subtract).then_inc(rope_lo, 1)

            def step0(hf, p, x):
                st, r = NS0 * hf + 4 * p + x, RU * hf + KV0 + 2 * p
                more, before = not (isinstance(p, int) and p >= P0 - 1), not (isinstance(p, int) and p in (0, P0))
                if lagged(p, x, 0, P0):
                    dve.wait_ge(scores, st + 1)
                    bank = odd_bank(hf) if x % 2 else 5
                    v.tensor_reduce(ST[:, x % 2, 0, :], PS[:, bank, :].rearrange("p (q k) -> p q k", q=2),
                                    AX.X, ALU.max).then_inc(max_done, 1)
                    dve.wait_ge(max_done, st + 1)
                    v.tensor_scalar(ST[:, x % 2, 1, :], ST[:, x % 2, 0, :], -SC0 / SQ ** 2, None,
                                    ALU.mult).then_inc(shift_done, 1)
                if x == 0 and before:
                    rope_cosine(r + 1, QB, 1)
                if x == 2 and more:
                    rope_cosine(r + 2, QB, 0)
                if x == 1 and before:
                    rope_low(r + 1, 1, QT0[:, 1, 1, :], QT0[:, 1, 0, :])
                if x == 3 and more:
                    rope_low(r + 2, 0, QT0[:, 0, 1, :], QT0[:, 0, 0, :])
                if lagged(p, x, 2, P0):
                    dve.wait_ge(pt_hi, st - 1)
                    bank = odd_bank(hf) + 1 if x % 2 else 6
                    v.scalar_tensor_tensor(PT0[:, x % 2, 1, :], PS[:, bank, :], SP, PT0[:, x % 2, 0, :], ALU.mult,
                                           ALU.subtract).then_inc(pt_lo, 1)
                if lagged(p, x, 0, P0):
                    dve.wait_ge(exp_done, 2 * st + 2)
                    v.reciprocal(ST[:, x % 2, 3, :], ST[:, x % 2, 2, :]).then_inc(recip_done, 1)
                if lagged(p, x, 3, P0):
                    dve.wait_ge(ot_hi, st - 2)
                    v.scalar_tensor_tensor(OT0[:, 1 - x % 2, 1, :], PS[:, OB, 0:S], 1 / SP, OT0[:, 1 - x % 2, 0, :],
                                           ALU.mult, ALU.subtract).then_inc(ot_lo, 1)

            def attention0(hf, n, th):
                r = RU * hf
                def value_low(i):
                    t = TPH * hf + i
                    dve.wait_ge(v_hi, t + 1)
                    v.scalar_tensor_tensor(V0[:, 1, t, :], PS[:, value_bank(hf, i), :], SQ / (SX * SW),
                                           V0[:, 0, t, :], ALU.mult, ALU.subtract).then_inc(v_lo, 1)

                for i in range(KV0):
                    rope_cosine(r + i, QB + i % 2, i % 2)
                    if i:
                        rope_low(r + i - 1, 1 - i % 2, KT0[:, 1, i - 1, :], KT0[:, 0, i - 1, :])
                    if hf and i < 3:
                        step0(0, P0, i)
                    if not hf:
                        turn_stats(n, th, (i,)) if i < 2 else value_low(i - 2)
                if hf:
                    turn_stats(n, th, (0,))
                else:
                    turn_norm(n, th)
                rope_cosine(r + KV0, QB, 0)
                if hf:
                    value_low(0)
                    turn_stats(n, th, (1,))
                rope_low(r + KV0 - 1, 1, KT0[:, 1, KV0 - 1, :], KT0[:, 0, KV0 - 1, :])
                if hf:
                    value_low(1)
                value_low(2)
                if hf:
                    turn_norm(n, th)
                rope_cosine(r + KV0 + 1, QB + 1, 1)
                value_low(3)
                rope_low(r + KV0, 0, QT0[:, 0, 1, :], QT0[:, 0, 0, :])
                turn_low(n, th)
                rope_low(r + KV0 + 1, 1, QT0[:, 1, 1, :], QT0[:, 1, 0, :])
                for x in range(4):
                    step0(hf, 0, x)
                with dve.Fori(1, P0 - 1) as p:
                    for x in range(4):
                        step0(hf, p, x)
                for x in range(4):
                    step0(hf, P0 - 1, x)

            def rotate1(hf, i, t):
                a = place(hf, i)
                dve.wait_ge(qk1_in, t + 1)
                ps = PS[:, qk_bank(hf, i), :]
                p2, t2 = (x.rearrange("p (h n e) -> p h n e", n=DH1 // 2, e=2) for x in (ps, T2[:, a, :]))
                sn = ROPE1[:, i % 2:i % 2 + 1, 1, :].rearrange("p o (n e) -> p o n e", e=2)
                v.tensor_tensor(T1[:, a, :].rearrange("p (h n) -> p h n", n=DH1), ps.rearrange("p (h n) -> p h n", n=DH1),
                                ROPE1[:, i % 2:i % 2 + 1, 0, :].broadcast_to([P, 2 * H1, DH1]),
                                ALU.mult).then_inc(rope1_mul, 1)
                for e in range(2):
                    v.tensor_tensor(t2[:, :, :, e], p2[:, :, :, 1 - e],
                                    sn[:, :, :, e].broadcast_to([P, 2 * H1, DH1 // 2]),
                                    ALU.mult).then_inc(rope1_mul, 1)

            def values1_low(hf, i, t):
                dve.wait_ge(v1_hi, t + 1)
                v.scalar_tensor_tensor(VB1[:, 1, t, :, 0:DH1],
                                       PS[:, v_bank(hf, i), 0:D].rearrange("p (h n) -> p h n", n=DH1),
                                       SQ / (SX * SW), VB1[:, 0, t, :, 0:DH1], ALU.mult,
                                       ALU.subtract).then_inc(v1_lo, 1)

            def copies1(hf, i, t):
                dve.wait_ge(qk1_turned, t + 1)
                k = PS[0:P // 2, turned_bank(hf) + 1, :].bitcast(F16).rearrange("p (h t) -> p h t", t=P)
                v.tensor_copy(KZ1.rearrange("p (h e) t -> p h e t", e=2)[0:P // 2, :, 0, ds(i * P, P)],
                              k).then_inc(k1_copied, 1)

            def tile1(t, e, x):
                if x == 0:
                    rotate1(0, e, t)
                    values1_low(0, e, t)
                if x == 2:
                    copies1(0, t, t)

            def step1(hf, p, q):
                g = NG1 * hf + 4 * p + q
                a = q % 2
                if lagged(p, q, 0, P1):
                    dve.wait_ge(scores1, g + 1)
                    bank = 4 if a else 2 * hf
                    for qt, cols in ((0, slice(0, P)), (1, slice(P, 3 * P))):
                        v.tensor_reduce(MB1[:, a, 2 * qt:2 * qt + 2], PS[:, bank:bank + 2, cols], AX.X, ALU.max,
                                        negate=True).then_inc(shift1_done, 1)
                item, turned_item = lagged(p, q, 3, P1), lagged(p, q, 2, P1)

                def low(i):
                    dve.wait_ge(pt1_hi, 2 * g - 3 + i)
                    v.tensor_tensor(pt1_part(a, 1, i), PS[:, 6 + i, 0:BLK1 * P], pt1_part(a, 0, i),
                                    ALU.subtract).then_inc(pt1_lo, 1)

                if turned_item:
                    low(0)
                if item:
                    b = 1 - a
                    o = PS[:, odd_bank(hf) + b, 0:128].rearrange("p (t n) -> p t n", t=4)
                    r1 = R1[:, b, :].rearrange("p (t n) -> p t n", n=1)
                    dve.wait_ge(pv1_done, g - 2)
                    v.reciprocal(r1, o[:, :, DH1:VC1]).then_inc(recip1_done, 1)
                if turned_item:
                    low(1)
                if item:
                    dve.wait_ge(recip1_done, g - 2)
                    v.tensor_tensor(O1S[:, TPH * hf:TPH * hf + 4, ds((4 * item[0] + item[1]) * DH1, DH1)],
                                    o[:, :, 0:DH1], r1.broadcast_to([P, 4, DH1]), ALU.mult).then_inc(o1_done, 1)

            def attention1():
                def half(hf):
                    for q in range(4):
                        step1(hf, 0, q)
                        if hf == 0 and q < 3:
                            (turn_stats, turn_norm, turn_low)[q](4, 1)
                        if hf and q == 0:
                            routing_weights(6, 0)
                            routing_turned(6, 0)
                    with dve.Fori(1, P1) as p:
                        for q in range(4):
                            step1(hf, p, q)
                    for q in range(3):
                        step1(hf, P1, q)

                def rotate(i):
                    dve.wait_ge(qk1_lo, 2 * (TPH + i) - 2)
                    rotate1(1, i, TPH + i)

                half(0)
                rotate(0)
                turn_low(5, 0)
                values1_low(1, 0, TPH)
                rotate(1)
                values1_low(1, 1, TPH + 1)
                turn_stats(6, 0)
                copies1(1, 0, TPH)
                rotate(2)
                values1_low(1, 2, TPH + 2)
                turn_norm(6, 0)
                copies1(1, 1, TPH + 1)
                rotate(3)
                values1_low(1, 3, TPH + 3)
                turn_low(6, 0)
                copies1(1, 2, TPH + 2)
                routing_ranks(6, 0)
                copies1(1, 3, TPH + 3)
                half(1)
                turn_low(5, 1)

            dve.wait_ge(dma_id, 16)
            v.tensor_copy(IDH[:, :], IDF[:, :]).then_inc(narrowed, 1)
            v.tensor_copy(IDB[:, :], IDF[:, :]).then_inc(narrowed, 1)
            turn_stats(0, 0)
            turn_norm(0, 0)
            split(*split_a(0))
            dve.wait_ge(dma_mask, 16)
            v.tensor_copy(MASK[:, :], T3[:, 0:P]).then_inc(narrowed, 1)
            turn_low(0, 0)
            dve.wait_ge(narrowed, 3)
            dve.wait_ge(wg_hi, 1)
            v.scalar_tensor_tensor(WGS[:, 1, :, :], WGR[:, :, :], SW, WGS[:, 0, :, :], ALU.mult,
                                   ALU.subtract).then_inc(wg_lo, 1)
            split(*split_a(1))
            glu(0, 0)
            glu(0, 1)
            dve.wait_ge(dma_const, 16 * N_CONST)
            attention0(0, 1, 1)
            attention0(1, 2, 0)
            for x in range(3):
                step0(1, P0, x)
            glu(1, 0)
            glu(1, 1)
            glu(2, 0)
            dve.wait_ge(kz_zero, 4)
            glu(2, 1, tile1)
            attention1()
            glu(3, 0)
            glu(3, 1)
            for u in range(UPH, NB):
                add_phase(5, u)

        @block.tensor
        def _(pe):
            te = nc.tensor

            def product(dst, left, right, first=True, last=True):
                for n, (a, b) in enumerate(PASSES):
                    ins = te.matmul(dst, left(a), right(b), start=first and n == 0, stop=last and n == 2,
                                    skip_group_check=True)
                return ins

            def turn(n, hf):
                for u in range(UPH * hf, UPH * hf + UPH):
                    if n == 5:
                        pe.wait_ge(o1_done, NG1 * (hf + 1))
                    else:
                        pe.wait_ge(xn_done, 2 * norm_count(n, u) + 2)
                    for t in range(2):
                        for k in range(KD):
                            src = O1S[:, 2 * u + t, k * P:(k + 1) * P] if n == 5 else XN[:, u % 2, t, k * P:(k + 1) * P]
                            ins = te.transpose(PS[:, u, k * S + t * P:k * S + (t + 1) * P], src, IDF[:, :])
                    ins.then_inc(turned, 1)

            def clear(hf):
                for u in range(UPH * hf, UPH * hf + UPH):
                    te.matmul(PS[:, u, :], ZERO[:, :], SEL[:, 0:512], start=True, stop=False, skip_group_check=True)

            def route_logits(n, hf):
                pe.wait_ge(turned_lo, turn_count(n, UPH * hf + 1) + 1)
                if (n, hf) == (3, 0):
                    pe.wait_ge(wg_lo, 1)
                for t in range(TPH):
                    tok = slice((TPH * hf + t) * P, (TPH * hf + t + 1) * P)
                    for k in range(KD):
                        ins = product(PS[:, 2 * hf, t * 16:(t + 1) * 16], lambda s: XT[:, s, k, tok],
                                      lambda s: WGS[:, s, k, :], k == 0, k == KD - 1)
                ins.then_inc(logits, 1)

            def route_turn(n, hf):
                m = ROUTED.index((n, hf))
                pe.wait_ge(route, ROUTE_STEPS * (m + 1))
                for t in range(TPH):
                    ins = te.transpose(PS[:, 2 * hf + 1, :].bitcast(F16)[:, t * P:(t + 1) * P], CMB[:, t, :], IDH[:, :])
                ins.then_inc(cmb_turned, 1)

            def down(f, hf, j, a, st):
                pe.wait_ge(hid_lo, st + 1)
                w, r = weights(f), rows(f, j)
                for t in range(TPH):
                    ins = product(y_tiles(UPH * hf + t // 2)[:, t % 2, :], lambda s: HH[r, a, s, t * P:(t + 1) * P],
                                  lambda s: w[r, j, s, 2 * D:3 * D], first=False, last=False)
                ins.then_inc(down_done, 1)

            def last_down(f, hf):
                j = TILES[f] - 1
                down(f, hf, j, j % 2, steps_before(f, hf) + j)

            def glu(f, hf, tail):
                w, n = weights(f), GLU_TURN[f]
                tok = slice(hf * HALF, (hf + 1) * HALF)

                def step(f, hf, j, a):
                    st = steps_before(f, hf) + j
                    start = isinstance(j, int) and j == 0
                    if start:
                        pe.wait_ge(turned_lo, turn_count(n, UPH * hf + 1) + 1)
                    if (f, hf) == (0, 0):
                        wait_split(pe, j + 1)
                    if (f, hf) == (2, 0) and isinstance(j, int) and j in (0, 4):
                        wait_split(pe, W_ALL if j else 3 * JF)
                    after(pe, gated, st if start else st - 1)
                    if start:
                        after(pe, up_done, st)
                    for k in range(KD):
                        ins = product(PS[:, GATE[a], :], lambda s: w[:, j, s, k * P:(k + 1) * P],
                                      lambda s: XT[:, s, k, tok], k == 0, k == KD - 1)
                    ins.then_inc(gate_done, 1)
                    if start:
                        tail[0]()
                    if not last_tile(f, j):
                        after(pe, up_mul, st if start or f >= 2 else st - 1)
                        for k in range(KD):
                            ins = product(PS[:, up_bank(f, a), :], lambda s: w[:, j, s, D + k * P:D + (k + 1) * P],
                                          lambda s: XT[:, s, k, tok], k == 0, k == KD - 1)
                        ins.then_inc(up_done, 1)
                    if f >= 2 and not (isinstance(j, int) and j >= JR and (f, hf) != (2, 1)):
                        if start:
                            pe.wait_ge(cbt_done, ROUTED.index((n, hf)) + 1)
                        after(pe, comb_mul, st - STEPS[2])
                        te.matmul(PS[:, COMB, :], SEL[:, ds(j * P, P)], CBT[:, hf, :], start=True,
                                  stop=True).then_inc(comb_done, 1)
                    if start:
                        tail[1]()
                        clear(hf)
                    else:
                        down(f, hf, j - 1, 1 - a, st - 1)

                def side(f, hf, j):
                    t = HOSTED[f, hf]
                    if t and j == 2:
                        turn(*t)
                    if t in ROUTED and j == 3:
                        route_logits(*t)

                run_glu(pe, f, hf, step, side, tile1)
                if HOSTED[f, hf] in ROUTED:
                    route_turn(*HOSTED[f, hf])

            def queries(hf, h, bank, r, read):
                pe.wait_ge(rope_cos, read)
                for k in range(KD):
                    ins = product(PS[:, bank, :], lambda s: WB16[:, h, s, k * P:(k + 1) * P],
                                  lambda s: XT[:, s, k, hf * HALF:(hf + 1) * HALF], k == 0, k == KD - 1)
                ins.then_inc(rope_in, 1)

            def step0(hf, p, x):
                st, r = NS0 * hf + 4 * p + x, RU * hf + KV0 + 2 * p
                a = x % 2
                if lagged(p, x, 0, P0):
                    g = p // (GRP // 2)
                    if x % 2 == 0:
                        pe.wait_ge(rope_lo, r + x // 2 + 1)
                    after(pe, exp_done, 2 * st - 2)
                    bank = odd_bank(hf) if a else 5
                    for qt in range(2):
                        q0 = a * S + qt * P
                        ins = product(PS[:, bank, qt * S:(qt + 1) * S], lambda s: QT0[:, x // 2, s, q0:q0 + P],
                                      lambda s: KT0[:, s, g, a * S:(a + 1) * S], True, qt == 1)
                        if qt == 0:
                            te.matmul(PS[:, bank, P:S], IDB[:, :], MASK[:, :], start=False, stop=True,
                                      skip_group_check=True)
                    ins.then_inc(scores, 1)
                if lagged(p, x, 2, P0):
                    pe.wait_ge(norm_done, st - 1)
                    after(pe, pt_lo, st - 3)
                    bank = odd_bank(hf) + 1 if a else 6
                    for qt in range(2):
                        for kt in range(2):
                            ins = te.transpose(PS[:, bank, kt * S + qt * P:kt * S + (qt + 1) * P],
                                               PR0[:, a, qt * S + kt * P:qt * S + (kt + 1) * P], IDF[:, :])
                    ins.then_inc(pt_done, 1)
                if item := lagged(p, x, 3, P0):
                    pp, xx = item
                    g = pp // (GRP // 2)
                    pe.wait_ge(pt_lo, st - 2)
                    after(pe, ot_lo, st - 3)
                    for kt in range(2):
                        ins = product(PS[:, OB, 0:S], lambda s: V0[:, s, TPH * hf + 2 * (xx % 2) + kt, ds(g * P, P)],
                                      lambda s: PT0[:, xx % 2, s, kt * S:(kt + 1) * S], kt == 0, kt == 1)
                    ins.then_inc(pv_done, 1)
                if item := lagged(p, x, 4, P0):
                    pp, xx = item
                    pe.wait_ge(ot_lo, st - 3)
                    for t in range(2):
                        ins = product(y_tiles(UPH * hf + xx % 2)[:, t, :], lambda s: OT0[:, xx % 2, s, t * P:(t + 1) * P],
                                      lambda s: WB16[:, 2 * pp + xx // 2, s, D:2 * D], False, False)
                    ins.then_inc(proj_done, 1)
                if x in ((1, 2) if isinstance(p, int) and p == 0 else (0, 2)) and not (isinstance(p, int) and p >= P0 - 1):
                    queries(hf, 2 * p + 2 + x // 2, QB, r + 2 + x // 2, r + 2 + x // 2)

            def attention0(hf, n, th):
                r = RU * hf
                tok = slice(hf * HALF, (hf + 1) * HALF)

                def values(i):
                    t = TPH * hf + i
                    for k in range(KD):
                        ins = product(PS[:, value_bank(hf, i), :].rearrange("p (c n) -> p c n", c=2),
                                      lambda s: XT[:, s, k, t * P:(t + 1) * P],
                                      lambda s: WA16[:, 4 + 2 * k:6 + 2 * k, s, GLU:], k == 0, k == KD - 1)
                    ins.then_inc(v_in, 1)

                pe.wait_ge(turned_lo, turn_count(1, UPH * hf + 1) + 1)
                for i in range(KV0):
                    after(pe, rope_cos, r + i - 1)
                    for k in range(KD):
                        ins = product(PS[:, QB + i % 2, :], lambda s: WA16[:, i, s, GLU + k * P:GLU + (k + 1) * P],
                                      lambda s: XT[:, s, k, tok], k == 0, k == KD - 1)
                    ins.then_inc(rope_in, 1)
                    if hf:
                        step0(0, P0, i)
                    elif i == 0:
                        last_down(0, 1)
                    else:
                        values(i - 1)
                if hf == 0:
                    wait_split(pe, 2 * JF)
                queries(hf, 0, QB, r + KV0, r + KV0 - 1)
                for i in range(0 if hf else KV0 - 1, TPH - 1):
                    values(i)
                queries(hf, 1, QB + 1, r + KV0 + 1, r + KV0)
                values(TPH - 1)
                turn(n, th)
                pe.wait_ge(v_lo, TPH * hf + 2)
                clear(hf)
                for x in range(4):
                    if x == 1:
                        pe.wait_ge(turned_lo, turn_count(n, UPH * th + 1) + 1)
                    if x == 2:
                        pe.wait_ge(v_lo, TPH * (hf + 1))
                    step0(hf, 0, x)
                with pe.Fori(1, P0 - 1) as p:
                    for x in range(4):
                        step0(hf, p, x)
                for x in range(4):
                    step0(hf, P0 - 1, x)

            def queries_keys1(hf, i, t):
                for k in range(KD):
                    ins = product(PS[:, qk_bank(hf, i), :].rearrange("p (c n) -> p c n", c=2),
                                  lambda s: XT[:, s, k, ds(t * P, P)], lambda s: WD16[:, 3 * k:3 * k + 2, s, :],
                                  k == 0, k == KD - 1)
                ins.then_inc(qk1_in, 1)

            def values1(hf, i, t):
                for k in range(KD):
                    ins = product(PS[:, v_bank(hf, i), 0:D], lambda s: XT[:, s, k, ds(t * P, P)],
                                  lambda s: WD16[:, 3 * k + 2, s, :], k == 0, k == KD - 1)
                ins.then_inc(v1_in, 1)

            def turn_qk(hf, t, a):
                pe.wait_ge(qk1_lo, 2 * t + 2)
                for x in range(H1):
                    src = QK1[:, a, :, :].rearrange("p h n -> p (h n)")[:, x * P:(x + 1) * P]
                    dst = PS[:, turned_bank(hf) + x // (H1 // 2), :].bitcast(F16)
                    y = x % (H1 // 2)
                    ins = te.transpose(dst[:, y * P:(y + 1) * P], src, IDH[:, :])
                ins.then_inc(qk1_turned, 1)

            def tile1(t, e, x):
                if x == 0:
                    pe.wait_ge(turned_lo, turn_count(4, 1) + 1)
                    queries_keys1(0, e, t)
                    values1(0, e, t)
                if x == 2:
                    pe.wait_ge(v1_lo, t + 1)
                    turn_qk(0, t, place(0, e))
                if x == 3:
                    pe.wait_ge(q1_copied, 2 * t + 2)

            def scores_of(hf, p, q):
                bank = 4 if q % 2 else 2 * hf
                after(pe, exp1_done, NG1 * hf + 4 * p + q - 1)
                for i in range(2):
                    for qt, c0 in ((0, 0), (1, P)):
                        te.matmul(PS[:, bank + i, c0:c0 + (qt + 1) * P],
                                  QT1[:, 2 * p + q // 2, i * S + qt * P:i * S + (qt + 1) * P],
                                  KZ1[:, 4 * p + q, i * S:i * S + (qt + 1) * P], start=qt == 0, stop=False,
                                  skip_group_check=True)
                        ins = te.matmul(PS[:, bank + i, 2 * c0:2 * c0 + P], IDB[:, :], MASK[:, :], start=False,
                                        stop=False, skip_group_check=True)
                ins.then_inc(scores1, 1)

            def step1(hf, p, q):
                g = NG1 * hf + 4 * p + q
                a = q % 2
                bank = 4 if a else 2 * hf
                if lagged(p, q, 2, P1):
                    pe.wait_ge(exp1_done, g - 1)
                    for i in range(2):
                        after(pe, pt1_lo, 2 * g - 5 + i)
                        for j in range(BLK1):
                            ins = te.transpose(PS[:, 6 + i, j * P:(j + 1) * P],
                                               PR1[:, a, (BLK1 * i + j) * P:(BLK1 * i + j + 1) * P], IDF[:, :])
                        ins.then_inc(pt1_done, 1)
                if item := lagged(p, q, 3, P1):
                    h, b = 4 * item[0] + item[1], 1 - a
                    pe.wait_ge(pt1_lo, 2 * g - 4)
                    for i in range(2):
                        for qt in range(2):
                            for kt in range(qt + 1):
                                blk = BLK1 * i + qt + kt
                                c0 = (2 * i + qt) * 32
                                ins = product(PS[:, odd_bank(hf) + b, c0:c0 + VC1],
                                              lambda s: PT1[:, b, s, blk * P:(blk + 1) * P],
                                              lambda s: VB1[:, s, TPH * hf + 2 * i + kt, h, :], kt == 0, kt == qt)
                    ins.then_inc(pv1_done, 1)
                if lagged(p, q, 0, P1):
                    pe.wait_ge(shift1_done, 2 * g + 2)
                    for i in range(2):
                        for qt, c0 in ((0, 0), (1, P)):
                            n = (qt + 1) * P
                            ins = te.matmul(PS[:, bank + i, c0:c0 + n], IDB[:, :],
                                            MB1[:, a, 2 * qt + i:2 * qt + i + 1].broadcast_to([P, n]),
                                            start=False, stop=qt == 1, skip_group_check=True)
                    ins.then_inc(shifted1, 1)
                if q < 3 and lagged(p, q, 0, P1):
                    scores_of(hf, p, q + 1)
                elif q == 3 and lagged(p + 1, 0, 0, P1):
                    scores_of(hf, p + 1, 0)

            def attention1():
                def half(hf):
                    scores_of(hf, 0, 0)
                    if hf == 0:
                        last_down(2, 1)
                    for q in range(4):
                        if q == 3:
                            if hf == 0:
                                turn(4, 1)
                                pe.wait_ge(turned_lo, turn_count(4, 3) + 1)
                            else:
                                pe.wait_ge(cbt_done, 3)
                        step1(hf, 0, q)
                        if q == 0 and hf:
                            route_turn(6, 0)
                    with pe.Fori(1, P1 - 1) as p:
                        for q in range(4):
                            step1(hf, p, q)
                    for q in range(4):
                        step1(hf, P1 - 1, q)
                    step1(hf, P1, 0)
                    step1(hf, P1, 1)

                def output(hf):
                    for u in range(UPH * hf, UPH * hf + UPH):
                        pe.wait_ge(turned_lo, turn_count(5, u) + 1)
                        for t in range(2):
                            for k in range(KD):
                                ins = product(y_tiles(u)[:, t, :],
                                              lambda s: XT[:, s, k, (2 * u + t) * P:(2 * u + t + 1) * P],
                                              lambda s: WD16[:, 6 + k, s, :], k == 0, k == KD - 1)
                        ins.then_inc(proj1_done, 1)

                def turn_tile(i):
                    if i:
                        pe.wait_ge(q1_copied, 2 * (TPH + i))
                    turn_qk(1, TPH + i, place(1, i))

                pe.wait_ge(ones_set, 2)
                half(0)
                queries_keys1(1, 0, TPH)
                step1(0, P1, 2)
                queries_keys1(1, 1, TPH + 1)
                turn(5, 0)
                values1(1, 0, TPH)
                values1(1, 1, TPH + 1)
                output(0)
                turn_tile(0)
                for i in (2, 3):
                    pe.wait_ge(rope1_mul, 3 * (TPH + i) - 3)
                    queries_keys1(1, i, TPH + i)
                    pe.wait_ge(v1_lo, TPH + i - 1)
                    values1(1, i, TPH + i)
                    if i == 2:
                        turn_tile(1)
                turn(6, 0)
                turn_tile(2)
                route_logits(6, 0)
                turn_tile(3)
                pe.wait_ge(q1_copied, 2 * TT)
                half(1)
                step1(1, P1, 2)
                turn(5, 1)
                output(1)

            def left_down(f, hf):
                return lambda: None, lambda: last_down(f, hf)

            def last_steps0():
                step0(1, P0, 1)
                step0(1, P0, 2)
                step0(1, P0, 3)

            def keep_busy(n):
                for _ in range(n):
                    te.matmul(PS[:, GATE[0], :], ZERO[:, :], CMB[:, :, :].rearrange("p t n -> p (t n)"),
                              start=True, stop=True)

            pe.wait_ge(zeroed, 2)
            keep_busy(12)
            pe.wait_ge(dma_id, 16)
            turn(0, 0)
            keep_busy(7)
            pe.wait_ge(narrowed, 3)
            pe.wait_ge(zeroed, 6)
            glu(0, 0, (lambda: None, lambda: pe.wait_ge(dma_sel, 16)))
            glu(0, 1, left_down(0, 0))
            attention0(0, 1, 1)
            attention0(1, 2, 0)
            glu(1, 0, (lambda: step0(1, P0, 0), last_steps0))
            glu(1, 1, left_down(1, 0))
            glu(2, 0, left_down(1, 1))
            glu(2, 1, left_down(2, 0))
            attention1()
            glu(3, 0, (lambda: None, lambda: None))
            glu(3, 1, left_down(3, 0))
            last_down(3, 1)


def _pack(np, t):
    def feats(w):
        return np.stack([w[:P], w[P:]], axis=1)

    def glu(gate, up, down):
        n = -(-gate.shape[1] // P) * P
        g, u, d = np.zeros((D, n), np.float32), np.zeros((D, n), np.float32), np.zeros((n, D), np.float32)
        g[:, :gate.shape[1]], u[:, :gate.shape[1]], d[:gate.shape[1]] = gate, up, down
        chunks = [np.concatenate([feats(g[:, c:c + P]).reshape(P, D), feats(u[:, c:c + P]).reshape(P, D),
                                  d[c:c + P]], axis=1) for c in range(0, n, P)]
        if gate.shape[1] < n:
            c, h = n - P, P // 2
            chunks[-1] = np.concatenate([feats(np.concatenate([g[:, c:c + h], u[:, c:c + h]], axis=1)).reshape(P, D),
                                         np.zeros((P, D), np.float32), d[c:]], axis=1)
        return chunks

    gu, wk, wv = t["L0_ffn_w_gate_up"], t["L0_attn_Wk"], t["L0_attn_Wv"]
    a = glu(gu[:INTER].T, gu[INTER:].T, t["L0_ffn_w_down"].T)
    kv = [feats(wk[g * P:(g + 1) * P].T).reshape(P, D) for g in range(KV0)]
    kv += [wv[(i % 2) * D:(i % 2 + 1) * D, (i // 2) * P:(i // 2 + 1) * P].T for i in range(4)]
    wa = np.concatenate([x for pair in zip(a, kv) for x in pair], axis=1)
    wq, wo = t["L0_attn_Wq"], t["L0_attn_Wo"]
    wb = np.concatenate([x for h in range(H0) for x in (feats(wq[h * P:(h + 1) * P].T).reshape(P, D),
                                                        wo[:, h * P:(h + 1) * P].T)], axis=1)
    side = lambda n, s: np.concatenate([t["L1_ffn_w_" + n].transpose(1, 0, 2).reshape(D, E * I_EXP), t["L1_ffn_sw_" + s]], axis=1)
    wc = np.concatenate(glu(side("gate", "gate"), side("up", "up"),
                            np.concatenate([t["L1_ffn_w_down"].reshape(E * I_EXP, D), t["L1_ffn_sw_down"]])), axis=1)
    qkv, wo1 = t["L1_attn_W_qkv"].T, t["L1_attn_W_o"].T
    wd = np.concatenate([qkv[:P], qkv[P:], wo1[:P], wo1[P:]], axis=1)
    wg = np.zeros((D, 16), np.float32)
    wg[:, :E], wg[:, E:E + 1] = t["L1_ffn_gate_w"].T, t["L1_ffn_shared_gate_w"]
    return [wa, wb, wc, wd, feats(wg)]


def _tables(np):
    f = np.float32
    scale = f(SQ / (SX * SW))

    def angles(n, half):
        inv = f(1.0) / np.power(f(10000.0), (np.arange(0, 2 * half, 2, dtype=f) / f(2 * half)))
        return np.repeat(np.arange(n, dtype=f)[:, None] * inv[None, :], 2, axis=1)

    a0 = angles(S, P // 2).T
    sign0 = np.where(np.arange(P) < P // 2, f(-1), f(1))[:, None]
    rope0 = np.stack([np.cos(a0) * scale, np.sin(a0) * sign0 * scale], axis=1)
    a1 = angles(S, DH1 // 2).reshape(2, P, DH1).transpose(1, 0, 2)
    sign1 = np.where(np.arange(DH1) % 2 == 0, f(-1), f(1))
    rope1 = np.stack([np.cos(a1) * scale, np.sin(a1) * sign1 * scale], axis=2)
    i = np.arange(P)
    mask = np.where(i[None, :] <= i[:, None], f(0), f(-1e30))
    eye = np.eye(P, dtype=f)
    e = np.arange(E)
    tri = np.broadcast_to((e[None, :] < e[:, None]).astype(f), (P, E, E))
    sel = np.zeros((32, JM * P), np.float16)
    owner = np.minimum(np.arange(JM * P) // I_EXP, E)
    for part in range(2):
        sel[part * GATES + owner, np.arange(JM * P)] = 1
    return [rope0, rope1, mask, eye, tri, sel]


def kernel(**inputs):
    import numpy as np
    import concourse.bacc as bacc
    from concourse.bass_utils import run_bass_kernel_spmd as run

    t = {k: np.asarray(v) for k, v in inputs.items()}
    nc = bacc.Bacc("TRN2", target_bir_lowering=False, num_devices=1)
    names = ["x", "wa", "wb", "wc", "wd", "wg", "rope0", "rope1", "mask", "idf", "tri", "sel"]
    arrays, args = {}, []
    for name, a in zip(names, [t["L0_attn_x"]] + _pack(np, t) + _tables(np)):
        a = np.ascontiguousarray(a)
        arrays[name + "_dram"] = a
        args.append(nc.dram_tensor(name + "_dram", a.shape, mybir.dt.from_np(a.dtype), kind="ExternalInput").ap())
    args.append(nc.dram_tensor("out_dram", (NB, S, D), F32, kind="ExternalOutput").ap())
    macaron(nc, *args)
    return run(nc, [arrays], core_ids=[0]).results[0]["out_dram"]
```
